# Optimizing a Trainium2 kernel written in Bass

```python
import numpy as np
import jax
import jax.numpy as jnp

def _softmax(x, axis=-1):
    return jax.nn.softmax(x, axis=axis)

def _gelu(x):
    return jax.nn.gelu(x, approximate=True)

def _silu(x):
    return jax.nn.silu(x)

def _sigmoid(x):
    return jax.nn.sigmoid(x)

def _layernorm(x, axis=-1, eps=1e-05):
    m = jnp.mean(x, axis=axis, keepdims=True)
    v = jnp.var(x, axis=axis, keepdims=True)
    return (x - m) / jnp.sqrt(v + eps)

def _scatter_add(tgt, idx, src, axis=0):
    return tgt.at[idx].add(src)

def _segment_sum(src, seg, n):
    return jax.ops.segment_sum(src, seg, n)
kernel_name = 'mk_sandwich_d1_jaxref_r8_c9979f'

def setup_inputs(seed: int=0):
    np.random.seed(seed)
    _w = jnp.asarray

    def _L0_attn_setup():
        import jax, jax.numpy as jnp
        import numpy as np
        D_MODEL = 128
        N_HEADS = 32
        D_INNER = 2 * D_MODEL
        HEADDIM = D_INNER // N_HEADS
        D_STATE = 128
        D_CONV = 4
        CONV_DIM = D_INNER + 2 * D_STATE
        D_IN_PROJ = 2 * D_INNER + 2 * D_STATE + N_HEADS
        D_FF = 512
        B, L = (2, 256)

        def layernorm(x, w, b, eps=1e-05):
            mu = jnp.mean(x, axis=-1, keepdims=True)
            var = jnp.mean(jnp.square(x - mu), axis=-1, keepdims=True)
            return (x - mu) * jax.lax.rsqrt(var + eps) * w + b

        def causal_conv1d(x, w, b):
            K = w.shape[1]
            xp = jnp.pad(x, ((0, 0), (K - 1, 0), (0, 0)))
            Ln = x.shape[1]
            y = b
            for k in range(K):
                y = y + xp[:, k:k + Ln, :] * w[:, k]
            return y

        def ssd_scan(xh, dt, Bm, Cm, A):
            dA = jnp.exp(dt * A)
            dBx = dt[..., None] * xh
            b, l, h, p = xh.shape
            n = Bm.shape[-1]

            def step(hst, inp):
                dA_t, dBx_t, B_t, C_t = inp
                hst = hst * dA_t[:, :, None, None] + dBx_t[..., None] * B_t[:, None, None, :]
                y = jnp.einsum('bhpn,bn->bhp', hst, C_t)
                return (hst, y)
            xs = (jnp.moveaxis(dA, 1, 0), jnp.moveaxis(dBx, 1, 0), jnp.moveaxis(Bm, 1, 0), jnp.moveaxis(Cm, 1, 0))
            h0 = jnp.zeros((b, h, p, n), dtype=xh.dtype)
            _, ys = jax.lax.scan(step, h0, xs)
            return jnp.moveaxis(ys, 0, 1)

        def mamba2_mixer(xn, in_proj_w, conv_w, conv_b, dt_bias, A_log, D_skip, rms_w, out_proj_w):
            zxbcdt = xn @ in_proj_w
            z = zxbcdt[..., :D_INNER]
            xBC = zxbcdt[..., D_INNER:D_INNER + CONV_DIM]
            dt = zxbcdt[..., D_INNER + CONV_DIM:]
            dt = jax.nn.softplus(dt + dt_bias)
            xBC = jax.nn.silu(causal_conv1d(xBC, conv_w, conv_b))
            x_ssm = xBC[..., :D_INNER]
            Bm = xBC[..., D_INNER:D_INNER + D_STATE]
            Cm = xBC[..., D_INNER + D_STATE:]
            A = -jnp.exp(A_log)
            xh = x_ssm.reshape(*x_ssm.shape[:-1], N_HEADS, HEADDIM)
            y = ssd_scan(xh, dt, Bm, Cm, A)
            y = y + D_skip[None, None, :, None] * xh
            y = y.reshape(*y.shape[:-2], D_INNER)
            y = y * jax.nn.silu(z)
            y = y * jax.lax.rsqrt(jnp.mean(jnp.square(y), axis=-1, keepdims=True) + 1e-05) * rms_w
            return y @ out_proj_w
        key = jax.random.key(seed)
        ks = jax.random.split(key, 12)
        s = 0.02
        dt = jnp.exp(jax.random.uniform(ks[1], (N_HEADS,)) * (np.log(0.1) - np.log(0.001)) + np.log(0.001))
        dt_bias = dt + jnp.log(-jnp.expm1(-dt))
        return {'x': jax.random.normal(ks[0], (B, L, D_MODEL), jnp.float32), 'ln_w': jnp.ones((D_MODEL,), jnp.float32), 'ln_b': jnp.zeros((D_MODEL,), jnp.float32), 'in_proj_w': jax.random.normal(ks[2], (D_MODEL, D_IN_PROJ), jnp.float32) * s, 'conv_w': jax.random.normal(ks[3], (CONV_DIM, D_CONV), jnp.float32) * 0.3, 'conv_b': jnp.zeros((CONV_DIM,), jnp.float32), 'dt_bias': dt_bias.astype(jnp.float32), 'A_log': jnp.log(jax.random.uniform(ks[4], (N_HEADS,), minval=1.0, maxval=16.0)).astype(jnp.float32), 'D_skip': jnp.ones((N_HEADS,), jnp.float32), 'rms_w': jnp.ones((D_INNER,), jnp.float32), 'out_proj_w': jax.random.normal(ks[5], (D_INNER, D_MODEL), jnp.float32) * s, 'mlp_w1': jax.random.normal(ks[6], (D_MODEL, D_FF), jnp.float32) * s, 'mlp_b1': jnp.zeros((D_FF,), jnp.float32), 'mlp_w2': jax.random.normal(ks[7], (D_FF, D_MODEL), jnp.float32) * s, 'mlp_b2': jnp.zeros((D_MODEL,), jnp.float32)}
    _L0_attn_in = _L0_attn_setup()

    def _L0_ffn_setup():
        import jax, jax.numpy as jnp
        import numpy as np
        import math
        E = 8
        K = 2
        CF = 1.2
        D = 128
        H = 512
        key = jax.random.key(seed)
        k0, k1, k2, k3 = jax.random.split(key, 4)
        B, T = (8, 256)
        x_btd = jax.random.normal(k0, (B, T, D), jnp.float32)
        Wr = jax.random.normal(k1, (D, E), jnp.float32) / np.sqrt(D)
        br = jnp.zeros((E,), jnp.float32)
        W1 = jax.random.normal(k2, (E, D, H), jnp.float32) / np.sqrt(D)
        b1 = jnp.zeros((E, H), jnp.float32)
        W2 = jax.random.normal(k3, (E, H, D), jnp.float32) / np.sqrt(H)
        b2 = jnp.zeros((E, D), jnp.float32)
        return dict(x_btd=x_btd, Wr=Wr, br=br, W1=W1, b1=b1, W2=W2, b2=b2)
    _L0_ffn_in = _L0_ffn_setup()
    _d = {'L0_attn_x': _L0_attn_in['x'], 'L0_attn_ln_w': _L0_attn_in['ln_w'], 'L0_attn_ln_b': _L0_attn_in['ln_b'], 'L0_attn_in_proj_w': _L0_attn_in['in_proj_w'], 'L0_attn_conv_w': _L0_attn_in['conv_w'], 'L0_attn_conv_b': _L0_attn_in['conv_b'], 'L0_attn_dt_bias': _L0_attn_in['dt_bias'], 'L0_attn_A_log': _L0_attn_in['A_log'], 'L0_attn_D_skip': _L0_attn_in['D_skip'], 'L0_attn_rms_w': _L0_attn_in['rms_w'], 'L0_attn_out_proj_w': _L0_attn_in['out_proj_w'], 'L0_attn_mlp_w1': _L0_attn_in['mlp_w1'], 'L0_attn_mlp_b1': _L0_attn_in['mlp_b1'], 'L0_attn_mlp_w2': _L0_attn_in['mlp_w2'], 'L0_attn_mlp_b2': _L0_attn_in['mlp_b2'], 'L0_ffn_Wr': _L0_ffn_in['Wr'], 'L0_ffn_br': _L0_ffn_in['br'], 'L0_ffn_W1': _L0_ffn_in['W1'], 'L0_ffn_b1': _L0_ffn_in['b1'], 'L0_ffn_W2': _L0_ffn_in['W2'], 'L0_ffn_b2': _L0_ffn_in['b2']}
    _x0 = _d['L0_attn_x']
    _d['L0_attn_x'] = jax.random.normal(jax.random.fold_in(jax.random.key(seed), 1), (8, 1024, 128), dtype=_x0.dtype)
    del _x0
    return _d

def reference(L0_attn_x, L0_attn_ln_w, L0_attn_ln_b, L0_attn_in_proj_w, L0_attn_conv_w, L0_attn_conv_b, L0_attn_dt_bias, L0_attn_A_log, L0_attn_D_skip, L0_attn_rms_w, L0_attn_out_proj_w, L0_attn_mlp_w1, L0_attn_mlp_b1, L0_attn_mlp_w2, L0_attn_mlp_b2, L0_ffn_Wr, L0_ffn_br, L0_ffn_W1, L0_ffn_b1, L0_ffn_W2, L0_ffn_b2):

    def _L0_attn_ref(x, ln_w, ln_b, in_proj_w, conv_w, conv_b, dt_bias, A_log, D_skip, rms_w, out_proj_w, mlp_w1, mlp_b1, mlp_w2, mlp_b2):
        import jax, jax.numpy as jnp
        import numpy as np
        D_MODEL = 128
        N_HEADS = 32
        D_INNER = 2 * D_MODEL
        HEADDIM = D_INNER // N_HEADS
        D_STATE = 128
        D_CONV = 4
        CONV_DIM = D_INNER + 2 * D_STATE
        D_IN_PROJ = 2 * D_INNER + 2 * D_STATE + N_HEADS
        D_FF = 512
        B, L = (2, 256)

        def layernorm(x, w, b, eps=1e-05):
            mu = jnp.mean(x, axis=-1, keepdims=True)
            var = jnp.mean(jnp.square(x - mu), axis=-1, keepdims=True)
            return (x - mu) * jax.lax.rsqrt(var + eps) * w + b

        def causal_conv1d(x, w, b):
            K = w.shape[1]
            xp = jnp.pad(x, ((0, 0), (K - 1, 0), (0, 0)))
            Ln = x.shape[1]
            y = b
            for k in range(K):
                y = y + xp[:, k:k + Ln, :] * w[:, k]
            return y

        def ssd_scan(xh, dt, Bm, Cm, A):
            dA = jnp.exp(dt * A)
            dBx = dt[..., None] * xh
            b, l, h, p = xh.shape
            n = Bm.shape[-1]

            def step(hst, inp):
                dA_t, dBx_t, B_t, C_t = inp
                hst = hst * dA_t[:, :, None, None] + dBx_t[..., None] * B_t[:, None, None, :]
                y = jnp.einsum('bhpn,bn->bhp', hst, C_t)
                return (hst, y)
            xs = (jnp.moveaxis(dA, 1, 0), jnp.moveaxis(dBx, 1, 0), jnp.moveaxis(Bm, 1, 0), jnp.moveaxis(Cm, 1, 0))
            h0 = jnp.zeros((b, h, p, n), dtype=xh.dtype)
            _, ys = jax.lax.scan(step, h0, xs)
            return jnp.moveaxis(ys, 0, 1)

        def mamba2_mixer(xn, in_proj_w, conv_w, conv_b, dt_bias, A_log, D_skip, rms_w, out_proj_w):
            zxbcdt = xn @ in_proj_w
            z = zxbcdt[..., :D_INNER]
            xBC = zxbcdt[..., D_INNER:D_INNER + CONV_DIM]
            dt = zxbcdt[..., D_INNER + CONV_DIM:]
            dt = jax.nn.softplus(dt + dt_bias)
            xBC = jax.nn.silu(causal_conv1d(xBC, conv_w, conv_b))
            x_ssm = xBC[..., :D_INNER]
            Bm = xBC[..., D_INNER:D_INNER + D_STATE]
            Cm = xBC[..., D_INNER + D_STATE:]
            A = -jnp.exp(A_log)
            xh = x_ssm.reshape(*x_ssm.shape[:-1], N_HEADS, HEADDIM)
            y = ssd_scan(xh, dt, Bm, Cm, A)
            y = y + D_skip[None, None, :, None] * xh
            y = y.reshape(*y.shape[:-2], D_INNER)
            y = y * jax.nn.silu(z)
            y = y * jax.lax.rsqrt(jnp.mean(jnp.square(y), axis=-1, keepdims=True) + 1e-05) * rms_w
            return y @ out_proj_w
        residual = x
        xn = layernorm(residual, ln_w, ln_b)
        y = mamba2_mixer(xn, in_proj_w, conv_w, conv_b, dt_bias, A_log, D_skip, rms_w, out_proj_w)
        out = y + residual
        h = layernorm(out, ln_w, ln_b)
        h = jax.nn.relu(h @ mlp_w1 + mlp_b1) @ mlp_w2 + mlp_b2
        return h + out

    def _L0_ffn_ref(x_btd, Wr, br, W1, b1, W2, b2):
        import jax, jax.numpy as jnp
        import numpy as np
        import math
        E = 8
        K = 2
        CF = 1.2
        D = 128
        H = 512
        B, T, Dm = x_btd.shape
        N = B * T
        x = x_btd.reshape(N, Dm)
        cap = int(math.ceil(CF * N / E))
        probs = jax.nn.softmax(x @ Wr + br, axis=-1)
        gates, ids = jax.lax.top_k(probs, K)
        flat_ids = ids.reshape(-1)
        flat_g = gates.reshape(-1)
        M = N * K
        order = jnp.lexsort((-flat_g, flat_ids))
        s_ids = flat_ids[order]
        s_tok = (order // K).astype(jnp.int32)
        s_g = flat_g[order]
        counts = jnp.bincount(flat_ids, length=E)
        starts = jnp.concatenate([jnp.zeros((1,), counts.dtype), jnp.cumsum(counts)[:-1]])
        rank = jnp.arange(M) - starts[s_ids]
        valid = rank < cap
        pos = jnp.where(valid, s_ids * cap + rank, E * cap)
        disp_tok = jnp.zeros((E * cap + 1,), jnp.int32).at[pos].set(s_tok)[:E * cap]
        disp_g = jnp.zeros((E * cap + 1,), x.dtype).at[pos].set(s_g)[:E * cap]
        xg = x[disp_tok].reshape(E, cap, Dm)
        h = jax.nn.silu(jnp.einsum('ecd,edh->ech', xg, W1) + b1[:, None, :])
        out = jnp.einsum('ech,ehd->ecd', h, W2) + b2[:, None, :]
        gated = out * disp_g.reshape(E, cap, 1)
        y = jnp.zeros((N, Dm), x.dtype).at[disp_tok].add(gated.reshape(E * cap, Dm))
        return y.reshape(B, T, Dm)
    x = L0_attn_x
    x = x + _layernorm(_L0_attn_ref(_layernorm(x, axis=-1), L0_attn_ln_w, L0_attn_ln_b, L0_attn_in_proj_w, L0_attn_conv_w, L0_attn_conv_b, L0_attn_dt_bias, L0_attn_A_log, L0_attn_D_skip, L0_attn_rms_w, L0_attn_out_proj_w, L0_attn_mlp_w1, L0_attn_mlp_b1, L0_attn_mlp_w2, L0_attn_mlp_b2), axis=-1)
    x = x + _layernorm(_L0_ffn_ref(_layernorm(x, axis=-1), L0_ffn_Wr, L0_ffn_br, L0_ffn_W1, L0_ffn_b1, L0_ffn_W2, L0_ffn_b2), axis=-1)
    return x

_drawn_inputs = setup_inputs


def setup_inputs(seed=0):
    import zlib

    import numpy as np

    out = dict(_drawn_inputs(seed))
    spreads = {'L0_attn_ln_w': (1.0, 0.2),
     'L0_attn_ln_b': (0.0, 0.1),
     'L0_attn_conv_b': (0.0, 0.1),
     'L0_attn_D_skip': (1.0, 0.2),
     'L0_attn_rms_w': (1.0, 0.2),
     'L0_attn_mlp_b1': (0.0, 0.1),
     'L0_attn_mlp_b2': (0.0, 0.1),
     'L0_ffn_br': (0.0, 0.1),
     'L0_ffn_b1': (0.0, 0.1),
     'L0_ffn_b2': (0.0, 0.1)}
    factors = {}
    for name, (base, spread) in spreads.items():
        noise = np.random.default_rng([zlib.crc32(name.encode()), seed]).standard_normal(out[name].shape)
        drawn = base * np.exp(spread * noise) if base else spread * noise
        out[name] = jnp.asarray(drawn.astype(out[name].dtype))
    for name, factor in factors.items():
        out[name] = (out[name] * factor).astype(out[name].dtype)
    return out
```

```python
from contextlib import ExitStack

import concourse.bass as bass
from concourse import mybir

F32 = mybir.dt.float32
BF16 = mybir.dt.bfloat16
I32 = mybir.dt.int32
U32 = mybir.dt.uint32
ALU = mybir.AluOpType
ACT = mybir.ActivationFunctionType
AX = mybir.AxisListType

P = 128
SEQS, LEN, D = 8, 1024, 128
STEPS = LEN // P
TILES = SEQS * STEPS
TOKENS = SEQS * LEN
HEADS, HD, INNER, STATE = 32, 8, 256, 128
TAPS = 4
HALO = TAPS - 1
XBLK = HALO + P
CONV = INNER + 2 * STATE
CHUNK = 64
FF = 512
NF = FF // P
EPS = 1e-5
EXPERTS = 8
CAP = -(-12 * TOKENS // (10 * EXPERTS))
ROWS = 256
ESTEPS = -(-CAP // ROWS)
REGION = ESTEPS * ROWS
TABLE = EXPERTS * REGION
ROWLEN = D + 4
FAR = 65536.0


def need(eng, sem, t, back=0):
    value = t + 1 - back
    if not isinstance(value, int) or value > 0:
        eng.wait_ge(sem, value)


carrier = [None]


def need_apart(eng, sem, t, back=0):
    need(eng, sem, t, back)
    if not isinstance(t, int):
        eng.sem_inc(carrier[0], 1)


def skewed(eng, steps, unroll, head, stages):
    def at(i, lo, which):
        for lag, stage in stages:
            t = i - lag
            if which is None:
                if 0 <= t < steps:
                    stage(t, t % unroll)
            else:
                stage(t, (which - lag) % unroll)
    for i in range(head):
        at(i, 0, None)
    with eng.Fori(head // unroll, steps // unroll) as j:
        for u in range(unroll):
            at(j * unroll + u, 0, u)
    for i in range(steps, steps + max(lag for lag, _ in stages)):
        at(i, 0, None)


def build(nc, x, ln_w, ln_b, in_proj_w, conv_w, conv_b, dt_bias, A_log, D_skip, rms_w, out_proj_w,
          mlp_w1, mlp_b1, mlp_w2, mlp_b2, Wr, br, W1, b1, W2, b2, out):
    table = nc.dram_tensor("expert_rows", (TABLE, ROWLEN), F32, kind="Internal").ap()
    choice = nc.dram_tensor("choice_rows", (2 * TOKENS, D), F32, kind="Internal").ap()
    with ExitStack() as ctx:
        ctx.enter_context(nc.allow_non_contiguous_dma(reason="columns of a few hundred biases, one element a partition"))

        def sb(name, shape, dt=F32):
            return ctx.enter_context(nc.sbuf_tensor(name, shape, dt))

        stage_sems = []
        carrier[0] = nc.alloc_semaphore(name="carrier")

        def sem(name):
            s = nc.alloc_semaphore(name=name)
            stage_sems.append(s)
            return s

        def stage_over():
            nc.clear_and_free_semaphores(list(stage_sems))
            stage_sems.clear()
            nc.all_engine_barrier()

        ident = sb("ident", [P, P])
        ones = sb("ones", [P, P])
        ones_bf = sb("ones_bf", [P, P], BF16)
        xbias3 = sb("xbias3", [P, INNER], BF16)
        centre = sb("centre", [P, P])
        spans = sb("spans", [P, 3, P])
        causal = sb("causal", [P, P])
        half = sb("half", [P, 16])
        lnw = sb("lnw", [P, 1])
        lnb = sb("lnb", [P, 1])
        bc_bias = sb("bc_bias", [P, 2])
        b1_col = sb("b1_col", [P, NF])
        brow = sb("brow", [P, EXPERTS])
        b2row = sb("b2row", [P, D])
        dskip = sb("dskip", [P, HEADS])
        w_conv = sb("w_conv", [P, TAPS, CONV])
        w_z = sb("w_z", [P, INNER])
        w_dt = sb("w_dt", [P, HEADS])
        w_out = sb("w_out", [P, 2, D])
        w_m1 = sb("w_m1", [P, FF])
        w_m2 = sb("w_m2", [P, NF, D])
        w_r = sb("w_r", [P, EXPERTS])
        mean = sb("mean", [P, TILES])
        rstd = sb("rstd", [P, TILES])
        ssq = sb("ssq", [P, TILES])
        logits = sb("logits", [P, TILES, EXPERTS])
        arena = sb("arena", [P, 72 * XBLK])
        xT = arena[:, :].rearrange("p (t c) -> p t c", c=XBLK)
        x1 = arena[:, 0:TILES * D].rearrange("p (t d) -> p t d", d=D)
        arena2 = sb("arena2", [P, TILES * ROWLEN])
        dec = arena2[:, 0:4 * TILES * HEADS].rearrange("p (f t h) -> p f t h", f=4, h=HEADS)
        pre, post, gapA, gapB = (dec[:, f] for f in range(4))
        rows = arena2[:, :].rearrange("p (t c) -> p t c", c=ROWLEN)
        arena3 = sb("arena3", [P, TILES * D])
        proj = arena3[:, :].rearrange("p (t d) -> p t d", d=D)
        tmp = arena3[:, :].rearrange("p (f t h) -> p f t h", f=4, h=HEADS)
        dt, da, tail, work = (tmp[:, f] for f in range(4))

        with ExitStack() as st:
            st.callback(stage_over)
            def sbt(name, shape, dt=F32):
                return st.enter_context(nc.sbuf_tensor(name, shape, dt))
            taps = sbt("taps", [P, CONV, TAPS])
            w_in = sbt("w_in", [P, CONV])
            xb = sbt("xb", [P, INNER])
            xr = sbt("xr", [P, INNER])
            xh = sbt("xh", [P, 3, INNER], BF16)
            wo = sbt("wo", [P, 2, D])
            rmsw = sbt("rmsw", [P, 2])
            zrow = sbt("zrow", [P, 8 * D])
            frow = sbt("frow", [P, 20, ROWLEN])
            loaded, fold, masks, zeroed, filled, split = (
                sem(n) for n in ("loaded", "fold", "masks", "zeroed", "filled", "split"))
            block = st.enter_context(nc.Block())

            @block.sync
            def _(sp):
                loads = [(w_in[:, :], in_proj_w[:, INNER:INNER + CONV]),
                         (taps[:, :, :].rearrange("p c k -> p (c k)"),
                          conv_w.rearrange("c k -> (c k)").partition_broadcast(P)),
                         (xb[:, :], conv_b[0:INNER].partition_broadcast(P)),
                         (wo[:, :, :], out_proj_w.rearrange("(c p) d -> p c d", p=P)),
                         (rmsw[:, :], rms_w.rearrange("(c p) -> p c", p=P)),
                         (lnw[:, :], ln_w.rearrange("(p a) -> p a", a=1)),
                         (lnb[:, :], ln_b.rearrange("(p a) -> p a", a=1)),
                         (bc_bias[:, :], conv_b[INNER:CONV].rearrange("(c p) -> p c", p=P)),
                         (b1_col[:, :], mlp_b1.rearrange("(c p) -> p c", p=P)),
                         (brow[:, :], br.partition_broadcast(P)),
                         (b2row[:, :], mlp_b2.partition_broadcast(P)),
                         (dskip[:, :], D_skip.partition_broadcast(P)),
                         (w_z[:, :], in_proj_w[:, 0:INNER]),
                         (w_dt[:, :], in_proj_w[:, INNER + CONV:INNER + CONV + HEADS]),
                         (w_m1[:, :], mlp_w1),
                         (w_m2[:, :, :], mlp_w2.rearrange("(c p) d -> p c d", p=P)),
                         (w_r[:, :], Wr)]
                for dst, src in loads:
                    sp.dma_start(dst, src).then_inc(loaded, 16)
                sp.wait_ge(loaded, 16 * len(loads))
                sp.wait_ge(zeroed, 1)
                zeros = choice.rearrange("(n p r) d -> n p (r d)", p=P, r=8)
                for n in range(2 * TOKENS // (8 * P)):
                    sp.dma_start(zeros[n], zrow[:, :]).then_inc(filled, 16)
                sp.wait_ge(zeroed, 3)
                empty = table.rearrange("(n p r) c -> n p (r c)", p=P, r=20)
                for n in range(TABLE // (20 * P)):
                    sp.dma_start(empty[n], frow[:, :, :].rearrange("p r c -> p (r c)")).then_inc(filled, 16)
                sp.wait_ge(filled, 16 * (2 * TOKENS // (8 * P) + TABLE // (20 * P)))

            @block.gpsimd
            def _(g):
                g.memset(zrow[:, :], 0.0).then_inc(zeroed, 1)
                g.memset(frow[:, :, :], 0.0).then_inc(zeroed, 1)
                g.wait_ge(zeroed, 2)
                g.memset(frow[:, :, D:D + 1], FAR).then_inc(zeroed, 1)
                g.memset(half[:, :], -0.5)
                g.memset(ones[:, :], 1.0)
                g.memset(ones_bf[:, :], 1.0)
                g.memset(xT[:, 0:SEQS, 0:HALO], 0.0)
                g.memset(ident[:, :], 0.0)
                g.memset(spans[:, :, :], 1.0)
                for q in range(4):
                    g.memset(centre[:, 32 * q:32 * q + 32], 1.0 if q % 2 else -1.0)
                g.memset(causal[:, :], 1.0).then_inc(masks, 1)
                g.wait_ge(masks, 1)
                n = 1

                def keep(ap, base, step, chan, cmp=ALU.is_ge, fill=0.0):
                    nonlocal n
                    g.affine_select(out=ap, in_=ap, compare_op=cmp, fill=fill, base=base,
                                    pattern=[[step, ap.shape[-1]]], channel_multiplier=chan).then_inc(masks, 1)
                    n += 1
                    g.wait_ge(masks, n)
                keep(ident[:, :], 0, -1, 1, ALU.not_equal, 1.0)
                for c in range(P // CHUNK):
                    part = causal[:, CHUNK * c:CHUNK * (c + 1)]
                    keep(part, CHUNK * c, 1, -1)
                    keep(part, -CHUNK * c, 0, 1)
                for q in range(4):
                    part = centre[:, 32 * q:32 * q + 32]
                    if q % 2:
                        keep(part, 32 * q, 1, -1)
                        keep(part, -32 * q, 0, 1)
                    else:
                        keep(part, -32 * q - 1, -1, 1)
                        keep(part, 32 * q + 31, 0, -1)
                keep(spans[:, 0, :], 31, 0, -1)
                keep(spans[:, 1, :], -32, 0, 1)
                keep(spans[:, 1, :], 95, 0, -1)
                keep(spans[:, 2, :], -96, 0, 1)

            @block.vector
            def _(v):
                v.wait_ge(loaded, 16 * 17)
                for k in range(TAPS):
                    v.tensor_tensor(w_conv[:, k, :], w_in[:, :], taps[:, :, k], ALU.mult).then_inc(fold, 1)
                for c in range(2):
                    v.tensor_scalar(w_out[:, c, :], wo[:, c, :], rmsw[:, c:c + 1], None, ALU.mult)
                v.memset(xbias3[:, :], 0.0).then_inc(split, 1)
                v.tensor_copy(xh[:, 0, :], xb[:, :]).then_inc(split, 1)
                v.wait_ge(split, 2)
                v.tensor_tensor(xr[:, :], xb[:, :], xh[:, 0, :], ALU.subtract).then_inc(split, 1)
                v.wait_ge(split, 3)
                v.tensor_copy(xh[:, 1, :], xr[:, :]).then_inc(split, 1)
                v.wait_ge(split, 4)
                v.tensor_tensor(xh[:, 2, :], xr[:, :], xh[:, 1, :], ALU.subtract).then_inc(split, 1)
                v.wait_ge(split, 5)
                for r in range(3):
                    v.tensor_copy(xbias3[32 * r:32 * r + 1, :], xh[32 * r:32 * r + 1, r, :]).then_inc(split, 1)

        with ExitStack() as st:
            st.callback(stage_over)
            def sbt(name, shape, dt=F32):
                return st.enter_context(nc.sbuf_tensor(name, shape, dt))

            def pst(name, shape):
                return st.enter_context(nc.psum_tensor(name, shape, F32))
            xin = sbt("n_xin", [P, 2, SEQS, D])
            stats = sbt("n_stats", [P, 2, SEQS, 6])
            mv = sbt("n_mv", [P, 2, SEQS, 2])
            small = sbt("n_small", [P, 2, 6, SEQS])
            hn = sbt("n_hn", [P, 2, SEQS, D])
            xs = sbt("n_xs", [P, 2, SEQS, P])
            dtb = sbt("n_dtb", [P, HEADS])
            pT = [pst(f"n_pT{k}", [P, SEQS, P]) for k in range(2)]
            pD = [pst(f"n_pD{k}", [P, 512]) for k in range(2)]
            names = ("stat", "var", "p1", "p2", "p3", "p4", "p5", "p6", "hnr", "turned", "xsr", "kept", "halo",
                     "raw", "rawr", "biasl")
            (s_stat, s_var, s_p1, s_p2, s_p3, s_p4, s_p5, s_p6, s_hn, s_turn, s_xs, s_kept, s_halo, s_raw,
             s_rawr, s_dtb) = (sem("n_" + n) for n in names)
            s_x = [sem("n_x0"), sem("n_x1")]
            s_p5b = sem("n_p5b")
            x_v = x.rearrange("b (s p) d -> s p b d", p=P)
            block = st.enter_context(nc.Block())

            @block.sync
            def _(sp):
                sp.dma_start(dtb[:, :], dt_bias.partition_broadcast(P)).then_inc(s_dtb, 16)
                for k in range(2):
                    sp.dma_start(xin[:, k], x_v[k]).then_inc(s_x[k], 16)
                with sp.Fori(1, STEPS // 2) as j:
                    for k in range(2):
                        sp.wait_ge(s_hn, 2 * j + k - 1)
                        sp.dma_start(xin[:, k], x_v[bass.ds(2 * j + k, 1)].rearrange("a p b d -> p (a b) d")).then_inc(s_x[k], 16)

            @block.vector
            def _(v):
                def statistics(g, k, n):
                    v.wait_ge(s_x[k], 16 * (n + 1))
                    need(v, s_p6, g, 2)
                    need(v, s_var, g, 2)
                    for b in range(SEQS):
                        i = v.bn_stats(stats[:, k, b, :], xin[:, k, b, :])
                    i.then_inc(s_stat, 1)
                    need_apart(v, s_stat, g)
                    for b in range(SEQS):
                        i = v.bn_aggr(mv[:, k, b, :], stats[:, k, b, :])
                    i.then_inc(s_var, 1)

                def apply(g, k):
                    need(v, s_p6, g)
                    need(v, s_turn, g, 2)
                    for b in range(SEQS):
                        i = v.tensor_scalar(hn[:, k, b, :], xin[:, k, b, :], mv[:, k, b, 0:1],
                                            small[:, k, 5, b:b + 1], ALU.subtract, ALU.mult)
                    i.then_inc(s_hn, 1)

                def raw_dt(g, k):
                    need(v, s_raw, g)
                    i = v.tensor_tensor(dt[:, bass.ds(SEQS * g, SEQS), :], pD[k][:, 0:SEQS * HEADS].rearrange("p (b h) -> p b h", h=HEADS),
                                        dtb[:, :].unsqueeze(1).broadcast_to([P, SEQS, HEADS]), ALU.add)
                    i.then_inc(s_rawr, 1)
                v.wait_ge(s_dtb, 16)
                for i in range(4):
                    statistics(i, i % 2, i // 2)
                    if i >= 1:
                        apply(i - 1, (i - 1) % 2)
                    if i >= 3:
                        raw_dt(i - 3, (i - 3) % 2)
                with v.Fori(2, STEPS // 2) as j:
                    for k in range(2):
                        statistics(2 * j + k, k, j)
                        apply(2 * j + k - 1, 1 - k)
                        raw_dt(2 * j + k - 3, 1 - k)
                for i in range(STEPS, STEPS + 3):
                    if i < STEPS + 1:
                        apply(i - 1, (i - 1) % 2)
                    raw_dt(i - 3, (i - 3) % 2)

            @block.gpsimd
            def _(g_):
                def roots(g, k):
                    m, s = mv[:, k], small[:, k]
                    need_apart(g_, s_var, g)
                    need_apart(g_, s_hn, g, 2)
                    g_.tensor_scalar(s[:, 0], m[:, :, 1], EPS, None, ALU.add).then_inc(s_p1, 1)
                    need_apart(g_, s_p1, g)
                    g_.tensor_tensor(s[:, 1], s[:, 0], half[:, 0:SEQS], ALU.pow).then_inc(s_p2, 1)
                    need_apart(g_, s_p2, g)
                    g_.tensor_tensor(s[:, 2], s[:, 1], s[:, 1], ALU.mult).then_inc(s_p3, 1)
                    g_.tensor_copy(rstd[:, bass.ds(SEQS * g, SEQS)], s[:, 1])
                    need_apart(g_, s_p3, g)
                    g_.tensor_tensor(s[:, 3], s[:, 2], m[:, :, 1], ALU.mult).then_inc(s_p4, 1)
                    g_.tensor_copy(mean[:, bass.ds(SEQS * g, SEQS)], m[:, :, 0])
                    need_apart(g_, s_p4, g)
                    g_.tensor_scalar(s[:, 4], s[:, 3], EPS, None, ALU.add).then_inc(s_p5, 1)
                    need_apart(g_, s_p5, g)
                    g_.tensor_tensor(s[:, 2], s[:, 4], half[:, 0:SEQS], ALU.pow).then_inc(s_p5b, 1)
                    need_apart(g_, s_p5b, g)
                    g_.tensor_tensor(s[:, 5], s[:, 2], s[:, 1], ALU.mult).then_inc(s_p6, 1)

                def store(g, k):
                    need_apart(g_, s_xs, g)
                    g_.tensor_copy(xT[:, bass.ds(SEQS * g, SEQS), HALO:XBLK], xs[:, k]).then_inc(s_kept, 1)
                    g_.tensor_copy(xT[:, bass.ds(SEQS * g + SEQS, SEQS), 0:HALO], xs[:, k, :, P - HALO:P]).then_inc(s_halo, 1)
                skewed(g_, STEPS, 2, 4, [(0, roots), (2, store)])

            @block.tensor
            def _(pe):
                def turn(g, k):
                    need(pe, s_hn, g)
                    need(pe, s_xs, g, 2)
                    for b in range(SEQS):
                        i = pe.transpose(pT[k][:, b, :], hn[:, k, b, :], ident[:, :])
                    i.then_inc(s_turn, 1)

                def dts(g, k):
                    need(pe, s_xs, g)
                    need(pe, s_rawr, g, 2)
                    for b in range(SEQS):
                        i = pe.matmul(pD[k][:, HEADS * b:HEADS * (b + 1)], xs[:, k, b, :], w_dt[:, :],
                                      start=True, stop=True)
                    i.then_inc(s_raw, 1)
                skewed(pe, STEPS, 2, 4, [(0, turn), (1, dts)])

            @block.scalar
            def _(a):
                def affine(g, k):
                    need(a, s_turn, g)
                    need(a, s_halo, g, 2)
                    need(a, s_kept, g, 2)
                    need(a, s_raw, g, 2)
                    for h in range(2):
                        i = a.activation(xs[:, k, 4 * h:4 * h + 4, :], pT[k][:, 4 * h:4 * h + 4, :], ACT.Identity,
                                         bias=lnb[:, 0:1], scale=lnw[:, 0:1])
                    i.then_inc(s_xs, 1)
                skewed(a, STEPS, 2, 4, [(0, affine)])

        with ExitStack() as st:
            st.callback(stage_over)
            def pst(name, shape):
                return st.enter_context(nc.psum_tensor(name, shape, F32))
            alog = st.enter_context(nc.sbuf_tensor("d_alog", [P, HEADS], F32))
            aneg = st.enter_context(nc.sbuf_tensor("d_aneg", [P, HEADS], F32))
            pc = [pst(f"d_pc{q}", [P, 512]) for q in range(4)]
            pg = [pst(f"d_pg{q}", [P, 512]) for q in range(4)]
            s_al, s_abs, s_exp, s_ln, s_a, s_neg, s_dt, s_da, s_pc, s_pg, s_post, s_pre, s_gap, s_fin = (
                sem("d_" + n) for n in ("al", "abs", "exp", "ln", "a", "neg", "dt", "da", "pc", "pg", "post",
                                        "pre", "gap", "fin"))
            QT = TILES // 4
            block = st.enter_context(nc.Block())

            def quarter(f, q):
                return f[:, QT * q:QT * (q + 1), :]

            def flat(f, q):
                return quarter(f, q).rearrange("p t h -> p (t h)")

            @block.sync
            def _(sp):
                sp.dma_start(alog[:, :], A_log.partition_broadcast(P)).then_inc(s_al, 16)

            @block.scalar
            def _(a):
                for q in range(4):
                    a.activation(flat(work, q), flat(dt, q), ACT.Abs).then_inc(s_abs, 1)
                a.wait_ge(s_al, 16)
                a.activation(aneg[:, :], alog[:, :], ACT.Exp).then_inc(s_a, 1)
                for q in range(4):
                    a.wait_ge(s_abs, q + 1)
                    a.activation(flat(work, q), flat(work, q), ACT.Exp, scale=-1.0).then_inc(s_exp, 1)
                for q in range(4):
                    a.wait_ge(s_exp, q + 1)
                    a.activation(flat(work, q), flat(work, q), ACT.Ln, bias=1.0).then_inc(s_ln, 1)
                for q in range(4):
                    a.wait_ge(s_pc, q + 1)
                    a.activation(flat(post, q), pc[q][:, :], ACT.Exp).then_inc(s_post, 1)
                    a.activation(flat(pre, q), pc[q][:, :], ACT.Exp, scale=-1.0).then_inc(s_pre, 1)
                for f, dst in enumerate((gapA, gapB, tail)):
                    for q in range(4):
                        a.wait_ge(s_pg, 4 * f + q + 1)
                        a.activation(flat(dst, q), pg[q][:, :], ACT.Exp).then_inc(s_gap, 1)

            @block.vector
            def _(v):
                v.wait_ge(s_a, 1)
                v.tensor_scalar(alog[:, :], aneg[:, :], -1.0, None, ALU.mult).then_inc(s_neg, 1)
                for q in range(4):
                    v.wait_ge(s_ln, q + 1)
                    v.scalar_tensor_tensor(out=flat(dt, q), in0=flat(dt, q), scalar=0.0, in1=flat(work, q),
                                           op0=ALU.max, op1=ALU.add).then_inc(s_dt, 1)
                v.wait_ge(s_neg, 1)
                for q in range(4):
                    v.wait_ge(s_dt, q + 1)
                    v.tensor_tensor(quarter(da, q), quarter(dt, q), alog[:, :].unsqueeze(1).broadcast_to([P, QT, HEADS]),
                                    ALU.mult).then_inc(s_da, 1)
                for q in range(4):
                    v.wait_ge(s_pre, q + 1)
                    v.tensor_tensor(flat(pre, q), flat(pre, q), flat(dt, q), ALU.mult).then_inc(s_fin, 1)
                v.wait_ge(s_gap, 12)
                v.tensor_tensor(gapA[:, SEQS:TILES, :], gapA[:, SEQS:TILES, :], tail[:, 0:TILES - SEQS, :],
                                ALU.mult).then_inc(s_fin, 1)

            @block.tensor
            def _(pe):
                for q in range(4):
                    pe.wait_ge(s_da, q + 1)
                    pe.matmul(pc[q][:, :], centre[:, :], flat(da, q), start=True, stop=True).then_inc(s_pc, 1)
                for f in range(3):
                    for q in range(4):
                        if f:
                            pe.wait_ge(s_gap, 4 * f + q - 3)
                        pe.matmul(pg[q][:, :], spans[:, f, :], flat(da, q), start=True, stop=True).then_inc(s_pg, 1)

        with ExitStack() as st:
            st.callback(stage_over)
            NB = 4

            def sbt(name, shape, dt=F32):
                return st.enter_context(nc.sbuf_tensor(name, shape, dt))

            def pst(name, shape=[P, 512]):
                return st.enter_context(nc.psum_tensor(name, shape, F32))
            xs = sbt("s_xs", [P, NB, XBLK])
            xz = sbt("s_xz", [P, NB, 2 * INNER])
            bs = sbt("s_b", [P, NB, P])
            cs = sbt("s_c", [P, NB, 2, 192])
            bt = sbt("s_bt", [P, NB, 2, P])
            gm = sbt("s_gm", [P, NB, P])
            xa = sbt("s_xa", [P, NB, INNER])
            dx = sbt("s_dx", [P, NB, INNER])
            state = sbt("s_state", [P, SEQS, INNER])
            sa = sbt("s_sa", [P, NB, INNER])
            ua = sbt("s_ua", [P, INNER])
            sB = sbt("s_sb", [P, NB, INNER])
            y1 = sbt("s_y1", [P, INNER])
            y2 = sbt("s_y2", [P, INNER])
            yg = sbt("s_yg", [P, NB, INNER])
            sq = sbt("s_sq", [P, INNER])
            yt = sbt("s_yt", [P, NB, 2, P])
            pXZ = [pst("s_pXZ0"), pst("s_pXZ1")]
            pBC, pBt, pG, pS, pY, pO = (pst("s_" + n) for n in ("pBC", "pBt", "pG", "pS", "pY", "pO"))
            (s_z, s_xs, s_pxz, s_pbc, s_xz, s_b, s_c, s_pg, s_gm, s_pbt, s_bt, s_xa, s_dx, s_ps, s_sa, s_ua, s_sb,
             s_st, s_py, s_y1, s_y2, s_yg, s_sq, s_pyt, s_yt, s_po, s_o) = (sem("s_" + n) for n in (
                 "z", "xs", "pxz", "pbc", "xz", "b", "c", "pg", "gm", "pbt", "bt", "xa", "dx", "ps", "sa", "ua",
                 "sb", "st", "py", "y1", "y2", "yg", "sq", "pyt", "yt", "po", "o"))
            block = st.enter_context(nc.Block())
            HEAD = 12

            def heads(ap):
                return ap.rearrange("p (h c) -> p h c", c=HD)

            def spread(f, t):
                return f[:, bass.ds(t, 1), :].rearrange("p a h -> p (a h)").unsqueeze(2).broadcast_to([P, HEADS, HD])

            def c_pair(k):
                return cs[:, k].rearrange("p a c -> p (a c)").rearrange("p (a c) -> p a c", c=192)[:, :, 0:CHUNK]

            def c_chunk(k, c):
                flat_c = cs[:, k].rearrange("p a c -> p (a c)")
                return flat_c[:, P * c:P * (c + 1)]

            @block.gpsimd
            def _(g):
                def fetch(t, k):
                    need_apart(g, s_pbc, t, NB)
                    need_apart(g, s_pxz, t, NB)
                    g.tensor_copy(xs[:, k, :], xT[:, bass.ds(t, 1), :].rearrange("p a c -> p (a c)")).then_inc(s_xs, 1)

                def scale(t, k):
                    need_apart(g, s_xz, t)
                    need_apart(g, s_py, t, NB)
                    g.tensor_tensor(heads(xa[:, k, :]), heads(xz[:, k, 0:INNER]), spread(pre, t), ALU.mult).then_inc(s_xa, 1)
                    need_apart(g, s_y2, t, NB)
                    g.tensor_tensor(heads(dx[:, k, :]), heads(xz[:, k, 0:INNER]),
                                    dskip[:, :].unsqueeze(2).broadcast_to([P, HEADS, HD]), ALU.mult).then_inc(s_dx, 1)
                skewed(g, TILES, NB, HEAD, [(0, fetch), (1, scale)])

            @block.tensor
            def _(pe):
                def project(t, k):
                    b = k % 2
                    need(pe, s_xs, t)
                    need(pe, s_xz, t, 2)
                    for tap in range(TAPS):
                        pe.matmul(pXZ[b][:, 0:INNER], xs[:, k, tap:tap + P], w_conv[:, tap, 0:INNER],
                                  start=(tap == 0), stop=False)
                    pe.matmul(pXZ[b][:, 0:INNER], ones_bf[:, :], xbias3[:, :], start=False, stop=True)
                    pe.matmul(pXZ[b][:, INNER:2 * INNER], xs[:, k, HALO:XBLK], w_z[:, :],
                              start=True, stop=True).then_inc(s_pxz, 1)
                    need(pe, s_c, t, 1)
                    need(pe, s_b, t, 1)
                    for m in range(2):
                        c0 = INNER + STATE * m
                        for tap in range(TAPS):
                            i = pe.matmul(pBC[:, P * m:P * (m + 1)], w_conv[:, tap, c0:c0 + STATE],
                                          xs[:, k, tap:tap + P], start=(tap == 0), stop=(tap == TAPS - 1))
                    i.then_inc(s_pbc, 1)

                def gram(t, k):
                    need(pe, s_b, t)
                    need(pe, s_bt, t, 1)
                    pe.transpose(pBt[:, 0:P], bs[:, k, :], ident[:, :]).then_inc(s_pbt, 1)
                    need(pe, s_c, t)
                    need(pe, s_gm, t, 1)
                    pe.matmul(pG[:, 0:P].rearrange("p (a c) -> p a c", a=2), bs[:, k, :], c_pair(k),
                              start=True, stop=True).then_inc(s_pg, 1)

                def states(t, k):
                    need(pe, s_bt, t)
                    need(pe, s_xa, t)
                    need(pe, s_st, t, 1)
                    for c in range(2):
                        i = pe.matmul(pS[:, INNER * c:INNER * (c + 1)], bt[:, k, c, :], xa[:, k, :], start=True, stop=True)
                    i.then_inc(s_ps, 1)

                def outputs(t, k):
                    need(pe, s_gm, t)
                    need(pe, s_y1, t, 1)
                    pe.matmul(pY[:, 0:INNER], gm[:, k, :], xa[:, k, :], start=True, stop=False)
                    need(pe, s_sa, t)
                    pe.matmul(pY[:, 0:INNER], c_chunk(k, 0), sa[:, k, :], start=False, stop=False)
                    need(pe, s_sb, t)
                    pe.matmul(pY[:, 0:INNER], c_chunk(k, 1), sB[:, k, :], start=False, stop=True).then_inc(s_py, 1)

                def turn(t, k):
                    need(pe, s_yg, t)
                    need(pe, s_o, t, 1)
                    for c in range(2):
                        i = pe.transpose(pO[:, P * c:P * (c + 1)], yg[:, k, P * c:P * (c + 1)], ident[:, :])
                    i.then_inc(s_pyt, 1)

                def out_project(t, k):
                    need(pe, s_yt, t)
                    for c in range(2):
                        i = pe.matmul(pO[:, 2 * P:3 * P], yt[:, k, c, :], w_out[:, c, :], start=(c == 0), stop=(c == 1))
                    i.then_inc(s_po, 1)
                skewed(pe, TILES, NB, HEAD, [(5, turn), (3, outputs), (1, gram), (0, project), (2, states), (5, out_project)])

            @block.scalar
            def _(a):
                def silus(t, k):
                    need(a, s_pxz, t)
                    need(a, s_dx, t, NB)
                    need(a, s_xa, t, NB)
                    need(a, s_yg, t, NB)
                    a.activation(xz[:, k, :], pXZ[k % 2][:, :], ACT.Silu).then_inc(s_xz, 1)
                    need(a, s_pbc, t)
                    need(a, s_pg, t, NB)
                    need(a, s_pbt, t, NB)
                    a.activation(bs[:, k, :], pBC[:, 0:P], ACT.Silu, bias=bc_bias[:, 0:1]).then_inc(s_b, 1)
                    need(a, s_py, t, NB)
                    a.activation(c_pair(k), pBC[:, P:2 * P].rearrange("p (a c) -> p a c", a=2), ACT.Silu,
                                 bias=bc_bias[:, 1:2]).then_inc(s_c, 1)

                def turned_b(t, k):
                    need(a, s_pbt, t)
                    need(a, s_ps, t, NB)
                    for c in range(2):
                        r = slice(CHUNK * c, CHUNK * (c + 1))
                        i = a.activation(bt[r, k, c, :], pBt[r, 0:P], ACT.Copy)
                    i.then_inc(s_bt, 1)

                def squares(t, k):
                    need(a, s_yg, t)
                    need(a, s_sq, t, 1)
                    a.activation(sq[:, :], yg[:, k, :], ACT.Square, accum_out=ssq[:, bass.ds(t, 1)]).then_inc(s_sq, 1)
                    need(a, s_pyt, t)
                    need(a, s_po, t, NB)
                    a.activation(yt[:, k].rearrange("p c n -> p (c n)"), pO[:, 0:2 * P], ACT.Copy).then_inc(s_yt, 1)

                def projected(t, k):
                    need(a, s_po, t)
                    a.activation(proj[:, bass.ds(t, 1), :].rearrange("p a d -> p (a d)"), pO[:, 2 * P:3 * P],
                                 ACT.Copy).then_inc(s_o, 1)
                a.wait_ge(s_z, 3)
                skewed(a, TILES, NB, HEAD, [(5, squares), (5, projected), (1, turned_b), (0, silus)])

            @block.vector
            def _(v):
                def mask(t, k):
                    need(v, s_pg, t)
                    need(v, s_py, t, NB)
                    v.tensor_tensor(gm[:, k, :], pG[:, 0:P], causal[:, :], ALU.mult).then_inc(s_gm, 1)

                def carry(t, k):
                    q = t % SEQS if isinstance(t, int) else t & (SEQS - 1)
                    mine = state[:, bass.ds(q, 1), :].rearrange("p a c -> p (a c)")
                    need(v, s_py, t, NB)
                    need(v, s_st, t, 1)
                    v.tensor_tensor(heads(sa[:, k, :]), heads(mine), spread(gapA, t), ALU.mult).then_inc(s_sa, 1)
                    need(v, s_ps, t)
                    need(v, s_sa, t)
                    need(v, s_sb, t, 1)
                    v.tensor_tensor(ua[:, :], sa[:, k, :], pS[:, 0:INNER], ALU.add).then_inc(s_ua, 1)
                    need(v, s_ua, t)
                    v.tensor_tensor(heads(sB[:, k, :]), heads(ua[:, :]), spread(gapB, t), ALU.mult).then_inc(s_sb, 1)
                    need(v, s_sb, t)
                    v.tensor_tensor(mine, sB[:, k, :], pS[:, INNER:2 * INNER], ALU.add).then_inc(s_st, 1)

                def gate(t, k):
                    need(v, s_py, t)
                    need(v, s_y2, t, 1)
                    v.tensor_tensor(heads(y1[:, :]), heads(pY[:, 0:INNER]), spread(post, t), ALU.mult).then_inc(s_y1, 1)
                    need(v, s_y1, t)
                    need(v, s_dx, t)
                    need(v, s_yg, t, 1)
                    v.tensor_tensor(y2[:, :], y1[:, :], dx[:, k, :], ALU.add).then_inc(s_y2, 1)
                    need(v, s_y2, t)
                    need(v, s_sq, t, NB)
                    need(v, s_pyt, t, NB)
                    v.tensor_tensor(yg[:, k, :], y2[:, :], xz[:, k, INNER:2 * INNER], ALU.mult).then_inc(s_yg, 1)
                v.memset(cs[:, :, :, :], 0.0).then_inc(s_z, 1)
                v.memset(bt[:, :, :, :], 0.0).then_inc(s_z, 1)
                v.memset(state[:, :, :], 0.0).then_inc(s_z, 1)
                v.wait_ge(s_z, 3)
                skewed(v, TILES, NB, HEAD, [(4, gate), (2, carry), (1, mask)])

        with ExitStack() as st:
            st.callback(stage_over)
            NB, G = 4, 2
            GROUPS, N = TILES // G, G * P

            def sbt(name, shape, dt=F32):
                return st.enter_context(nc.sbuf_tensor(name, shape, dt))

            def pst(name, shape=[P, 512]):
                return st.enter_context(nc.psum_tensor(name, shape, F32))
            rsc = sbt("m_rsc", [P, 3, TILES])
            minus_m = sbt("m_mm", [P, TILES])
            hmr = sbt("m_half", [P, TILES])
            xin = sbt("m_x", [P, 8, G, D])
            res = sbt("m_res", [P, NB, G, D])
            h0 = sbt("m_h0", [P, NB, G, D])
            h0b = sbt("m_h0b", [P, NB, G, D])
            stats = sbt("m_stats", [P, 3, NB, G, 6])
            mv = sbt("m_mv", [P, 3, NB, G, 2])
            ve = sbt("m_ve", [P, 3, NB, G])
            rs = sbt("m_rs", [P, 3, NB, G])
            hn = sbt("m_hn", [P, NB, G, D])
            hT = sbt("m_hT", [P, NB, N])
            h1 = sbt("m_h1", [P, NB, NF, N])
            at = sbt("m_at", [P, NB, G, D])
            un = sbt("m_un", [P, NB, G, D])
            xl = sbt("m_xl", [P, NB, G, D])
            xlT = sbt("m_xlT", [P, NB, N])
            pT, pX, pM0, pM1, pL = (pst("m_" + n) for n in ("pT", "pX", "pM0", "pM1", "pL"))
            pM = [pM0, pM1]
            pH = [pst("m_pH0", [P, 512]), pst("m_pH1", [P, 512])]
            s_x = [sem(f"m_x{k}") for k in range(8)]
            (s_r, s_res, s_h0, s_h0b, s_pT, s_hT, s_ph, s_h1a, s_h1b, s_pm, s_at, s_un, s_x1, s_xl, s_keep, s_px, s_xlT, s_pl,
             s_lg, s_hn, s_extra) = (sem("m_" + n) for n in (
                 "r", "res", "h0", "h0b", "pT", "hT", "ph", "h1a", "h1b", "pm", "at", "un", "xone", "xl", "keep", "px",
                 "xlT", "pl", "lg", "hn", "extra"))
            s_ph2 = sem("m_ph2")
            s_st = [sem(f"m_st{i}") for i in range(3)]
            s_var = [sem(f"m_var{i}") for i in range(3)]
            s_ve = [sem(f"m_ve{i}") for i in range(3)]
            s_rs = [sem(f"m_rs{i}") for i in range(3)]
            HEAD = 12
            x_v = x.rearrange("(u v) (s p) d -> s u p v d", p=P, v=G)
            block = st.enter_context(nc.Block())

            def skewed8(eng, stages, slotted):
                def run(stage, t, m):
                    stage(t, m % NB, m % 8) if stage in slotted else stage(t, m % NB)
                for i in range(16):
                    for lag, stage in stages:
                        if 0 <= i - lag < GROUPS:
                            run(stage, i - lag, i - lag)
                with eng.Fori(2, GROUPS // 8) as j:
                    for u in range(8):
                        for lag, stage in stages:
                            run(stage, 8 * j + u - lag, u - lag)
                for i in range(GROUPS, GROUPS + max(lag for lag, _ in stages)):
                    for lag, stage in stages:
                        if 0 <= i - lag < GROUPS:
                            run(stage, i - lag, i - lag)

            @block.sync
            def _(sp):
                U = SEQS // G
                for g in range(8):
                    sp.dma_start(xin[:, g], x_v[g // U, g % U]).then_inc(s_x[g], 16)
                with sp.Fori(1, GROUPS // 8) as j:
                    for u in range(8):
                        sp.wait_ge(s_x1, 8 * j + u - 7)
                        sp.dma_start(xin[:, u], x_v[bass.ds(2 * j + u // U, 1), u % U].rearrange("a p v d -> p (a v) d")).then_inc(s_x[u], 16)

            def tiles(ap, g):
                return ap[:, bass.ds(G * g, G), :]

            @block.gpsimd
            def _(g_):
                def root(n):
                    def stage(g, k):
                        need_apart(g_, s_var[n], g)
                        g_.tensor_scalar(ve[:, n, k], mv[:, n, k, :, 1], EPS, None, ALU.add).then_inc(s_ve[n], 1)
                        need_apart(g_, s_ve[n], g)
                        g_.tensor_tensor(rs[:, n, k], ve[:, n, k], half[:, 0:G], ALU.pow).then_inc(s_rs[n], 1)
                    return stage

                def residual_bias(g, k):
                    need_apart(g_, s_h0, g)
                    need_apart(g_, s_at, g, NB)
                    g_.tensor_tensor(h0b[:, k], h0[:, k], b2row[:, :].unsqueeze(1).broadcast_to([P, G, D]), ALU.add).then_inc(s_h0b, 1)

                def add_x(g, k, slot):
                    need_apart(g_, s_un, g)
                    g_.tensor_tensor(tiles(x1, g), xin[:, slot], un[:, k], ALU.add).then_inc(s_x1, 1)

                def keep(g, k):
                    need_apart(g_, s_xl, g)
                    g_.tensor_copy(rows[:, bass.ds(G * g, G), 0:D], xl[:, k]).then_inc(s_keep, 1)
                g_.tensor_scalar(rsc[:, 0], ssq[:, :], 1.0 / INNER, EPS, ALU.mult, ALU.add).then_inc(s_extra, 1)
                g_.memset(hmr[:, :], -0.5).then_inc(s_extra, 1)
                g_.tensor_tensor(rsc[:, 1], mean[:, :], rstd[:, :], ALU.mult).then_inc(s_extra, 1)
                g_.wait_ge(s_extra, 3)
                g_.tensor_tensor(rsc[:, 2], rsc[:, 0], hmr[:, :], ALU.pow).then_inc(s_r, 1)
                g_.tensor_scalar(minus_m[:, :], rsc[:, 1], -1.0, None, ALU.mult).then_inc(s_r, 1)
                skewed8(g_, [(0, root(0)), (1, residual_bias), (4, root(1)), (5, add_x), (6, root(2)), (7, keep)], {add_x})

            @block.scalar
            def _(a):
                def centre_x(g, k, slot):
                    a.wait_ge(s_x[slot], 16 * (g // 8 + 1) if isinstance(g, int) else 16 * (g >> 3) + 16)
                    need(a, s_h0, g, NB)
                    for i in range(G):
                        t = bass.ds(G * g + i, 1)
                        ins = a.activation(res[:, k, i, :], xin[:, slot, i, :], ACT.Identity, bias=minus_m[:, t], scale=rstd[:, t])
                    ins.then_inc(s_res, 1)

                def turned(g, k):
                    need(a, s_pT, g)
                    need(a, s_ph, g, NB)
                    a.activation(hT[:, k, :], pT[:, 0:N], ACT.Identity, bias=lnb[:, 0:1], scale=lnw[:, 0:1]).then_inc(s_hT, 1)

                def relus(g, k):
                    need(a, s_pm, g, NB)
                    a.wait_ge(s_ph, g + 1)
                    for c in range(NF // 2):
                        ins = a.activation(h1[:, k, c, :], pH[0][:, N * c:N * (c + 1)], ACT.Relu, bias=b1_col[:, c:c + 1])
                    ins.then_inc(s_h1a, 1)

                def turned_xl(g, k):
                    need(a, s_px, g)
                    need(a, s_pl, g, NB)
                    a.activation(xlT[:, k, :], pX[:, 0:N], ACT.Copy).then_inc(s_xlT, 1)
                a.wait_ge(s_r, 2)
                skewed8(a, [(0, centre_x), (2, turned), (3, relus), (7, turned_xl)], {centre_x})

            @block.vector
            def _(v):
                def norm_stats(n, src, g, k):
                    need(v, s_rs[n], g, NB)
                    for i in range(G):
                        ins = v.bn_stats(stats[:, n, k, i, :], src(i))
                    ins.then_inc(s_st[n], 1)
                    need_apart(v, s_st[n], g)
                    for i in range(G):
                        ins = v.bn_aggr(mv[:, n, k, i, :], stats[:, n, k, i, :])
                    ins.then_inc(s_var[n], 1)

                def normed(n, dst, src, k, done):
                    for i in range(G):
                        ins = v.tensor_scalar(dst[:, k, i, :], src(i), mv[:, n, k, i, 0:1], rs[:, n, k, i:i + 1],
                                              ALU.subtract, ALU.mult)
                    ins.then_inc(done, 1)

                def residual(g, k):
                    need(v, s_res, g)
                    need(v, s_h0b, g, NB)
                    need(v, s_hn, g, NB)
                    for i in range(G):
                        t = bass.ds(G * g + i, 1)
                        ins = v.scalar_tensor_tensor(out=h0[:, k, i, :], in0=proj[:, t, :].rearrange("p a d -> p (a d)"),
                                                     scalar=rsc[:, 2, t], in1=res[:, k, i, :], op0=ALU.mult, op1=ALU.add)
                    ins.then_inc(s_h0, 1)
                    need(v, s_h0, g)
                    norm_stats(0, lambda i: h0[:, k, i, :], g, k)

                def apply0(g, k):
                    need(v, s_rs[0], g)
                    need(v, s_pT, g, NB)
                    normed(0, hn, lambda i: h0[:, k, i, :], k, s_hn)

                def relus(g, k):
                    need(v, s_pm, g, NB)
                    v.wait_ge(s_ph2, g + 1)
                    for c in range(NF // 2, NF):
                        c2 = c - NF // 2
                        ins = v.tensor_scalar(h1[:, k, c, :], pH[1][:, N * c2:N * (c2 + 1)], b1_col[:, c:c + 1], 0.0, ALU.add, ALU.max)
                    ins.then_inc(s_h1b, 1)

                def mlp_out(g, k):
                    need(v, s_pm, g)
                    need(v, s_h0b, g)
                    need(v, s_un, g, NB)
                    v.tensor_tensor(at[:, k].rearrange("p a d -> p (a d)"), pM[k % 2][:, 0:N], h0b[:, k].rearrange("p a d -> p (a d)"), ALU.add).then_inc(s_at, 1)
                    need(v, s_at, g)
                    norm_stats(1, lambda i: at[:, k, i, :], g, k)

                def apply1(g, k):
                    need(v, s_rs[1], g)
                    need(v, s_x1, g, NB)
                    normed(1, un, lambda i: at[:, k, i, :], k, s_un)

                def x1_of(g):
                    return lambda i: x1[:, bass.ds(G * g + i, 1), :].rearrange("p a d -> p (a d)")

                def stats_x1(g, k):
                    need(v, s_x1, g)
                    norm_stats(2, x1_of(g), g, k)

                def apply2(g, k):
                    need(v, s_rs[2], g)
                    need(v, s_px, g, NB)
                    need(v, s_keep, g, NB)
                    normed(2, xl, x1_of(g), k, s_xl)

                def logit(g, k):
                    need(v, s_pl, g)
                    v.tensor_tensor(tiles(logits, g), pL[:, 0:G * EXPERTS].rearrange("p (a e) -> p a e", e=EXPERTS),
                                    brow[:, :].unsqueeze(1).broadcast_to([P, G, EXPERTS]), ALU.add).then_inc(s_lg, 1)
                v.wait_ge(s_r, 2)
                skewed8(v, [(0, residual), (1, apply0), (3, relus), (4, mlp_out), (5, apply1), (6, stats_x1), (7, apply2),
                            (8, logit)], set())

            @block.tensor
            def _(pe):
                def turn(g, k):
                    need(pe, s_hn, g)
                    need(pe, s_hT, g, 1)
                    for i in range(G):
                        ins = pe.transpose(pT[:, P * i:P * (i + 1)], hn[:, k, i, :], ident[:, :])
                    ins.then_inc(s_pT, 1)

                def up(g, k):
                    need(pe, s_hT, g)
                    for half_, (done, free) in enumerate(((s_ph, s_h1a), (s_ph2, s_h1b))):
                        need(pe, free, g, 1)
                        for c in range(2):
                            m = 2 * half_ + c
                            ins = pe.matmul(pH[half_][:, N * c:N * (c + 1)], w_m1[:, P * m:P * (m + 1)], hT[:, k, :], start=True, stop=True)
                        ins.then_inc(done, 1)

                def down(g, k):
                    need(pe, s_h1a, g)
                    need(pe, s_h1b, g)
                    need(pe, s_at, g, 2)
                    for i in range(G):
                        for c in range(NF):
                            ins = pe.matmul(pM[k % 2][:, P * i:P * (i + 1)], h1[:, k, c, P * i:P * (i + 1)], w_m2[:, c, :],
                                            start=(c == 0), stop=(c == NF - 1))
                    ins.then_inc(s_pm, 1)

                def turn_xl(g, k):
                    need(pe, s_xl, g)
                    need(pe, s_xlT, g, 1)
                    for i in range(G):
                        ins = pe.transpose(pX[:, P * i:P * (i + 1)], xl[:, k, i, :], ident[:, :])
                    ins.then_inc(s_px, 1)

                def route(g, k):
                    need(pe, s_xlT, g)
                    need(pe, s_lg, g, 1)
                    for i in range(G):
                        ins = pe.matmul(pL[:, EXPERTS * i:EXPERTS * (i + 1)], xlT[:, k, P * i:P * (i + 1)], w_r[:, :], start=True, stop=True)
                    ins.then_inc(s_pl, 1)
                skewed8(pe, [(8, route), (7, turn_xl), (1, turn), (2, up), (3, down)], set())

        with ExitStack() as st:
            st.callback(stage_over)
            def sbt(name, shape, dt=F32):
                return st.enter_context(nc.sbuf_tensor(name, shape, dt))

            def pst(name, shape=[P, 512]):
                return st.enter_context(nc.psum_tensor(name, shape, F32))
            E = EXPERTS
            pr, eq, w, gt_, f1, f2, gates, selq = (sbt("r_" + n, [P, TILES, E]) for n in (
                "pr", "eq", "w", "gt", "f1", "f2", "gates", "selq"))
            rev = sbt("r_rev", [P, E])
            mx, sm, m1, m2, wm, tok = (sbt("r_" + n, [P, TILES]) for n in ("mx", "sm", "m1", "m2", "wm", "tok"))
            idx = [sbt(f"r_idx{c}", [P, TILES], U32) for c in range(2)]
            gq = sbt("r_gq", [P, 4, P])
            gT, above, same, scg, sce, pos, full = (sbt("r_" + n, [P, 512]) for n in (
                "gT", "above", "same", "scg", "sce", "pos", "full"))
            thr, cand, bit, nxt, pick = (sbt("r_" + n, [P, 1], I32) for n in ("thr", "cand", "bit", "nxt", "pick"))
            cnt = sbt("r_cnt", [P, 1])
            ends = sbt("r_ends", [P, 2])
            offs = sbt("r_offs", [P, 5])
            base = sbt("r_base", [P, 1])
            same_e = sbt("r_same_e", [P, P])
            before = sbt("r_before", [P, P])
            pG, pC, pI = pst("r_pG"), pst("r_pC"), pst("r_pI")
            s_c, s_v, s_ex, s_exp, s_q, s_pg, s_cnt, s_tot, s_end, s_off, s_pos, s_pi, s_idx, s_scat, s_go = (
                sem("r_" + n) for n in ("c", "v", "ex", "exp", "q", "pg", "cnt", "tot", "end", "off", "pos", "pi", "idx",
                                        "scat", "go"))
            s_pick, s_thr, s_nxt, s_cand = (sem("r_" + n) for n in ("pick", "thr", "nxt", "cand"))
            BITS = 30
            block = st.enter_context(nc.Block())

            def over_e(ap):
                return ap.unsqueeze(2).broadcast_to([P, TILES, E])

            def by_chunk(ap, q):
                return ap.rearrange("p (h q b) e -> p q e b h", h=2, q=4)[:, q]

            @block.gpsimd
            def _(g):
                g.memset(full[:, :], 1.0).then_inc(s_c, 1)
                g.memset(same_e[:, :], 1.0).then_inc(s_c, 1)
                g.iota(rev[:, :], [[-1, E]], base=E, channel_multiplier=0, allow_small_or_imprecise_dtypes=True).then_inc(s_c, 1)
                g.iota(tok[:, :], [[P, STEPS], [LEN, SEQS]], base=0, channel_multiplier=1, allow_small_or_imprecise_dtypes=True).then_inc(s_c, 1)
                g.memset(base[:, :], -1.0).then_inc(s_c, 1)
                g.wait_ge(s_c, 5)
                n = 5
                se = same_e[:, :].rearrange("p (e c) -> p e c", c=16)
                for b_, s_, m_ in ((0, -16, 1), (15, 16, -1)):
                    g.affine_select(out=se, in_=se, compare_op=ALU.is_ge, fill=0.0, base=b_, pattern=[[s_, E], [0, 16]],
                                    channel_multiplier=m_).then_inc(s_c, 1)
                    n += 1
                    g.wait_ge(s_c, n)
                g.affine_select(out=before[:, :], in_=same_e[:, :], compare_op=ALU.is_ge, fill=0.0, base=-1,
                                pattern=[[1, P]], channel_multiplier=-1).then_inc(s_c, 1)
                for e in range(1, E):
                    g.affine_select(out=base[:, :], in_=base[:, :], compare_op=ALU.is_ge, fill=REGION * e - 1.0,
                                    base=16 * e - 1, pattern=[[0, 1]], channel_multiplier=-1).then_inc(s_c, 1)
                    g.wait_ge(s_c, n + 1 + e)
                g.wait_ge(s_idx, 2)
                g.wait_ge(s_go, 4)
                for t in range(TILES):
                    for c in range(2):
                        g.indirect_dma_start(table, bass.IndirectOffsetOnAxis(ap=idx[c][:, t:t + 1], axis=0), rows[:, t, :],
                                             None, bounds_check=TABLE - 1, oob_is_err=False).then_inc(s_scat, 16)
                g.wait_ge(s_scat, 16 * 2 * TILES)

            @block.scalar
            def _(a):
                a.wait_ge(s_ex, 1)
                a.activation(pr[:, :, :], eq[:, :, :], ACT.Exp).then_inc(s_exp, 1)

            @block.tensor
            def _(pe):
                for q in range(4):
                    pe.wait_ge(s_q, q + 1)
                    pe.transpose(pG[:, P * q:P * (q + 1)], gq[:, q, :], ident[:, :]).then_inc(s_pg, 1)
                pe.wait_ge(s_c, 15)
                with pe.Fori(0, BITS) as i:
                    pe.wait_ge(s_cnt, i + 1)
                    pe.matmul(pC[:, 0:1], same_e[:, :], cnt[:, :], start=True, stop=True).then_inc(s_tot, 1)
                pe.wait_ge(s_end, 2)
                pe.matmul(pC[:, 0:2], before[:, :], ends[:, :], start=True, stop=True)
                pe.matmul(pC[:, 2:4], same_e[:, :], ends[:, :], start=True, stop=True).then_inc(s_off, 1)
                pe.wait_ge(s_pos, 1)
                for q in range(4):
                    pe.transpose(pI[:, P * q:P * (q + 1)], pos[:, P * q:P * (q + 1)], ident[:, :]).then_inc(s_pi, 1)

            @block.vector
            def _(v):
                chain = [0]

                def link(ins):
                    chain[0] += 1
                    ins.then_inc(s_v, 1)
                    v.wait_ge(s_v, chain[0])

                def best(src, top, first, weight):
                    link(v.tensor_reduce(top, src, AX.X, ALU.max))
                    link(v.tensor_tensor(eq[:, :, :], src, over_e(top), ALU.is_equal))
                    link(v.tensor_tensor(w[:, :, :], eq[:, :, :], rev[:, :].unsqueeze(1).broadcast_to([P, TILES, E]), ALU.mult))
                    link(v.tensor_reduce(weight, w[:, :, :], AX.X, ALU.max))
                    link(v.tensor_tensor(first, w[:, :, :], over_e(weight), ALU.is_equal))
                v.wait_ge(s_c, 5)
                link(v.tensor_reduce(mx[:, :], logits[:, :, :], AX.X, ALU.max))
                v.tensor_tensor(eq[:, :, :], logits[:, :, :], over_e(mx[:, :]), ALU.subtract).then_inc(s_ex, 1)
                v.wait_ge(s_exp, 1)
                link(v.tensor_reduce(sm[:, :], pr[:, :, :], AX.X, ALU.add))
                link(v.reciprocal(mx[:, :], sm[:, :]))
                link(v.tensor_tensor(pr[:, :, :], pr[:, :, :], over_e(mx[:, :]), ALU.mult))
                best(pr[:, :, :], m1[:, :], f1[:, :, :], wm[:, :])
                link(v.tensor_scalar(rows[:, :, D + 1], wm[:, :], -1.0, float(E), ALU.mult, ALU.add))
                link(v.scalar_tensor_tensor(out=gt_[:, :, :], in0=f1[:, :, :], scalar=-2.0, in1=pr[:, :, :], op0=ALU.mult, op1=ALU.add))
                best(gt_[:, :, :], m2[:, :], f2[:, :, :], wm[:, :])
                link(v.tensor_tensor(selq[:, :, :], f1[:, :, :], f2[:, :, :], ALU.add))
                link(v.tensor_tensor(gates[:, :, :], pr[:, :, :], selq[:, :, :], ALU.mult))
                link(v.scalar_tensor_tensor(out=gates[:, :, :], in0=selq[:, :, :], scalar=-1.0, in1=gates[:, :, :],
                                            op0=ALU.add, op1=ALU.add))
                for q in range(4):
                    v.tensor_copy(gq[:, q, :].rearrange("p (e b h) -> p e b h", e=E, h=2), by_chunk(gates[:, :, :], q)).then_inc(s_q, 1)
                v.tensor_copy(rows[:, :, D], tok[:, :]).then_inc(s_go, 1)
                v.tensor_copy(rows[:, :, D + 2], m1[:, :]).then_inc(s_go, 1)
                v.tensor_copy(rows[:, :, D + 3], m2[:, :]).then_inc(s_go, 1)
                v.memset(thr[:, :], 0)
                v.memset(bit[:, :], 1 << (BITS - 1))
                v.memset(cand[:, :], 1 << (BITS - 1))
                v.wait_ge(s_pg, 4)
                link(v.tensor_copy(gT[:, :], pG[:, :]))
                with v.Fori(0, BITS) as i:
                    v.tensor_scalar(above[:, :], gT[:, :], cand[:, :].bitcast(F32), 0.0, ALU.is_ge, ALU.add,
                                    accum_out=cnt[:, :]).then_inc(s_cnt, 1)
                    v.tensor_scalar(nxt[:, :], bit[:, :], 1, None, ALU.logical_shift_right).then_inc(s_nxt, 1)
                    v.wait_ge(s_tot, i + 1)
                    v.scalar_tensor_tensor(out=pick[:, :], in0=pC[:, 0:1], scalar=float(CAP), in1=bit[:, :],
                                           op0=ALU.is_ge, op1=ALU.mult).then_inc(s_pick, 1)
                    v.wait_ge(s_pick, i + 1)
                    v.tensor_tensor(thr[:, :], thr[:, :], pick[:, :], ALU.bitwise_or).then_inc(s_thr, 1)
                    v.wait_ge(s_nxt, i + 1)
                    v.tensor_copy(bit[:, :], nxt[:, :])
                    v.wait_ge(s_thr, i + 1)
                    v.tensor_tensor(cand[:, :], thr[:, :], nxt[:, :], ALU.bitwise_or).then_inc(s_cand, 1)
                    v.wait_ge(s_cand, i + 1)
                    v.wait_ge(s_cnt, i + 1)
                t = thr[:, :].bitcast(F32)
                v.tensor_scalar(above[:, :], gT[:, :], t, None, ALU.is_gt).then_inc(s_v, 1)
                chain[0] += 1
                link(v.tensor_scalar(same[:, :], gT[:, :], t, None, ALU.is_equal))
                v.tensor_tensor_scan(scg[:, :], full[:, :], above[:, :], 0.0, ALU.mult, ALU.add).then_inc(s_v, 1)
                chain[0] += 1
                link(v.tensor_tensor_scan(sce[:, :], full[:, :], same[:, :], 0.0, ALU.mult, ALU.add))
                v.tensor_copy(ends[:, 0:1], scg[:, 511:512]).then_inc(s_end, 1)
                v.tensor_copy(ends[:, 1:2], sce[:, 511:512]).then_inc(s_end, 1)
                v.wait_ge(s_off, 1)
                link(v.tensor_copy(offs[:, 0:4], pC[:, 0:4]))
                link(v.tensor_scalar(offs[:, 4:5], offs[:, 2:3], -1.0, float(CAP), ALU.mult, ALU.add))
                link(v.tensor_scalar(sce[:, :], sce[:, :], offs[:, 1:2], None, ALU.add))
                link(v.scalar_tensor_tensor(out=same[:, :], in0=sce[:, :], scalar=offs[:, 4:5], in1=same[:, :], op0=ALU.is_le, op1=ALU.mult))
                link(v.tensor_tensor(same[:, :], same[:, :], above[:, :], ALU.add))
                link(v.tensor_scalar(sce[:, :], sce[:, :], offs[:, 4:5], None, ALU.min))
                link(v.scalar_tensor_tensor(out=scg[:, :], in0=scg[:, :], scalar=offs[:, 0:1], in1=sce[:, :], op0=ALU.add, op1=ALU.add))
                link(v.tensor_scalar(scg[:, :], scg[:, :], base[:, 0:1], -FAR, ALU.add, ALU.add))
                link(v.tensor_tensor(scg[:, :], scg[:, :], same[:, :], ALU.mult))
                v.tensor_scalar(pos[:, :], scg[:, :], FAR, None, ALU.add).then_inc(s_pos, 1)
                for q in range(4):
                    v.wait_ge(s_pi, 4)
                    link(v.tensor_copy(by_chunk(gates[:, :, :], q), pI[:, P * q:P * (q + 1)].rearrange("p (e b h) -> p e b h", e=E, h=2)))
                for c, f in enumerate((f1, f2)):
                    link(v.tensor_tensor(w[:, :, :], f[:, :, :], gates[:, :, :], ALU.mult))
                    link(v.tensor_reduce(mx[:, :], w[:, :, :], AX.X, ALU.add))
                    v.tensor_copy(idx[c][:, :], mx[:, :]).then_inc(s_idx, 1)
                    v.wait_ge(s_idx, c + 1)
                v.wait_ge(s_v, chain[0])
                v.memset(cnt[:, :], 0.0).then_inc(s_go, 1)

        with ExitStack() as st:
            st.callback(stage_over)
            NB = 2
            G = ROWS // P
            STEPS_E = ESTEPS

            def sbt(name, shape, dt=F32):
                return st.enter_context(nc.sbuf_tensor(name, shape, dt))

            def pst(name, shape=[P, 512]):
                return st.enter_context(nc.psum_tensor(name, shape, F32))
            xg = sbt("e_xg", [P, NB, G, ROWLEN])
            info = sbt("e_info", [P, NB, 5, G])
            gate = sbt("e_gate", [P, 4, G])
            dest = sbt("e_dest", [P, 4, G], U32)
            xgT = sbt("e_xgT", [P, NB, ROWS])
            hb = sbt("e_h", [P, NB, NF, ROWS])
            ysum = sbt("e_ysum", [P, NB, G, D])
            yo = sbt("e_yo", [P, 4, G, D])
            we1 = sbt("e_w1", [P, 2, FF])
            we2 = sbt("e_w2", [P, 2, NF, D])
            be1 = sbt("e_b1", [P, 2, NF])
            be2 = sbt("e_b2", [P, 2, D])
            ecur = sbt("e_ecur", [P, 2])
            pT = [pst("e_pT0"), pst("e_pT1")]
            pH = [pst("e_pH0"), pst("e_pH1")]
            pO = [pst("e_pO0"), pst("e_pO1")]
            s_xg = [sem("e_xg0"), sem("e_xg1")]
            s_we = [sem("e_we0"), sem("e_we1")]
            s_scat = [sem(f"e_scat{k}") for k in range(4)]
            (s_e, s_ef, s_i1, s_i2, s_i3, s_gate, s_dest, s_pt, s_xgT, s_ph0, s_ph1, s_h0, s_h1, s_po, s_ys, s_yo) = (
                sem("e_" + n) for n in ("e", "ef", "i1", "i2", "i3", "gate", "dest", "pt", "xgT", "ph0", "ph1", "h0",
                                        "h1", "po", "ys", "yo"))
            s_i4 = sem("e_i4")
            TURN = 2 * STEPS_E
            TOTAL = EXPERTS * STEPS_E
            rows_v = table.rearrange("(n p r) c -> n p r c", p=P, r=G)
            block = st.enter_context(nc.Block())

            def turns(eng, stages):
                def body(j):
                    for i in range(TURN + max(lag for lag, _ in stages)):
                        for lag, stage in stages:
                            m = i - lag
                            if 0 <= m < TURN:
                                stage(TURN * j + m, m, j)
                body(0)
                with eng.Fori(1, EXPERTS // 2) as j:
                    body(j)

            @block.sync
            def _(sp):
                def step(n, m, j):
                    if m % STEPS_E == 0:
                        par = m // STEPS_E
                        e = 2 * j + par
                        if not isinstance(j, int):
                            sp.wait_ge(s_po, TURN * j - TURN + STEPS_E * (par + 1))
                            sp.wait_ge(s_ys, TURN * j - TURN + STEPS_E * (par + 1))
                        de = bass.ds(e, 1)
                        sp.dma_start(we1[:, par, :], W1[de].rearrange("a p f -> p (a f)")).then_inc(s_we[par], 16)
                        sp.dma_start(we2[:, par], W2[de].rearrange("a (c p) d -> p (a c) d", p=P)).then_inc(s_we[par], 16)
                        sp.dma_start(be1[:, par, :], b1[de].rearrange("a (c p) -> p (a c)", p=P)).then_inc(s_we[par], 16)
                        sp.dma_start(be2[:, par, :], b2[de].rearrange("a d -> (a d)").partition_broadcast(P)).then_inc(s_we[par], 16)
                    need(sp, s_pt, n, NB)
                    need(sp, s_dest, n, NB)
                    need(sp, s_gate, n, NB)
                    sp.dma_start(xg[:, m % 2], rows_v[bass.ds(n, 1)].rearrange("a p r c -> p (a r) c")).then_inc(s_xg[m % 2], 16)
                turns(sp, [(0, step)])

            def arrived(eng, m, j):
                eng.wait_ge(s_xg[m % 2], 16 * (STEPS_E * j + m // 2 + 1))

            def weights(eng, m, j):
                eng.wait_ge(s_we[m // STEPS_E], 64 * (j + 1))

            @block.tensor
            def _(pe):
                def turn(n, m, j):
                    arrived(pe, m, j)
                    need(pe, s_xgT, n, 2)
                    for i in range(G):
                        ins = pe.transpose(pT[m % 2][:, P * i:P * (i + 1)], xg[:, m % 2, i, 0:D], ident[:, :])
                    ins.then_inc(s_pt, 1)

                def up(n, m, j):
                    weights(pe, m, j)
                    need(pe, s_xgT, n)
                    for half_, (done, free) in enumerate(((s_ph0, s_h0), (s_ph1, s_h1))):
                        need(pe, free, n, 1)
                        for c in range(2):
                            f = 2 * half_ + c
                            ins = pe.matmul(pH[half_][:, ROWS * c:ROWS * (c + 1)], we1[:, m // STEPS_E, P * f:P * (f + 1)],
                                            xgT[:, m % 2, :], start=True, stop=True)
                        ins.then_inc(done, 1)

                def down(n, m, j):
                    need(pe, s_h0, n)
                    need(pe, s_h1, n)
                    need(pe, s_ys, n, 2)
                    for i in range(G):
                        for c in range(NF):
                            ins = pe.matmul(pO[m % 2][:, P * i:P * (i + 1)], hb[:, m % 2, c, P * i:P * (i + 1)],
                                            we2[:, m // STEPS_E, c, :], start=(c == 0), stop=(c == NF - 1))
                    ins.then_inc(s_po, 1)
                turns(pe, [(0, turn), (1, up), (2, down)])

            @block.scalar
            def _(a):
                def silus(n, m, j):
                    weights(a, m, j)
                    need(a, s_po, n, 2)
                    for half_, (src, done) in enumerate(((s_ph0, s_h0), (s_ph1, s_h1))):
                        need(a, src, n)
                        for c in range(2):
                            f = 2 * half_ + c
                            ins = a.activation(hb[:, m % 2, f, :], pH[half_][:, ROWS * c:ROWS * (c + 1)], ACT.Silu,
                                               bias=be1[:, m // STEPS_E, f:f + 1])
                        ins.then_inc(done, 1)
                turns(a, [(0, silus)])

            @block.vector
            def _(v):
                def fetched(n, m, j):
                    need(v, s_pt, n)
                    need(v, s_ph1, n, 2)
                    need(v, s_ph0, n, 2)
                    v.tensor_copy(xgT[:, m % 2, :], pT[m % 2][:, 0:ROWS]).then_inc(s_xgT, 1)

                def facts(n, m, j):
                    if m % STEPS_E == 0 and m:
                        need(v, s_i1, n, 1)
                        v.tensor_scalar(ecur[:, 1:2], ecur[:, 0:1], 1.0, None, ALU.add).then_inc(s_ef, 1)
                        v.wait_ge(s_ef, 2 * j + 1)
                    elif m == 0 and not isinstance(j, int):
                        need(v, s_i1, n, 1)
                        v.tensor_scalar(ecur[:, 0:1], ecur[:, 1:2], 1.0, None, ALU.add).then_inc(s_ef, 1)
                        v.wait_ge(s_ef, 2 * j)
                    arrived(v, m, j)
                    k, r = m % 2, xg[:, m % 2]
                    kk = (m % 4)
                    first, other, g1, g2 = (info[:, k, i] for i in range(4))
                    e = m // STEPS_E
                    v.tensor_scalar(first, r[:, :, D + 1], ecur[:, e:e + 1], None, ALU.is_equal).then_inc(s_i1, 1)
                    need(v, s_i1, n)
                    v.tensor_scalar(other, first, -1.0, 1.0, ALU.mult, ALU.add).then_inc(s_i2, 1)
                    v.tensor_tensor(g1, first, r[:, :, D + 2], ALU.mult).then_inc(s_i3, 1)
                    need(v, s_i2, n)
                    v.tensor_tensor(g2, other, r[:, :, D + 3], ALU.mult).then_inc(s_i4, 1)
                    scattered(v, m, j)
                    v.scalar_tensor_tensor(out=dest[:, kk, :], in0=other, scalar=float(TOKENS), in1=r[:, :, D], op0=ALU.mult,
                                           op1=ALU.add).then_inc(s_dest, 1)
                    need(v, s_i3, n)
                    need(v, s_i4, n)
                    v.tensor_tensor(gate[:, kk, :], g1, g2, ALU.add).then_inc(s_gate, 1)

                def scattered(eng, m, j):
                    before_ = [x for x in range(TURN) if x % 4 == m % 4 and x < m]
                    per = len([x for x in range(TURN) if x % 4 == m % 4])
                    count = (j * per + len(before_)) * 16 * G
                    if not isinstance(count, int) or count > 0:
                        eng.wait_ge(s_scat[m % 4], count)

                def results(n, m, j):
                    weights(v, m, j)
                    need(v, s_po, n)
                    need(v, s_yo, n, 2)
                    v.tensor_tensor(ysum[:, m % 2], pO[m % 2][:, 0:ROWS].rearrange("p (g d) -> p g d", g=G),
                                    be2[:, m // STEPS_E, :].unsqueeze(1).broadcast_to([P, G, D]), ALU.add).then_inc(s_ys, 1)
                    need(v, s_ys, n)
                    need(v, s_gate, n)
                    for i in range(G):
                        ins = v.tensor_scalar(yo[:, m % 4, i, :], ysum[:, m % 2, i, :], gate[:, m % 4, i:i + 1], None, ALU.mult)
                    ins.then_inc(s_yo, 1)
                v.memset(ecur[:, :], 0.0).then_inc(s_e, 1)
                v.wait_ge(s_e, 1)
                turns(v, [(2, results), (0, fetched), (0, facts)])

            @block.gpsimd
            def _(g):
                def leave(n, m, j):
                    need_apart(g, s_yo, n)
                    need_apart(g, s_dest, n)
                    for i in range(G):
                        g.indirect_dma_start(choice, bass.IndirectOffsetOnAxis(ap=dest[:, m % 4, i:i + 1], axis=0), yo[:, m % 4, i, :],
                                             None, bounds_check=2 * TOKENS - 1, oob_is_err=False).then_inc(s_scat[m % 4], 16)
                turns(g, [(0, leave)])
                for k in range(4):
                    per = len([x for x in range(TURN) if x % 4 == k])
                    g.wait_ge(s_scat[k], (EXPERTS // 2) * per * 16 * G)

        with ExitStack() as st:
            st.callback(stage_over)
            G = 4
            GROUPS = TILES // G

            def sbt(name, shape, dt=F32):
                return st.enter_context(nc.sbuf_tensor(name, shape, dt))
            ya = sbt("c_ya", [P, 2, G, D])
            yb = sbt("c_yb", [P, 2, G, D])
            ys = sbt("c_ys", [P, 2, G, D])
            yn = sbt("c_yn", [P, 2, G, D])
            ot = sbt("c_ot", [P, 2, G, D])
            stats = sbt("c_stats", [P, 2, G, 6])
            mv = sbt("c_mv", [P, 2, G, 2])
            ve = sbt("c_ve", [P, 2, G])
            rs = sbt("c_rs", [P, 2, G])
            s_in = [sem("c_in0"), sem("c_in1")]
            s_out = [sem("c_out0"), sem("c_out1")]
            s_ys, s_st, s_var, s_ve, s_rs, s_yn, s_ot = (sem("c_" + n) for n in ("ys", "st", "var", "ve", "rs", "yn", "ot"))
            first_v = choice[0:TOKENS].rearrange("(u v s p) d -> s u p v d", v=G, s=STEPS, p=P)
            other_v = choice[TOKENS:2 * TOKENS].rearrange("(u v s p) d -> s u p v d", v=G, s=STEPS, p=P)
            out_v = out.rearrange("(u v) (s p) d -> s u p v d", v=G, p=P)
            block = st.enter_context(nc.Block())

            def part(v_, g, k):
                return v_[bass.ds((g - k) // 2 if isinstance(g, int) else (g - k) >> 1, 1), k].rearrange("a p v d -> p (a v) d")

            @block.sync
            def _(sp):
                def load(g, k):
                    need(sp, s_ys, g, 2)
                    sp.dma_start(ya[:, k], part(first_v, g, k)).then_inc(s_in[k], 16)
                    sp.dma_start(yb[:, k], part(other_v, g, k)).then_inc(s_in[k], 16)
                skewed(sp, GROUPS, 2, 4, [(0, load)])

            @block.vector
            def _(v):
                def total(g, k):
                    v.wait_ge(s_in[k], 32 * (g // 2 + 1) if isinstance(g, int) else 32 * (g >> 1) + 32)
                    need(v, s_yn, g, 2)
                    v.tensor_tensor(ys[:, k], ya[:, k], yb[:, k], ALU.add).then_inc(s_ys, 1)
                    need(v, s_ys, g)
                    for i in range(G):
                        ins = v.bn_stats(stats[:, k, i, :], ys[:, k, i, :])
                    ins.then_inc(s_st, 1)
                    need_apart(v, s_st, g)
                    need_apart(v, s_ve, g, 2)
                    for i in range(G):
                        ins = v.bn_aggr(mv[:, k, i, :], stats[:, k, i, :])
                    ins.then_inc(s_var, 1)

                def finish(g, k):
                    need(v, s_rs, g)
                    need(v, s_ot, g, 2)
                    for i in range(G):
                        ins = v.tensor_scalar(yn[:, k, i, :], ys[:, k, i, :], mv[:, k, i, 0:1], rs[:, k, i:i + 1],
                                              ALU.subtract, ALU.mult)
                    ins.then_inc(s_yn, 1)
                skewed(v, GROUPS, 2, 6, [(0, total), (1, finish)])

            @block.gpsimd
            def _(g_):
                def root(g, k):
                    need_apart(g_, s_var, g)
                    g_.tensor_scalar(ve[:, k], mv[:, k, :, 1], EPS, None, ALU.add).then_inc(s_ve, 1)
                    need_apart(g_, s_ve, g)
                    need_apart(g_, s_yn, g, 2)
                    g_.tensor_tensor(rs[:, k], ve[:, k], half[:, 0:G], ALU.pow).then_inc(s_rs, 1)

                def add_x1(g, k):
                    need_apart(g_, s_yn, g)
                    count = 16 * (g // 2) if isinstance(g, int) else 16 * (g >> 1)
                    if not isinstance(g, int) or g >= 2:
                        g_.wait_ge(s_out[k], count)
                    g_.tensor_tensor(ot[:, k], yn[:, k], x1[:, bass.ds(G * g, G), :], ALU.add).then_inc(s_ot, 1)
                skewed(g_, GROUPS, 2, 6, [(0, root), (1, add_x1)])

            @block.scalar
            def _(a):
                def store(g, k):
                    need(a, s_ot, g)
                    a.dma_start(part(out_v, g, k), ot[:, k]).then_inc(s_out[k], 16)
                skewed(a, GROUPS, 2, 4, [(0, store)])
                for k in range(2):
                    a.wait_ge(s_out[k], 16 * GROUPS // 2)


_INS = ['L0_attn_x', 'L0_attn_ln_w', 'L0_attn_ln_b', 'L0_attn_in_proj_w', 'L0_attn_conv_w', 'L0_attn_conv_b',
        'L0_attn_dt_bias', 'L0_attn_A_log', 'L0_attn_D_skip', 'L0_attn_rms_w', 'L0_attn_out_proj_w', 'L0_attn_mlp_w1',
        'L0_attn_mlp_b1', 'L0_attn_mlp_w2', 'L0_attn_mlp_b2', 'L0_ffn_Wr', 'L0_ffn_br', 'L0_ffn_W1', 'L0_ffn_b1',
        'L0_ffn_W2', 'L0_ffn_b2']


def kernel(**inputs):
    import numpy as _np
    import concourse.bacc as _bacc
    from concourse import mybir as _mybir
    from concourse.bass_utils import run_bass_kernel_spmd as _run

    nc = _bacc.Bacc("TRN2", target_bir_lowering=False, num_devices=1)
    arrays, args = {}, []
    for name in _INS:
        a = _np.ascontiguousarray(inputs[name])
        arrays[f"in_{name}_dram"] = a
        args.append(nc.dram_tensor(f"in_{name}_dram", a.shape, _mybir.dt.from_np(a.dtype), kind="ExternalInput").ap())
    args.append(nc.dram_tensor("out_0_dram", (SEQS, LEN, D), F32, kind="ExternalOutput").ap())
    build(nc, *args)
    r = _run(nc, [arrays], core_ids=[0])
    return r.results[0]["out_0_dram"]
```

```python
from contextlib import ExitStack

import concourse.bass as bass
from concourse import mybir

F32 = mybir.dt.float32
BF16 = mybir.dt.bfloat16
I32 = mybir.dt.int32
U32 = mybir.dt.uint32
ALU = mybir.AluOpType
ACT = mybir.ActivationFunctionType
AX = mybir.AxisListType

P = 128
SEQS, LEN, D = 8, 1024, 128
STEPS = LEN // P
TILES = SEQS * STEPS
TOKENS = SEQS * LEN
HEADS, HD, INNER, STATE = 32, 8, 256, 128
TAPS = 4
HALO = TAPS - 1
XBLK = HALO + P
CONV = INNER + 2 * STATE
CHUNK = 64
FF = 512
NF = FF // P
EPS = 1e-5
EXPERTS = 8
CAP = -(-12 * TOKENS // (10 * EXPERTS))
ROWS = 256
ESTEPS = -(-CAP // ROWS)
REGION = ESTEPS * ROWS
TABLE = EXPERTS * REGION
FILLS = 2 * TOKENS // (8 * P) + TABLE // (5 * P)
ROWLEN = D + 4
FAR = 65536.0


def need(eng, sem, t, back=0):
    value = t + 1 - back
    if not isinstance(value, int) or value > 0:
        eng.wait_ge(sem, value)


carrier = [None]


def need_apart(eng, sem, t, back=0):
    need(eng, sem, t, back)
    if not isinstance(t, int):
        eng.sem_inc(carrier[0], 1)


def skewed(eng, steps, unroll, head, stages):
    def at(i, lo, which):
        for lag, stage in stages:
            t = i - lag
            if which is None:
                if 0 <= t < steps:
                    stage(t, t % unroll)
            else:
                stage(t, (which - lag) % unroll)
    for i in range(head):
        at(i, 0, None)
    with eng.Fori(head // unroll, steps // unroll) as j:
        for u in range(unroll):
            at(j * unroll + u, 0, u)
    for i in range(steps, steps + max(lag for lag, _ in stages)):
        at(i, 0, None)


def build(nc, x, ln_w, ln_b, in_proj_w, conv_w, conv_b, dt_bias, A_log, D_skip, rms_w, out_proj_w,
          mlp_w1, mlp_b1, mlp_w2, mlp_b2, Wr, br, W1, b1, W2, b2, out):
    table = nc.dram_tensor("expert_rows", (TABLE, ROWLEN), F32, kind="Internal").ap()
    choice = nc.dram_tensor("choice_rows", (2 * TOKENS, D), F32, kind="Internal").ap()
    with ExitStack() as ctx:
        ctx.enter_context(nc.allow_non_contiguous_dma(reason="columns of a few hundred biases, one element a partition"))

        def sb(name, shape, dt=F32):
            return ctx.enter_context(nc.sbuf_tensor(name, shape, dt))

        stage_sems = []
        carrier[0] = nc.alloc_semaphore(name="carrier")

        def sem(name):
            s = nc.alloc_semaphore(name=name)
            stage_sems.append(s)
            return s

        def stage_over():
            nc.clear_and_free_semaphores(list(stage_sems))
            stage_sems.clear()
            nc.all_engine_barrier()

        ident = sb("ident", [P, P])
        ones = sb("ones", [P, P])
        centre = sb("centre", [P, P])
        spans = sb("spans", [P, 3, P])
        causal = sb("causal", [P, P])
        eps = sb("eps", [P, 1])
        zrow = sb("zrow", [P, 8 * D])
        frow = sb("frow", [P, 5, ROWLEN])
        filled = nc.alloc_semaphore(name="filled")
        lnw = sb("lnw", [P, 1])
        lnb = sb("lnb", [P, 1])
        b1_col = sb("b1_col", [P, NF])
        brow = sb("brow", [P, EXPERTS])
        b2row = sb("b2row", [P, D])
        dskip = sb("dskip", [P, HEADS])
        w_in = sb("w_in", [P, CONV])
        tap_w = sb("tap_w", [P, 4, TAPS])
        tap_b = sb("tap_b", [P, 4])
        w_z = sb("w_z", [P, INNER])
        w_dt = sb("w_dt", [P, HEADS])
        w_out = sb("w_out", [P, 2, D])
        w_m1 = sb("w_m1", [P, FF])
        w_m2 = sb("w_m2", [P, NF, D])
        w_r = sb("w_r", [P, EXPERTS])
        mean = sb("mean", [P, TILES])
        rstd = sb("rstd", [P, TILES])
        ssq = sb("ssq", [P, TILES])
        logits = sb("logits", [P, TILES, EXPERTS])
        arena = sb("arena", [P, 72 * XBLK])
        xT = arena[:, :].rearrange("p (t c) -> p t c", c=XBLK)
        x1 = arena[:, 0:TILES * D].rearrange("p (t d) -> p t d", d=D)
        arena2 = sb("arena2", [P, TILES * ROWLEN])
        dec = arena2[:, 0:4 * TILES * HEADS].rearrange("p (f t h) -> p f t h", f=4, h=HEADS)
        pre, post, gapA, gapB = (dec[:, f] for f in range(4))
        rows = arena2[:, :].rearrange("p (t c) -> p t c", c=ROWLEN)
        arena3 = sb("arena3", [P, TILES * D])
        proj = arena3[:, :].rearrange("p (t d) -> p t d", d=D)
        tmp = arena3[:, :].rearrange("p (f t h) -> p f t h", f=4, h=HEADS)
        dt, da, tail, work = (tmp[:, f] for f in range(4))

        with ExitStack() as st:
            st.callback(stage_over)
            def sbt(name, shape, dt=F32):
                return st.enter_context(nc.sbuf_tensor(name, shape, dt))
            wo = sbt("wo", [P, 2, D])
            rmsw = sbt("rmsw", [P, 2])
            LOADS = 16
            loaded, fold, masks, zeroed = (sem(n) for n in ("loaded", "fold", "masks", "zeroed"))
            block = st.enter_context(nc.Block())

            @block.sync
            def _(sp):
                loads = [(w_in[:, :], in_proj_w[:, INNER:INNER + CONV]),
                         (tap_w[:, :, :], conv_w.rearrange("(m p) k -> p m k", p=P)),
                         (tap_b[:, :], conv_b.rearrange("(m p) -> p m", p=P)),
                         (wo[:, :, :], out_proj_w.rearrange("(c p) d -> p c d", p=P)),
                         (rmsw[:, :], rms_w.rearrange("(c p) -> p c", p=P)),
                         (lnw[:, :], ln_w.rearrange("(p a) -> p a", a=1)),
                         (lnb[:, :], ln_b.rearrange("(p a) -> p a", a=1)),
                         (b1_col[:, :], mlp_b1.rearrange("(c p) -> p c", p=P)),
                         (brow[:, :], br.partition_broadcast(P)),
                         (b2row[:, :], mlp_b2.partition_broadcast(P)),
                         (dskip[:, :], D_skip.partition_broadcast(P)),
                         (w_z[:, :], in_proj_w[:, 0:INNER]),
                         (w_dt[:, :], in_proj_w[:, INNER + CONV:INNER + CONV + HEADS]),
                         (w_m1[:, :], mlp_w1),
                         (w_m2[:, :, :], mlp_w2.rearrange("(c p) d -> p c d", p=P)),
                         (w_r[:, :], Wr)]
                assert len(loads) == LOADS
                for dst, src in loads:
                    sp.dma_start(dst, src).then_inc(loaded, 16)
                sp.wait_ge(zeroed, 1)
                zeros = choice.rearrange("(n p r) d -> n p (r d)", p=P, r=8)
                for n in range(2 * TOKENS // (8 * P)):
                    sp.dma_start(zeros[n], zrow[:, :]).then_inc(filled, 16)
                sp.wait_ge(zeroed, 3)
                empty = table.rearrange("(n p r) c -> n p (r c)", p=P, r=5)
                for n in range(TABLE // (5 * P)):
                    sp.dma_start(empty[n], frow[:, :, :].rearrange("p r c -> p (r c)")).then_inc(filled, 16)
                sp.wait_ge(loaded, 16 * len(loads))

            @block.gpsimd
            def _(g):
                g.memset(zrow[:, :], 0.0).then_inc(zeroed, 1)
                g.memset(frow[:, :, :], 0.0).then_inc(zeroed, 1)
                g.wait_ge(zeroed, 2)
                g.memset(frow[:, :, D:D + 1], FAR).then_inc(zeroed, 1)
                g.memset(eps[:, :], EPS)
                g.memset(ones[:, :], 1.0)
                g.memset(xT[:, 0:SEQS, 0:HALO], 0.0)
                g.memset(ident[:, :], 0.0)
                g.memset(spans[:, :, :], 1.0)
                for q in range(4):
                    g.memset(centre[:, 32 * q:32 * q + 32], 1.0 if q % 2 else -1.0)
                g.memset(causal[:, :], 1.0).then_inc(masks, 1)
                g.wait_ge(masks, 1)
                n = 1

                def keep(ap, base, step, chan, cmp=ALU.is_ge, fill=0.0):
                    nonlocal n
                    g.affine_select(out=ap, in_=ap, compare_op=cmp, fill=fill, base=base,
                                    pattern=[[step, ap.shape[-1]]], channel_multiplier=chan).then_inc(masks, 1)
                    n += 1
                    g.wait_ge(masks, n)
                keep(ident[:, :], 0, -1, 1, ALU.not_equal, 1.0)
                for c in range(P // CHUNK):
                    part = causal[:, CHUNK * c:CHUNK * (c + 1)]
                    keep(part, CHUNK * c, 1, -1)
                    keep(part, -CHUNK * c, 0, 1)
                for q in range(4):
                    part = centre[:, 32 * q:32 * q + 32]
                    if q % 2:
                        keep(part, 32 * q, 1, -1)
                        keep(part, -32 * q, 0, 1)
                    else:
                        keep(part, -32 * q - 1, -1, 1)
                        keep(part, 32 * q + 31, 0, -1)
                keep(spans[:, 0, :], 31, 0, -1)
                keep(spans[:, 1, :], -32, 0, 1)
                keep(spans[:, 1, :], 95, 0, -1)
                keep(spans[:, 2, :], -96, 0, 1)

            @block.vector
            def _(v):
                v.wait_ge(loaded, 16 * LOADS)
                for c in range(2):
                    v.tensor_scalar(w_out[:, c, :], wo[:, c, :], rmsw[:, c:c + 1], None, ALU.mult).then_inc(fold, 1)

        with ExitStack() as st:
            st.callback(stage_over)

            def sbt(name, shape, dt=F32):
                return st.enter_context(nc.sbuf_tensor(name, shape, dt))

            def pst(name, shape):
                return st.enter_context(nc.psum_tensor(name, shape, F32))
            xall = arena2[:, 0:TILES * D].rearrange("p (t d) -> p t d", d=D)
            stats = sbt("n_stats", [P, 2, SEQS, 6])
            mv = sbt("n_mv", [P, TILES, 2])
            mvs = sbt("n_mvs", [P, 2, SEQS, 2])
            var2, ln1, ln2, sq1, scale2 = (sbt("n_" + n, [P, TILES]) for n in ("var2", "ln1", "ln2", "sq1", "scale2"))
            hn = sbt("n_hn", [P, 2, SEQS, D])
            xs = sbt("n_xs", [P, 2, SEQS, P])
            dtb = sbt("n_dtb", [P, HEADS])
            pT = [pst(f"n_pT{k}", [P, SEQS, P]) for k in range(2)]
            pD = [pst(f"n_pD{k}", [P, 512]) for k in range(2)]
            (s_stat, s_var, s_l1, s_l2, s_q, s_v2, s_sum, s_root, s_hn, s_turn, s_xs, s_kept, s_halo, s_raw,
             s_rawr, s_dtb, s_r, s_agg) = (sem("n_" + n) for n in (
                 "stat", "var", "lone", "ltwo", "q", "vtwo", "sum", "root", "hn", "turned", "xs", "kept", "halo", "raw",
                 "rawr", "dtb", "r", "agg"))
            s_x = [sem("n_x0"), sem("n_x1")]
            x_v = x.rearrange("b (s p) d -> s p b d", p=P)
            block = st.enter_context(nc.Block())

            def group(g):
                return bass.ds(SEQS * g, SEQS)

            @block.sync
            def _(sp):
                sp.dma_start(dtb[:, :], dt_bias.partition_broadcast(P)).then_inc(s_dtb, 16)
                for k in range(2):
                    sp.dma_start(xall[:, group(k), :], x_v[k]).then_inc(s_x[k], 16)
                with sp.Fori(1, STEPS // 2) as j:
                    for k in range(2):
                        sp.wait_ge(s_x[k], 16 * j)
                        sp.dma_start(xall[:, group(2 * j + k), :],
                                     x_v[bass.ds(2 * j + k, 1)].rearrange("a p b d -> p (a b) d")).then_inc(s_x[k], 16)

            @block.vector
            def _(v):
                def tile(g, b):
                    return xall[:, bass.ds(SEQS * g + b, 1), :].rearrange("p a d -> p (a d)")

                def statistics(g, k):
                    n = g // 2 if isinstance(g, int) else (g - k) >> 1
                    v.wait_ge(s_x[k], 16 * (n + 1))
                    need(v, s_var, g, 2)
                    for b in range(SEQS):
                        i = v.bn_stats(stats[:, k, b, :], tile(g, b))
                    i.then_inc(s_stat, 1)

                def moments(g, k):
                    need_apart(v, s_stat, g)
                    for b in range(SEQS):
                        i = v.bn_aggr(mvs[:, k, b, :], stats[:, k, b, :])
                    i.then_inc(s_agg, 1)

                def keep_moments(g, k):
                    need(v, s_agg, g)
                    v.tensor_copy(mv[:, group(g), :], mvs[:, k]).then_inc(s_var, 1)

                def apply(g, k):
                    need(v, s_turn, g, 2)
                    for b in range(SEQS):
                        t = bass.ds(SEQS * g + b, 1)
                        i = v.tensor_scalar(hn[:, k, b, :], tile(g, b), mean[:, t], scale2[:, t], ALU.subtract, ALU.mult)
                    i.then_inc(s_hn, 1)

                def raw_dt(g, k):
                    need(v, s_raw, g)
                    v.tensor_tensor(dt[:, group(g), :], pD[k][:, 0:SEQS * HEADS].rearrange("p (b h) -> p b h", h=HEADS),
                                    dtb[:, :].unsqueeze(1).broadcast_to([P, SEQS, HEADS]), ALU.add).then_inc(s_rawr, 1)
                v.wait_ge(s_dtb, 16)
                skewed(v, STEPS, 2, 4, [(2, keep_moments), (1, moments), (0, statistics)])
                v.wait_ge(s_var, STEPS)
                v.tensor_copy(mean[:, :], mv[:, :, 0]).then_inc(s_r, 1)
                v.wait_ge(s_q, 1)
                v.tensor_tensor(var2[:, :], sq1[:, :], mv[:, :, 1], ALU.mult).then_inc(s_v2, 1)
                v.wait_ge(s_l2, 1)
                v.tensor_tensor(ln2[:, :], ln2[:, :], ln1[:, :], ALU.add).then_inc(s_sum, 1)
                v.wait_ge(s_root, 2)
                v.wait_ge(s_r, 1)
                skewed(v, STEPS, 2, 4, [(0, apply), (3, raw_dt)])

            @block.gpsimd
            def _(g_):
                def store(g, k):
                    need_apart(g_, s_xs, g)
                    g_.tensor_copy(xT[:, group(g), HALO:XBLK], xs[:, k]).then_inc(s_kept, 1)
                    g_.tensor_copy(xT[:, bass.ds(SEQS * g + SEQS, SEQS), 0:HALO], xs[:, k, :, P - HALO:P]).then_inc(s_halo, 1)
                skewed(g_, STEPS, 2, 4, [(0, store)])

            @block.tensor
            def _(pe):
                def turn(g, k):
                    need(pe, s_hn, g)
                    need(pe, s_xs, g, 2)
                    for b in range(SEQS):
                        i = pe.transpose(pT[k][:, b, :], hn[:, k, b, :], ident[:, :])
                    i.then_inc(s_turn, 1)

                def dts(g, k):
                    need(pe, s_xs, g)
                    need(pe, s_rawr, g, 2)
                    for b in range(SEQS):
                        i = pe.matmul(pD[k][:, HEADS * b:HEADS * (b + 1)], xs[:, k, b, :], w_dt[:, :],
                                      start=True, stop=True)
                    i.then_inc(s_raw, 1)
                skewed(pe, STEPS, 2, 4, [(0, turn), (1, dts)])

            @block.scalar
            def _(a):
                a.wait_ge(s_var, STEPS)
                a.activation(ln1[:, :], mv[:, :, 1], ACT.Ln, bias=eps[:, 0:1]).then_inc(s_l1, 1)
                a.wait_ge(s_l1, 1)
                a.activation(sq1[:, :], ln1[:, :], ACT.Exp, scale=-1.0).then_inc(s_q, 1)
                a.activation(rstd[:, :], ln1[:, :], ACT.Exp, scale=-0.5).then_inc(s_root, 1)
                a.wait_ge(s_v2, 1)
                a.activation(ln2[:, :], var2[:, :], ACT.Ln, bias=eps[:, 0:1]).then_inc(s_l2, 1)
                a.wait_ge(s_sum, 1)
                a.activation(scale2[:, :], ln2[:, :], ACT.Exp, scale=-0.5).then_inc(s_root, 1)

                def affine(g, k):
                    need(a, s_turn, g)
                    need(a, s_halo, g, 2)
                    need(a, s_kept, g, 2)
                    need(a, s_raw, g, 2)
                    for h in range(2):
                        i = a.activation(xs[:, k, 4 * h:4 * h + 4, :], pT[k][:, 4 * h:4 * h + 4, :], ACT.Identity,
                                         bias=lnb[:, 0:1], scale=lnw[:, 0:1])
                    i.then_inc(s_xs, 1)
                skewed(a, STEPS, 2, 4, [(0, affine)])

        with ExitStack() as st:
            st.callback(stage_over)
            def pst(name, shape):
                return st.enter_context(nc.psum_tensor(name, shape, F32))
            alog = st.enter_context(nc.sbuf_tensor("d_alog", [P, HEADS], F32))
            aneg = st.enter_context(nc.sbuf_tensor("d_aneg", [P, HEADS], F32))
            pc = [pst(f"d_pc{q}", [P, 512]) for q in range(4)]
            pg = [pst(f"d_pg{q}", [P, 512]) for q in range(4)]
            s_al, s_abs, s_exp, s_ln, s_a, s_neg, s_dt, s_da, s_pc, s_pg, s_post, s_pre, s_gap, s_fin = (
                sem("d_" + n) for n in ("al", "abs", "exp", "ln", "a", "neg", "dt", "da", "pc", "pg", "post",
                                        "pre", "gap", "fin"))
            QT = TILES // 4
            block = st.enter_context(nc.Block())

            def quarter(f, q):
                return f[:, QT * q:QT * (q + 1), :]

            def flat(f, q):
                return quarter(f, q).rearrange("p t h -> p (t h)")

            @block.sync
            def _(sp):
                sp.dma_start(alog[:, :], A_log.partition_broadcast(P)).then_inc(s_al, 16)

            @block.scalar
            def _(a):
                for q in range(4):
                    a.activation(flat(work, q), flat(dt, q), ACT.Abs).then_inc(s_abs, 1)
                a.wait_ge(s_al, 16)
                a.activation(aneg[:, :], alog[:, :], ACT.Exp).then_inc(s_a, 1)
                for q in range(4):
                    a.wait_ge(s_abs, q + 1)
                    a.activation(flat(work, q), flat(work, q), ACT.Exp, scale=-1.0).then_inc(s_exp, 1)
                for q in range(4):
                    a.wait_ge(s_exp, q + 1)
                    a.activation(flat(work, q), flat(work, q), ACT.Ln, bias=1.0).then_inc(s_ln, 1)
                for q in range(4):
                    a.wait_ge(s_pc, q + 1)
                    a.activation(flat(post, q), pc[q][:, :], ACT.Exp).then_inc(s_post, 1)
                    a.activation(flat(pre, q), pc[q][:, :], ACT.Exp, scale=-1.0).then_inc(s_pre, 1)
                for f, dst in enumerate((gapA, gapB, tail)):
                    for q in range(4):
                        a.wait_ge(s_pg, 4 * f + q + 1)
                        a.activation(flat(dst, q), pg[q][:, :], ACT.Exp).then_inc(s_gap, 1)

            @block.vector
            def _(v):
                v.wait_ge(s_a, 1)
                v.tensor_scalar(alog[:, :], aneg[:, :], -1.0, None, ALU.mult).then_inc(s_neg, 1)
                for q in range(4):
                    v.wait_ge(s_ln, q + 1)
                    v.scalar_tensor_tensor(out=flat(dt, q), in0=flat(dt, q), scalar=0.0, in1=flat(work, q),
                                           op0=ALU.max, op1=ALU.add).then_inc(s_dt, 1)
                v.wait_ge(s_neg, 1)
                for q in range(4):
                    v.wait_ge(s_dt, q + 1)
                    v.tensor_tensor(quarter(da, q), quarter(dt, q), alog[:, :].unsqueeze(1).broadcast_to([P, QT, HEADS]),
                                    ALU.mult).then_inc(s_da, 1)
                for q in range(4):
                    v.wait_ge(s_pre, q + 1)
                    v.tensor_tensor(flat(pre, q), flat(pre, q), flat(dt, q), ALU.mult).then_inc(s_fin, 1)
                v.wait_ge(s_gap, 12)
                v.tensor_tensor(gapA[:, SEQS:TILES, :], gapA[:, SEQS:TILES, :], tail[:, 0:TILES - SEQS, :],
                                ALU.mult).then_inc(s_fin, 1)

            @block.tensor
            def _(pe):
                for q in range(4):
                    pe.wait_ge(s_da, q + 1)
                    pe.matmul(pc[q][:, :], centre[:, :], flat(da, q), start=True, stop=True).then_inc(s_pc, 1)
                for f in range(3):
                    for q in range(4):
                        if f:
                            pe.wait_ge(s_gap, 4 * f + q - 3)
                        pe.matmul(pg[q][:, :], spans[:, f, :], flat(da, q), start=True, stop=True).then_inc(s_pg, 1)

        with ExitStack() as st:
            st.callback(stage_over)
            NB = 4

            def sbt(name, shape, dt=F32):
                return st.enter_context(nc.sbuf_tensor(name, shape, dt))

            def pst(name, shape=[P, 512]):
                return st.enter_context(nc.psum_tensor(name, shape, F32))
            cv = sbt("s_cv", [P, NB, 4, P])
            xs = sbt("s_xs", [P, NB, P])
            xt = sbt("s_xt", [P, NB, INNER])
            zs = sbt("s_zs", [P, NB, INNER])
            bs = sbt("s_bs", [P, NB, P])
            cs = sbt("s_cs", [P, NB, 3 * P])
            bt = sbt("s_bt", [P, NB, 2, P])
            gm = sbt("s_gm", [P, NB, P])
            xa = sbt("s_xa", [P, NB, INNER])
            dx = sbt("s_dx", [P, NB, INNER])
            state = sbt("s_state", [P, SEQS, INNER])
            sa = sbt("s_sa", [P, NB, INNER])
            ua = sbt("s_ua", [P, 2, INNER])
            sB = sbt("s_sb", [P, NB, INNER])
            y1 = sbt("s_y1", [P, NB, INNER])
            y2 = sbt("s_y2", [P, 2, INNER])
            yg = sbt("s_yg", [P, NB, INNER])
            sq = sbt("s_sq", [P, INNER])
            yt = sbt("s_yt", [P, NB, 2, P])
            pU = [pst("s_pU0"), pst("s_pU1")]
            pZ, pTr, pG, pS, pY, pO = (pst("s_" + n) for n in ("pZ", "pTr", "pG", "pS", "pY", "pO"))
            (s_z0, s_xs, s_pz, s_zs, s_ptr, s_xt, s_bs, s_cs, s_pg, s_gm, s_bt, s_xa, s_dx, s_ps, s_sa, s_ua, s_sb,
             s_st, s_py, s_y1, s_y2, s_yg, s_sq, s_pyt, s_yt, s_po, s_o) = (sem("s_" + n) for n in (
                 "zero", "xs", "pz", "zs", "ptr", "xt", "bs", "cs", "pg", "gm", "bt", "xa", "dx", "ps", "sa",
                 "ua", "sb", "st", "py", "y1", "y2", "yg", "sq", "pyt", "yt", "po", "o"))
            s_u, s_tap0, s_tap1, s_tap2, s_tap3 = ([sem(f"s_{n}{m}") for m in range(2)] for n in ("u", "ta", "tb", "tc", "td"))
            s_tap = [s_tap0, s_tap1, s_tap2, s_tap3]
            block = st.enter_context(nc.Block())
            HEAD = 16

            def heads(ap):
                return ap.rearrange("p (h c) -> p h c", c=HD)

            def spread(f, t):
                return f[:, bass.ds(t, 1), :].rearrange("p a h -> p (a h)").unsqueeze(2).broadcast_to([P, HEADS, HD])

            def c_pair(k):
                return cs[:, k, :].rearrange("p (a c) -> p a c", c=P + CHUNK)[:, :, 0:CHUNK]

            def columns(b):
                return pU[b][:, 0:2 * XBLK].rearrange("p (m c) -> p m c", c=XBLK)

            @block.gpsimd
            def _(g):
                def gated(t, k):
                    need_apart(g, s_y1, t)
                    need_apart(g, s_dx, t)
                    g.tensor_tensor(y2[:, k % 2, :], y1[:, k, :], dx[:, k, :], ALU.add).then_inc(s_y2, 1)
                    need_apart(g, s_y2, t)
                    need_apart(g, s_zs, t)
                    need_apart(g, s_sq, t, NB)
                    need_apart(g, s_pyt, t, NB)
                    g.tensor_tensor(yg[:, k, :], y2[:, k % 2, :], zs[:, k, :], ALU.mult).then_inc(s_yg, 1)

                def scale(t, k):
                    need_apart(g, s_xt, t)
                    need_apart(g, s_py, t, NB)
                    g.tensor_tensor(heads(xa[:, k, :]), heads(xt[:, k, :]), spread(pre, t), ALU.mult).then_inc(s_xa, 1)
                    need_apart(g, s_y2, t, NB)
                    g.tensor_tensor(heads(dx[:, k, :]), heads(xt[:, k, :]),
                                    dskip[:, :].unsqueeze(2).broadcast_to([P, HEADS, HD]), ALU.mult).then_inc(s_dx, 1)

                def fetch(t, k):
                    need_apart(g, s_pz, t, NB)
                    g.tensor_copy(xs[:, k, :], xT[:, bass.ds(t, 1), HALO:XBLK].rearrange("p a c -> p (a c)")).then_inc(s_xs, 1)
                skewed(g, TILES, NB, HEAD, [(7, gated), (3, scale), (4, fetch)])

            @block.tensor
            def _(pe):
                def project(t, k):
                    tile = xT[:, bass.ds(t, 1), :].rearrange("p a c -> p (a c)")
                    for b in range(2):
                        need(pe, s_tap[3][b], t, 1)
                        for m in range(2):
                            c0 = P * (2 * b + m)
                            i = pe.matmul(pU[b][:, XBLK * m:XBLK * (m + 1)], w_in[:, c0:c0 + P], tile, start=True, stop=True)
                        i.then_inc(s_u[b], 1)

                def project_z(t, k):
                    need(pe, s_xs, t)
                    need(pe, s_zs, t, 1)
                    pe.matmul(pZ[:, 0:INNER], xs[:, k, :], w_z[:, :], start=True, stop=True).then_inc(s_pz, 1)

                def turn_in(t, k):
                    need(pe, s_xt, t, 1)
                    need(pe, s_bt, t, 1)
                    need(pe, s_tap[3][0], t)
                    for m in range(2):
                        pe.transpose(pTr[:, P * m:P * (m + 1)], cv[:, k, m, :], ident[:, :])
                    need(pe, s_tap[3][1], t)
                    pe.transpose(pTr[:, 2 * P:3 * P], cv[:, k, 2, :], ident[:, :]).then_inc(s_ptr, 1)

                def gram(t, k):
                    need(pe, s_bs, t)
                    need(pe, s_cs, t)
                    need(pe, s_gm, t, 1)
                    pe.matmul(pG[:, 0:P].rearrange("p (a c) -> p a c", a=2), bs[:, k, :], c_pair(k),
                              start=True, stop=True).then_inc(s_pg, 1)

                def states(t, k):
                    need(pe, s_bt, t)
                    need(pe, s_xa, t)
                    need(pe, s_st, t, 1)
                    for c in range(2):
                        i = pe.matmul(pS[:, INNER * c:INNER * (c + 1)], bt[:, k, c, :], xa[:, k, :], start=True, stop=True)
                    i.then_inc(s_ps, 1)

                def outputs(t, k):
                    need(pe, s_gm, t)
                    need(pe, s_y1, t, 1)
                    pe.matmul(pY[:, 0:INNER], gm[:, k, :], xa[:, k, :], start=True, stop=False)
                    need(pe, s_sa, t)
                    pe.matmul(pY[:, 0:INNER], cs[:, k, 0:P], sa[:, k, :], start=False, stop=False)
                    need(pe, s_sb, t)
                    pe.matmul(pY[:, 0:INNER], cs[:, k, P:2 * P], sB[:, k, :], start=False, stop=True).then_inc(s_py, 1)

                def turn_out(t, k):
                    need(pe, s_yg, t)
                    need(pe, s_o, t, 1)
                    for c in range(2):
                        i = pe.transpose(pO[:, P * c:P * (c + 1)], yg[:, k, P * c:P * (c + 1)], ident[:, :])
                    i.then_inc(s_pyt, 1)

                def out_project(t, k):
                    need(pe, s_yt, t)
                    for c in range(2):
                        i = pe.matmul(pO[:, 2 * P:3 * P], yt[:, k, c, :], w_out[:, c, :], start=(c == 0), stop=(c == 1))
                    i.then_inc(s_po, 1)
                skewed(pe, TILES, NB, HEAD, [(0, project), (9, out_project), (6, outputs), (4, states), (2, turn_in),
                                             (3, gram), (5, project_z), (8, turn_out)])

            @block.scalar
            def _(a):
                def first_tap(t, k):
                    need(a, s_ptr, t, NB)
                    need(a, s_bs, t, NB)
                    need(a, s_cs, t, NB)
                    for b in range(2):
                        need(a, s_u[b], t)
                        for m in range(2 * b, 2 * b + 2):
                            i = a.activation(cv[:, k, m, :], columns(b)[:, m - 2 * b, 0:P], ACT.Identity,
                                             bias=tap_b[:, m:m + 1], scale=tap_w[:, m, 0:1])
                        i.then_inc(s_tap[0][b], 1)

                def silu_bc(t, k):
                    need(a, s_tap[3][1], t)
                    need(a, s_pg, t, NB)
                    a.activation(bs[:, k, :], cv[:, k, 2, :], ACT.Silu).then_inc(s_bs, 1)
                    need(a, s_py, t, NB)
                    a.activation(c_pair(k), cv[:, k, 3, :].rearrange("p (a c) -> p a c", a=2), ACT.Silu).then_inc(s_cs, 1)

                def silu_turned(t, k):
                    need(a, s_ptr, t)
                    need(a, s_xa, t, NB)
                    need(a, s_dx, t, NB)
                    a.activation(xt[:, k, :], pTr[:, 0:INNER], ACT.Silu).then_inc(s_xt, 1)
                    need(a, s_ps, t, NB)
                    for c in range(2):
                        r = slice(CHUNK * c, CHUNK * (c + 1))
                        i = a.activation(bt[r, k, c, :], pTr[r, INNER:INNER + P], ACT.Silu)
                    i.then_inc(s_bt, 1)

                def silu_z(t, k):
                    need(a, s_pz, t)
                    need(a, s_yg, t, NB)
                    a.activation(zs[:, k, :], pZ[:, 0:INNER], ACT.Silu).then_inc(s_zs, 1)

                def squares(t, k):
                    need(a, s_pyt, t)
                    need(a, s_po, t, NB)
                    a.activation(yt[:, k].rearrange("p c n -> p (c n)"), pO[:, 0:2 * P], ACT.Copy).then_inc(s_yt, 1)
                    need(a, s_sq, t, 1)
                    a.activation(sq[:, :], yg[:, k, :], ACT.Square, accum_out=ssq[:, bass.ds(t, 1)]).then_inc(s_sq, 1)

                def projected(t, k):
                    need(a, s_po, t)
                    a.activation(proj[:, bass.ds(t, 1), :].rearrange("p a d -> p (a d)"), pO[:, 2 * P:3 * P],
                                 ACT.Copy).then_inc(s_o, 1)
                a.wait_ge(s_z0, 3)
                skewed(a, TILES, NB, HEAD, [(0, first_tap), (9, projected), (3, silu_turned), (2, silu_bc), (6, silu_z),
                                            (8, squares)])

            @block.vector
            def _(v):
                def taps(b):
                    def stage(t, k):
                        for tap in range(1, TAPS):
                            need(v, s_tap[tap - 1][b], t)
                            for m in range(2 * b, 2 * b + 2):
                                i = v.scalar_tensor_tensor(out=cv[:, k, m, :], in0=columns(b)[:, m - 2 * b, tap:tap + P],
                                                           scalar=tap_w[:, m, tap:tap + 1], in1=cv[:, k, m, :],
                                                           op0=ALU.mult, op1=ALU.add)
                            i.then_inc(s_tap[tap][b], 1)
                    return stage

                def mask(t, k):
                    need(v, s_pg, t)
                    need(v, s_py, t, NB)
                    v.tensor_tensor(gm[:, k, :], pG[:, 0:P], causal[:, :], ALU.mult).then_inc(s_gm, 1)

                def mine(t):
                    q = t % SEQS if isinstance(t, int) else t & (SEQS - 1)
                    return state[:, bass.ds(q, 1), :].rearrange("p a c -> p (a c)")

                def carry_a(t, k):
                    need(v, s_py, t, NB)
                    need(v, s_st, t, 1)
                    v.tensor_tensor(heads(sa[:, k, :]), heads(mine(t)), spread(gapA, t), ALU.mult).then_inc(s_sa, 1)

                def add_a(t, k):
                    need(v, s_ps, t)
                    need(v, s_sa, t)
                    need(v, s_sb, t, 2)
                    v.tensor_tensor(ua[:, k % 2, :], sa[:, k, :], pS[:, 0:INNER], ALU.add).then_inc(s_ua, 1)

                def carry_b(t, k):
                    need(v, s_ua, t)
                    v.tensor_tensor(heads(sB[:, k, :]), heads(ua[:, k % 2, :]), spread(gapB, t), ALU.mult).then_inc(s_sb, 1)

                def add_b(t, k):
                    need(v, s_sb, t)
                    v.tensor_tensor(mine(t), sB[:, k, :], pS[:, INNER:2 * INNER], ALU.add).then_inc(s_st, 1)

                def scaled(t, k):
                    need(v, s_py, t)
                    need(v, s_y2, t, NB)
                    v.tensor_tensor(heads(y1[:, k, :]), heads(pY[:, 0:INNER]), spread(post, t), ALU.mult).then_inc(s_y1, 1)
                v.memset(cs[:, :, :], 0.0).then_inc(s_z0, 1)
                v.memset(bt[:, :, :, :], 0.0).then_inc(s_z0, 1)
                v.memset(state[:, :, :], 0.0).then_inc(s_z0, 1)
                v.wait_ge(s_z0, 3)
                skewed(v, TILES, NB, HEAD, [(1, taps(0)), (5, carry_a), (1, taps(1)), (5, add_a), (4, mask), (5, carry_b),
                                            (7, scaled), (5, add_b)])

        with ExitStack() as st:
            st.callback(stage_over)
            NB, G = 4, 2
            GROUPS, N = TILES // G, G * P

            def sbt(name, shape, dt=F32):
                return st.enter_context(nc.sbuf_tensor(name, shape, dt))

            def pst(name, shape=[P, 512]):
                return st.enter_context(nc.psum_tensor(name, shape, F32))
            root_y, ln_y, minus_m, mr = (sbt("m_" + n, [P, TILES]) for n in ("rooty", "lny", "mm", "mr"))
            res = sbt("m_res", [P, NB, G, D])
            h0 = sbt("m_h0", [P, NB, G, D])
            h0b = sbt("m_h0b", [P, 8, G, D])
            stats = sbt("m_stats", [P, 3, NB, G, 6])
            mv = sbt("m_mv", [P, 3, NB, G, 2])
            lv = sbt("m_lv", [P, 3, NB, G])
            rs = sbt("m_rs", [P, 3, NB, G])
            hn = sbt("m_hn", [P, NB, G, D])
            hT = sbt("m_hT", [P, NB, N])
            h1 = sbt("m_h1", [P, NB, NF, N])
            at = sbt("m_at", [P, NB, G, D])
            un = sbt("m_un", [P, NB, G, D])
            xl = sbt("m_xl", [P, NB, G, D])
            xlT = sbt("m_xlT", [P, NB, N])
            pT, pX, pM0, pM1, pL = (pst("m_" + n) for n in ("pT", "pX", "pM0", "pM1", "pL"))
            pM = [pM0, pM1]
            pH = [pst("m_pH0", [P, 512]), pst("m_pH1", [P, 512])]
            s_x = [sem(f"m_x{k}") for k in range(2)]
            (s_r, s_res, s_h0, s_h0b, s_pT, s_hT, s_ph, s_h1a, s_h1b, s_pm, s_at, s_un, s_x1, s_xl, s_keep, s_px, s_xlT, s_pl,
             s_lg, s_hn, s_extra) = (sem("m_" + n) for n in (
                 "r", "res", "h0", "h0b", "pT", "hT", "ph", "h1a", "h1b", "pm", "at", "un", "xone", "xl", "keep", "px",
                 "xlT", "pl", "lg", "hn", "extra"))
            s_ph2 = sem("m_ph2")
            s_extra2 = sem("m_extra2")
            s_st = [sem(f"m_st{i}") for i in range(3)]
            s_var = [sem(f"m_var{i}") for i in range(3)]
            s_ln = [sem(f"m_ln{i}") for i in range(3)]
            s_rs = [sem(f"m_rs{i}") for i in range(3)]
            x_v = x.rearrange("b (s p) d -> s p b d", p=P)
            block = st.enter_context(nc.Block())

            def skewed8(eng, stages):
                skewed(eng, GROUPS, 8, 16, stages)

            @block.sync
            def _(sp):
                for k in range(2):
                    sp.dma_start(rows[:, bass.ds(SEQS * k, SEQS), 0:D], x_v[k]).then_inc(s_x[k], 16)
                with sp.Fori(1, STEPS // 2) as j:
                    for k in range(2):
                        sp.wait_ge(s_x[k], 16 * j)
                        sp.dma_start(rows[:, bass.ds(2 * SEQS * j + SEQS * k, SEQS), 0:D],
                                     x_v[bass.ds(2 * j + k, 1)].rearrange("a p b d -> p (a b) d")).then_inc(s_x[k], 16)

            def tiles(ap, g):
                return ap[:, bass.ds(G * g, G), :]


            @block.gpsimd
            def _(g_):
                def residual_bias(g, m):
                    need_apart(g_, s_h0, g)
                    need_apart(g_, s_at, g, 8)
                    g_.tensor_tensor(h0b[:, m], h0[:, m % NB], b2row[:, :].unsqueeze(1).broadcast_to([P, G, D]), ALU.add).then_inc(s_h0b, 1)

                def add_x(g, m):
                    need_apart(g_, s_un, g)
                    g_.tensor_tensor(tiles(x1, g), rows[:, bass.ds(G * g, G), 0:D], un[:, m % NB], ALU.add).then_inc(s_x1, 1)

                def keep(g, m):
                    need_apart(g_, s_xl, g)
                    g_.tensor_copy(rows[:, bass.ds(G * g, G), 0:D], xl[:, m % NB]).then_inc(s_keep, 1)
                g_.tensor_tensor(mr[:, :], mean[:, :], rstd[:, :], ALU.mult).then_inc(s_extra, 1)
                g_.wait_ge(s_extra, 1)
                g_.tensor_scalar(minus_m[:, :], mr[:, :], -1.0, None, ALU.mult).then_inc(s_r, 1)
                skewed8(g_, [(0, residual_bias), (8, add_x), (11, keep)])

            @block.scalar
            def _(a):
                def root(n):
                    def stage(g, m):
                        k = m % NB
                        need(a, s_var[n], g)
                        a.activation(lv[:, n, k], mv[:, n, k, :, 1], ACT.Ln, bias=eps[:, 0:1]).then_inc(s_ln[n], 1)
                    return stage

                def root_end(n):
                    def stage(g, m):
                        k = m % NB
                        need(a, s_ln[n], g)
                        a.activation(rs[:, n, k], lv[:, n, k], ACT.Exp, scale=-0.5).then_inc(s_rs[n], 1)
                    return stage

                def centre_x(g, m):
                    a.wait_ge(s_x[m // 4], 16 * (g // 8 + 1) if isinstance(g, int) else 16 * ((g - m) >> 3) + 16)
                    need(a, s_h0, g, NB)
                    for i in range(G):
                        t = bass.ds(G * g + i, 1)
                        ins = a.activation(res[:, m % NB, i, :], rows[:, t, 0:D].rearrange("p a d -> p (a d)"), ACT.Identity, bias=minus_m[:, t], scale=rstd[:, t])
                    ins.then_inc(s_res, 1)

                def turned(g, m):
                    need(a, s_pT, g)
                    need(a, s_ph, g, NB)
                    a.activation(hT[:, m % NB, :], pT[:, 0:N], ACT.Identity, bias=lnb[:, 0:1], scale=lnw[:, 0:1]).then_inc(s_hT, 1)

                def relus(g, m):
                    need(a, s_pm, g, NB)
                    need(a, s_ph, g)
                    for c in range(NF // 2):
                        ins = a.activation(h1[:, m % NB, c, :], pH[0][:, N * c:N * (c + 1)], ACT.Relu, bias=b1_col[:, c:c + 1])
                    ins.then_inc(s_h1a, 1)

                def turned_xl(g, m):
                    need(a, s_px, g)
                    need(a, s_pl, g, NB)
                    a.activation(xlT[:, m % NB, :], pX[:, 0:N], ACT.Copy).then_inc(s_xlT, 1)
                a.activation(ln_y[:, :], ssq[:, :], ACT.Ln, bias=eps[:, 0:1], scale=1.0 / INNER).then_inc(s_extra2, 1)
                a.wait_ge(s_extra2, 1)
                a.activation(root_y[:, :], ln_y[:, :], ACT.Exp, scale=-0.5).then_inc(s_r, 1)
                a.wait_ge(s_r, 2)
                skewed8(a, [(4, relus), (3, turned), (1, root(0)), (7, root(1)), (10, root(2)), (1, root_end(0)), (7, root_end(1)),
                            (10, root_end(2)), (12, turned_xl), (0, centre_x)])

            @block.vector
            def _(v):
                def x1_of(g):
                    return lambda i: x1[:, bass.ds(G * g + i, 1), :].rearrange("p a d -> p (a d)")

                def statistics(n, of):
                    def stage(g, m):
                        need(v, s_rs[n], g, NB)
                        need(v, (s_h0, s_at, s_x1)[n], g)
                        for i in range(G):
                            ins = v.bn_stats(stats[:, n, m % NB, i, :], of(g, m % NB)(i))
                        ins.then_inc(s_st[n], 1)
                    return stage

                def moments(n):
                    def stage(g, m):
                        need_apart(v, s_st[n], g)
                        for i in range(G):
                            ins = v.bn_aggr(mv[:, n, m % NB, i, :], stats[:, n, m % NB, i, :])
                        ins.then_inc(s_var[n], 1)
                    return stage

                def normed(n, dst, src, k, done):
                    for i in range(G):
                        ins = v.tensor_scalar(dst[:, k, i, :], src(i), mv[:, n, k, i, 0:1], rs[:, n, k, i:i + 1],
                                              ALU.subtract, ALU.mult)
                    ins.then_inc(done, 1)

                def of_h0(g, k):
                    return lambda i: h0[:, k, i, :]

                def of_at(g, k):
                    return lambda i: at[:, k, i, :]

                def of_x1(g, k):
                    return x1_of(g)

                def residual(g, m):
                    k = m % NB
                    need(v, s_res, g)
                    need(v, s_h0b, g, NB)
                    need(v, s_hn, g, NB)
                    for i in range(G):
                        t = bass.ds(G * g + i, 1)
                        ins = v.scalar_tensor_tensor(out=h0[:, k, i, :], in0=proj[:, t, :].rearrange("p a d -> p (a d)"),
                                                     scalar=root_y[:, t], in1=res[:, k, i, :], op0=ALU.mult, op1=ALU.add)
                    ins.then_inc(s_h0, 1)

                def apply0(g, m):
                    need(v, s_rs[0], g)
                    need(v, s_pT, g, NB)
                    normed(0, hn, of_h0(g, m % NB), m % NB, s_hn)

                def relus(g, m):
                    need(v, s_pm, g, NB)
                    need(v, s_ph2, g)
                    for c in range(NF // 2, NF):
                        c2 = c - NF // 2
                        ins = v.tensor_scalar(h1[:, m % NB, c, :], pH[1][:, N * c2:N * (c2 + 1)], b1_col[:, c:c + 1], 0.0, ALU.add, ALU.max)
                    ins.then_inc(s_h1b, 1)

                def mlp_out(g, m):
                    need(v, s_pm, g)
                    need(v, s_h0b, g)
                    need(v, s_un, g, NB)
                    v.tensor_tensor(at[:, m % NB].rearrange("p a d -> p (a d)"), pM[m % 2][:, 0:N], h0b[:, m].rearrange("p a d -> p (a d)"), ALU.add).then_inc(s_at, 1)

                def apply1(g, m):
                    need(v, s_rs[1], g)
                    need(v, s_x1, g, NB)
                    normed(1, un, of_at(g, m % NB), m % NB, s_un)

                def apply2(g, m):
                    need(v, s_rs[2], g)
                    need(v, s_px, g, NB)
                    need(v, s_keep, g, NB)
                    normed(2, xl, x1_of(g), m % NB, s_xl)

                def logit(g, m):
                    need(v, s_pl, g)
                    v.tensor_tensor(tiles(logits, g), pL[:, 0:G * EXPERTS].rearrange("p (a e) -> p a e", e=EXPERTS),
                                    brow[:, :].unsqueeze(1).broadcast_to([P, G, EXPERTS]), ALU.add).then_inc(s_lg, 1)
                v.wait_ge(s_r, 2)
                skewed8(v, [(4, relus), (6, mlp_out), (0, residual), (9, statistics(2, of_x1)), (6, statistics(1, of_at)),
                            (0, statistics(0, of_h0)), (9, moments(2)), (6, moments(1)), (0, moments(0)), (2, apply0),
                            (8, apply1), (11, apply2), (13, logit)])

            @block.tensor
            def _(pe):
                def turn(g, m):
                    need(pe, s_hn, g)
                    need(pe, s_hT, g, 1)
                    for i in range(G):
                        ins = pe.transpose(pT[:, P * i:P * (i + 1)], hn[:, m % NB, i, :], ident[:, :])
                    ins.then_inc(s_pT, 1)

                def up(g, m):
                    need(pe, s_hT, g)
                    for half_, (done, free) in enumerate(((s_ph, s_h1a), (s_ph2, s_h1b))):
                        need(pe, free, g, 1)
                        for c in range(2):
                            f = 2 * half_ + c
                            ins = pe.matmul(pH[half_][:, N * c:N * (c + 1)], w_m1[:, P * f:P * (f + 1)], hT[:, m % NB, :], start=True, stop=True)
                        ins.then_inc(done, 1)

                def down(g, m):
                    need(pe, s_h1a, g)
                    need(pe, s_h1b, g)
                    need(pe, s_at, g, 2)
                    for i in range(G):
                        for c in range(NF):
                            ins = pe.matmul(pM[m % 2][:, P * i:P * (i + 1)], h1[:, m % NB, c, P * i:P * (i + 1)], w_m2[:, c, :],
                                            start=(c == 0), stop=(c == NF - 1))
                    ins.then_inc(s_pm, 1)

                def turn_xl(g, m):
                    need(pe, s_xl, g)
                    need(pe, s_xlT, g, 1)
                    for i in range(G):
                        ins = pe.transpose(pX[:, P * i:P * (i + 1)], xl[:, m % NB, i, :], ident[:, :])
                    ins.then_inc(s_px, 1)

                def route(g, m):
                    need(pe, s_xlT, g)
                    need(pe, s_lg, g, 1)
                    for i in range(G):
                        ins = pe.matmul(pL[:, EXPERTS * i:EXPERTS * (i + 1)], xlT[:, m % NB, P * i:P * (i + 1)], w_r[:, :], start=True, stop=True)
                    ins.then_inc(s_pl, 1)
                skewed8(pe, [(3, up), (5, down), (2, turn), (11, turn_xl), (12, route)])

        with ExitStack() as st:
            st.callback(stage_over)
            def sbt(name, shape, dt=F32):
                return st.enter_context(nc.sbuf_tensor(name, shape, dt))

            def pst(name, shape=[P, 512]):
                return st.enter_context(nc.psum_tensor(name, shape, F32))
            E = EXPERTS
            pr, eq, w, gt_, f1, f2, gates, selq = (sbt("r_" + n, [P, TILES, E]) for n in (
                "pr", "eq", "w", "gt", "f1", "f2", "gates", "selq"))
            rev = sbt("r_rev", [P, E])
            mx, sm, m1, m2, wm, tok = (sbt("r_" + n, [P, TILES]) for n in ("mx", "sm", "m1", "m2", "wm", "tok"))
            idx = [sbt(f"r_idx{c}", [P, TILES], U32) for c in range(2)]
            gq = sbt("r_gq", [P, 4, P])
            gT, above, same, scg, sce, pos, full = (sbt("r_" + n, [P, 512]) for n in (
                "gT", "above", "same", "scg", "sce", "pos", "full"))
            thr, cand, bit, nxt, pick = (sbt("r_" + n, [P, 1], I32) for n in ("thr", "cand", "bit", "nxt", "pick"))
            cnt = sbt("r_cnt", [P, 1])
            ends = sbt("r_ends", [P, 2])
            offs = sbt("r_offs", [P, 5])
            base = sbt("r_base", [P, 1])
            same_e = sbt("r_same_e", [P, P])
            before = sbt("r_before", [P, P])
            pG, pC, pI = pst("r_pG"), pst("r_pC"), pst("r_pI")
            s_c, s_v, s_ex, s_exp, s_q, s_pg, s_cnt, s_tot, s_end, s_off, s_pos, s_pi, s_idx, s_scat, s_go = (
                sem("r_" + n) for n in ("c", "v", "ex", "exp", "q", "pg", "cnt", "tot", "end", "off", "pos", "pi", "idx",
                                        "scat", "go"))
            s_pick, s_thr, s_nxt, s_cand = (sem("r_" + n) for n in ("pick", "thr", "nxt", "cand"))
            BITS = 30
            block = st.enter_context(nc.Block())

            def over_e(ap):
                return ap.unsqueeze(2).broadcast_to([P, TILES, E])

            def by_chunk(ap, q):
                return ap.rearrange("p (h q b) e -> p q e b h", h=2, q=4)[:, q]

            @block.gpsimd
            def _(g):
                g.memset(full[:, :], 1.0).then_inc(s_c, 1)
                g.memset(same_e[:, :], 1.0).then_inc(s_c, 1)
                g.iota(rev[:, :], [[-1, E]], base=E, channel_multiplier=0, allow_small_or_imprecise_dtypes=True).then_inc(s_c, 1)
                g.iota(tok[:, :], [[P, STEPS], [LEN, SEQS]], base=0, channel_multiplier=1, allow_small_or_imprecise_dtypes=True).then_inc(s_c, 1)
                g.memset(base[:, :], -1.0).then_inc(s_c, 1)
                g.wait_ge(s_c, 5)
                n = 5
                se = same_e[:, :].rearrange("p (e c) -> p e c", c=16)
                for b_, s_, m_ in ((0, -16, 1), (15, 16, -1)):
                    g.affine_select(out=se, in_=se, compare_op=ALU.is_ge, fill=0.0, base=b_, pattern=[[s_, E], [0, 16]],
                                    channel_multiplier=m_).then_inc(s_c, 1)
                    n += 1
                    g.wait_ge(s_c, n)
                g.affine_select(out=before[:, :], in_=same_e[:, :], compare_op=ALU.is_ge, fill=0.0, base=-1,
                                pattern=[[1, P]], channel_multiplier=-1).then_inc(s_c, 1)
                for e in range(1, E):
                    g.affine_select(out=base[:, :], in_=base[:, :], compare_op=ALU.is_ge, fill=REGION * e - 1.0,
                                    base=16 * e - 1, pattern=[[0, 1]], channel_multiplier=-1).then_inc(s_c, 1)
                    g.wait_ge(s_c, n + 1 + e)
                g.wait_ge(s_idx, 2)
                g.wait_ge(s_go, 4)
                g.wait_ge(filled, 16 * FILLS)
                for t in range(TILES):
                    for c in range(2):
                        g.indirect_dma_start(table, bass.IndirectOffsetOnAxis(ap=idx[c][:, t:t + 1], axis=0), rows[:, t, :],
                                             None, bounds_check=TABLE - 1, oob_is_err=False).then_inc(s_scat, 16)
                g.wait_ge(s_scat, 16 * 2 * TILES)

            @block.scalar
            def _(a):
                a.wait_ge(s_ex, 1)
                a.activation(pr[:, :, :], eq[:, :, :], ACT.Exp).then_inc(s_exp, 1)

            @block.tensor
            def _(pe):
                for q in range(4):
                    pe.wait_ge(s_q, q + 1)
                    pe.transpose(pG[:, P * q:P * (q + 1)], gq[:, q, :], ident[:, :]).then_inc(s_pg, 1)
                pe.wait_ge(s_c, 15)
                with pe.Fori(0, BITS) as i:
                    pe.wait_ge(s_cnt, i + 1)
                    pe.matmul(pC[:, 0:1], same_e[:, :], cnt[:, :], start=True, stop=True).then_inc(s_tot, 1)
                pe.wait_ge(s_end, 2)
                pe.matmul(pC[:, 0:2], before[:, :], ends[:, :], start=True, stop=True)
                pe.matmul(pC[:, 2:4], same_e[:, :], ends[:, :], start=True, stop=True).then_inc(s_off, 1)
                pe.wait_ge(s_pos, 1)
                for q in range(4):
                    pe.transpose(pI[:, P * q:P * (q + 1)], pos[:, P * q:P * (q + 1)], ident[:, :]).then_inc(s_pi, 1)

            @block.vector
            def _(v):
                chain = [0]

                def link(ins):
                    chain[0] += 1
                    ins.then_inc(s_v, 1)
                    v.wait_ge(s_v, chain[0])

                def best(src, top, first, weight):
                    link(v.tensor_reduce(top, src, AX.X, ALU.max))
                    link(v.tensor_tensor(eq[:, :, :], src, over_e(top), ALU.is_equal))
                    link(v.tensor_tensor(w[:, :, :], eq[:, :, :], rev[:, :].unsqueeze(1).broadcast_to([P, TILES, E]), ALU.mult))
                    link(v.tensor_reduce(weight, w[:, :, :], AX.X, ALU.max))
                    link(v.tensor_tensor(first, w[:, :, :], over_e(weight), ALU.is_equal))
                v.wait_ge(s_c, 5)
                link(v.tensor_reduce(mx[:, :], logits[:, :, :], AX.X, ALU.max))
                v.tensor_tensor(eq[:, :, :], logits[:, :, :], over_e(mx[:, :]), ALU.subtract).then_inc(s_ex, 1)
                v.wait_ge(s_exp, 1)
                link(v.tensor_reduce(sm[:, :], pr[:, :, :], AX.X, ALU.add))
                link(v.reciprocal(mx[:, :], sm[:, :]))
                link(v.tensor_tensor(pr[:, :, :], pr[:, :, :], over_e(mx[:, :]), ALU.mult))
                best(pr[:, :, :], m1[:, :], f1[:, :, :], wm[:, :])
                link(v.tensor_scalar(rows[:, :, D + 1], wm[:, :], -1.0, float(E), ALU.mult, ALU.add))
                link(v.scalar_tensor_tensor(out=gt_[:, :, :], in0=f1[:, :, :], scalar=-2.0, in1=pr[:, :, :], op0=ALU.mult, op1=ALU.add))
                best(gt_[:, :, :], m2[:, :], f2[:, :, :], wm[:, :])
                link(v.tensor_tensor(selq[:, :, :], f1[:, :, :], f2[:, :, :], ALU.add))
                link(v.tensor_tensor(gates[:, :, :], pr[:, :, :], selq[:, :, :], ALU.mult))
                link(v.scalar_tensor_tensor(out=gates[:, :, :], in0=selq[:, :, :], scalar=-1.0, in1=gates[:, :, :],
                                            op0=ALU.add, op1=ALU.add))
                for q in range(4):
                    v.tensor_copy(gq[:, q, :].rearrange("p (e b h) -> p e b h", e=E, h=2), by_chunk(gates[:, :, :], q)).then_inc(s_q, 1)
                v.tensor_copy(rows[:, :, D], tok[:, :]).then_inc(s_go, 1)
                v.tensor_copy(rows[:, :, D + 2], m1[:, :]).then_inc(s_go, 1)
                v.tensor_copy(rows[:, :, D + 3], m2[:, :]).then_inc(s_go, 1)
                v.memset(thr[:, :], 0)
                v.memset(bit[:, :], 1 << (BITS - 1))
                v.memset(cand[:, :], 1 << (BITS - 1))
                v.wait_ge(s_pg, 4)
                link(v.tensor_copy(gT[:, :], pG[:, :]))
                with v.Fori(0, BITS) as i:
                    v.tensor_scalar(above[:, :], gT[:, :], cand[:, :].bitcast(F32), 0.0, ALU.is_ge, ALU.add,
                                    accum_out=cnt[:, :]).then_inc(s_cnt, 1)
                    v.tensor_scalar(nxt[:, :], bit[:, :], 1, None, ALU.logical_shift_right).then_inc(s_nxt, 1)
                    v.wait_ge(s_tot, i + 1)
                    v.scalar_tensor_tensor(out=pick[:, :], in0=pC[:, 0:1], scalar=float(CAP), in1=bit[:, :],
                                           op0=ALU.is_ge, op1=ALU.mult).then_inc(s_pick, 1)
                    v.wait_ge(s_pick, i + 1)
                    v.tensor_tensor(thr[:, :], thr[:, :], pick[:, :], ALU.bitwise_or).then_inc(s_thr, 1)
                    v.wait_ge(s_nxt, i + 1)
                    v.tensor_copy(bit[:, :], nxt[:, :])
                    v.wait_ge(s_thr, i + 1)
                    v.tensor_tensor(cand[:, :], thr[:, :], nxt[:, :], ALU.bitwise_or).then_inc(s_cand, 1)
                    v.wait_ge(s_cand, i + 1)
                    v.wait_ge(s_cnt, i + 1)
                t = thr[:, :].bitcast(F32)
                v.tensor_scalar(above[:, :], gT[:, :], t, None, ALU.is_gt).then_inc(s_v, 1)
                chain[0] += 1
                link(v.tensor_scalar(same[:, :], gT[:, :], t, None, ALU.is_equal))
                v.tensor_tensor_scan(scg[:, :], full[:, :], above[:, :], 0.0, ALU.mult, ALU.add).then_inc(s_v, 1)
                chain[0] += 1
                link(v.tensor_tensor_scan(sce[:, :], full[:, :], same[:, :], 0.0, ALU.mult, ALU.add))
                v.tensor_copy(ends[:, 0:1], scg[:, 511:512]).then_inc(s_end, 1)
                v.tensor_copy(ends[:, 1:2], sce[:, 511:512]).then_inc(s_end, 1)
                v.wait_ge(s_off, 1)
                link(v.tensor_copy(offs[:, 0:4], pC[:, 0:4]))
                link(v.tensor_scalar(offs[:, 4:5], offs[:, 2:3], -1.0, float(CAP), ALU.mult, ALU.add))
                link(v.tensor_scalar(sce[:, :], sce[:, :], offs[:, 1:2], None, ALU.add))
                link(v.scalar_tensor_tensor(out=same[:, :], in0=sce[:, :], scalar=offs[:, 4:5], in1=same[:, :], op0=ALU.is_le, op1=ALU.mult))
                link(v.tensor_tensor(same[:, :], same[:, :], above[:, :], ALU.add))
                link(v.tensor_scalar(sce[:, :], sce[:, :], offs[:, 4:5], None, ALU.min))
                link(v.scalar_tensor_tensor(out=scg[:, :], in0=scg[:, :], scalar=offs[:, 0:1], in1=sce[:, :], op0=ALU.add, op1=ALU.add))
                link(v.tensor_scalar(scg[:, :], scg[:, :], base[:, 0:1], -FAR, ALU.add, ALU.add))
                link(v.tensor_tensor(scg[:, :], scg[:, :], same[:, :], ALU.mult))
                v.tensor_scalar(pos[:, :], scg[:, :], FAR, None, ALU.add).then_inc(s_pos, 1)
                for q in range(4):
                    v.wait_ge(s_pi, 4)
                    link(v.tensor_copy(by_chunk(gates[:, :, :], q), pI[:, P * q:P * (q + 1)].rearrange("p (e b h) -> p e b h", e=E, h=2)))
                for c, f in enumerate((f1, f2)):
                    link(v.tensor_tensor(w[:, :, :], f[:, :, :], gates[:, :, :], ALU.mult))
                    link(v.tensor_reduce(mx[:, :], w[:, :, :], AX.X, ALU.add))
                    v.tensor_copy(idx[c][:, :], mx[:, :]).then_inc(s_idx, 1)
                    v.wait_ge(s_idx, c + 1)
                v.wait_ge(s_v, chain[0])
                v.memset(cnt[:, :], 0.0).then_inc(s_go, 1)

        with ExitStack() as st:
            st.callback(stage_over)
            NB = 2
            G = ROWS // P
            STEPS_E = ESTEPS

            def sbt(name, shape, dt=F32):
                return st.enter_context(nc.sbuf_tensor(name, shape, dt))

            def pst(name, shape=[P, 512]):
                return st.enter_context(nc.psum_tensor(name, shape, F32))
            xg = sbt("e_xg", [P, NB, G, ROWLEN])
            info = sbt("e_info", [P, NB, 5, G])
            gate = sbt("e_gate", [P, 4, G])
            dest = sbt("e_dest", [P, 4, G], U32)
            xgT = sbt("e_xgT", [P, NB, ROWS])
            hb = sbt("e_h", [P, NB, NF, ROWS])
            ysum = sbt("e_ysum", [P, NB, G, D])
            yo = sbt("e_yo", [P, 4, G, D])
            we1 = sbt("e_w1", [P, 2, FF])
            we2 = sbt("e_w2", [P, 2, NF, D])
            be1 = sbt("e_b1", [P, 2, NF])
            be2 = sbt("e_b2", [P, 2, D])
            ecur = sbt("e_ecur", [P, 2])
            pT = [pst("e_pT0"), pst("e_pT1")]
            pH = [pst("e_pH0"), pst("e_pH1")]
            pO = [pst("e_pO0"), pst("e_pO1")]
            s_xg = [sem("e_xg0"), sem("e_xg1")]
            s_we = [sem("e_we0"), sem("e_we1")]
            s_scat = [sem(f"e_scat{k}") for k in range(4)]
            (s_e, s_ef, s_i1, s_i2, s_i3, s_gate, s_dest, s_pt, s_xgT, s_ph0, s_ph1, s_h0, s_h1, s_po, s_ys, s_yo) = (
                sem("e_" + n) for n in ("e", "ef", "i1", "i2", "i3", "gate", "dest", "pt", "xgT", "ph0", "ph1", "h0",
                                        "h1", "po", "ys", "yo"))
            s_i4 = sem("e_i4")
            TURN = 2 * STEPS_E
            TOTAL = EXPERTS * STEPS_E
            rows_v = table.rearrange("(n p r) c -> n p r c", p=P, r=G)
            block = st.enter_context(nc.Block())

            def turns(eng, stages):
                def body(j):
                    for i in range(TURN + max(lag for lag, _ in stages)):
                        for lag, stage in stages:
                            m = i - lag
                            if 0 <= m < TURN:
                                stage(TURN * j + m, m, j)
                body(0)
                with eng.Fori(1, EXPERTS // 2) as j:
                    body(j)

            @block.sync
            def _(sp):
                def step(n, m, j):
                    if m % STEPS_E == 0:
                        par = m // STEPS_E
                        e = 2 * j + par
                        if not isinstance(j, int):
                            sp.wait_ge(s_po, TURN * j - TURN + STEPS_E * (par + 1))
                            sp.wait_ge(s_ys, TURN * j - TURN + STEPS_E * (par + 1))
                        de = bass.ds(e, 1)
                        sp.dma_start(we1[:, par, :], W1[de].rearrange("a p f -> p (a f)")).then_inc(s_we[par], 16)
                        sp.dma_start(we2[:, par], W2[de].rearrange("a (c p) d -> p (a c) d", p=P)).then_inc(s_we[par], 16)
                        sp.dma_start(be1[:, par, :], b1[de].rearrange("a (c p) -> p (a c)", p=P)).then_inc(s_we[par], 16)
                        sp.dma_start(be2[:, par, :], b2[de].rearrange("a d -> (a d)").partition_broadcast(P)).then_inc(s_we[par], 16)
                    need(sp, s_pt, n, NB)
                    need(sp, s_dest, n, NB)
                    need(sp, s_gate, n, NB)
                    sp.dma_start(xg[:, m % 2], rows_v[bass.ds(n, 1)].rearrange("a p r c -> p (a r) c")).then_inc(s_xg[m % 2], 16)
                turns(sp, [(0, step)])

            def arrived(eng, m, j):
                eng.wait_ge(s_xg[m % 2], 16 * (STEPS_E * j + m // 2 + 1))

            def weights(eng, m, j):
                eng.wait_ge(s_we[m // STEPS_E], 64 * (j + 1))

            @block.tensor
            def _(pe):
                def turn(n, m, j):
                    arrived(pe, m, j)
                    need(pe, s_xgT, n, 2)
                    for i in range(G):
                        ins = pe.transpose(pT[m % 2][:, P * i:P * (i + 1)], xg[:, m % 2, i, 0:D], ident[:, :])
                    ins.then_inc(s_pt, 1)

                def up(n, m, j):
                    weights(pe, m, j)
                    need(pe, s_xgT, n)
                    for half_, (done, free) in enumerate(((s_ph0, s_h0), (s_ph1, s_h1))):
                        need(pe, free, n, 1)
                        for c in range(2):
                            f = 2 * half_ + c
                            ins = pe.matmul(pH[half_][:, ROWS * c:ROWS * (c + 1)], we1[:, m // STEPS_E, P * f:P * (f + 1)],
                                            xgT[:, m % 2, :], start=True, stop=True)
                        ins.then_inc(done, 1)

                def down(n, m, j):
                    need(pe, s_h0, n)
                    need(pe, s_h1, n)
                    need(pe, s_ys, n, 2)
                    for i in range(G):
                        for c in range(NF):
                            ins = pe.matmul(pO[m % 2][:, P * i:P * (i + 1)], hb[:, m % 2, c, P * i:P * (i + 1)],
                                            we2[:, m // STEPS_E, c, :], start=(c == 0), stop=(c == NF - 1))
                    ins.then_inc(s_po, 1)
                turns(pe, [(0, turn), (1, up), (2, down)])

            @block.scalar
            def _(a):
                def silus(n, m, j):
                    weights(a, m, j)
                    need(a, s_po, n, 2)
                    for half_, (src, done) in enumerate(((s_ph0, s_h0), (s_ph1, s_h1))):
                        need(a, src, n)
                        for c in range(2):
                            f = 2 * half_ + c
                            ins = a.activation(hb[:, m % 2, f, :], pH[half_][:, ROWS * c:ROWS * (c + 1)], ACT.Silu,
                                               bias=be1[:, m // STEPS_E, f:f + 1])
                        ins.then_inc(done, 1)
                turns(a, [(0, silus)])

            @block.vector
            def _(v):
                def fetched(n, m, j):
                    need(v, s_pt, n)
                    need(v, s_ph1, n, 2)
                    need(v, s_ph0, n, 2)
                    v.tensor_copy(xgT[:, m % 2, :], pT[m % 2][:, 0:ROWS]).then_inc(s_xgT, 1)

                def facts(n, m, j):
                    if m % STEPS_E == 0 and m:
                        need(v, s_i1, n, 1)
                        v.tensor_scalar(ecur[:, 1:2], ecur[:, 0:1], 1.0, None, ALU.add).then_inc(s_ef, 1)
                        v.wait_ge(s_ef, 2 * j + 1)
                    elif m == 0 and not isinstance(j, int):
                        need(v, s_i1, n, 1)
                        v.tensor_scalar(ecur[:, 0:1], ecur[:, 1:2], 1.0, None, ALU.add).then_inc(s_ef, 1)
                        v.wait_ge(s_ef, 2 * j)
                    arrived(v, m, j)
                    k, r = m % 2, xg[:, m % 2]
                    kk = (m % 4)
                    first, other, g1, g2 = (info[:, k, i] for i in range(4))
                    e = m // STEPS_E
                    v.tensor_scalar(first, r[:, :, D + 1], ecur[:, e:e + 1], None, ALU.is_equal).then_inc(s_i1, 1)
                    need(v, s_i1, n)
                    v.tensor_scalar(other, first, -1.0, 1.0, ALU.mult, ALU.add).then_inc(s_i2, 1)
                    v.tensor_tensor(g1, first, r[:, :, D + 2], ALU.mult).then_inc(s_i3, 1)
                    need(v, s_i2, n)
                    v.tensor_tensor(g2, other, r[:, :, D + 3], ALU.mult).then_inc(s_i4, 1)
                    scattered(v, m, j)
                    v.scalar_tensor_tensor(out=dest[:, kk, :], in0=other, scalar=float(TOKENS), in1=r[:, :, D], op0=ALU.mult,
                                           op1=ALU.add).then_inc(s_dest, 1)
                    need(v, s_i3, n)
                    need(v, s_i4, n)
                    v.tensor_tensor(gate[:, kk, :], g1, g2, ALU.add).then_inc(s_gate, 1)

                def scattered(eng, m, j):
                    before_ = [x for x in range(TURN) if x % 4 == m % 4 and x < m]
                    per = len([x for x in range(TURN) if x % 4 == m % 4])
                    count = (j * per + len(before_)) * 16 * G
                    if not isinstance(count, int) or count > 0:
                        eng.wait_ge(s_scat[m % 4], count)

                def results(n, m, j):
                    weights(v, m, j)
                    need(v, s_po, n)
                    need(v, s_yo, n, 2)
                    v.tensor_tensor(ysum[:, m % 2], pO[m % 2][:, 0:ROWS].rearrange("p (g d) -> p g d", g=G),
                                    be2[:, m // STEPS_E, :].unsqueeze(1).broadcast_to([P, G, D]), ALU.add).then_inc(s_ys, 1)
                    need(v, s_ys, n)
                    need(v, s_gate, n)
                    for i in range(G):
                        ins = v.tensor_scalar(yo[:, m % 4, i, :], ysum[:, m % 2, i, :], gate[:, m % 4, i:i + 1], None, ALU.mult)
                    ins.then_inc(s_yo, 1)
                v.memset(ecur[:, :], 0.0).then_inc(s_e, 1)
                v.wait_ge(s_e, 1)
                turns(v, [(2, results), (0, fetched), (0, facts)])

            @block.gpsimd
            def _(g):
                def leave(n, m, j):
                    need_apart(g, s_yo, n)
                    need_apart(g, s_dest, n)
                    for i in range(G):
                        g.indirect_dma_start(choice, bass.IndirectOffsetOnAxis(ap=dest[:, m % 4, i:i + 1], axis=0), yo[:, m % 4, i, :],
                                             None, bounds_check=2 * TOKENS - 1, oob_is_err=False).then_inc(s_scat[m % 4], 16)
                turns(g, [(0, leave)])
                for k in range(4):
                    per = len([x for x in range(TURN) if x % 4 == k])
                    g.wait_ge(s_scat[k], (EXPERTS // 2) * per * 16 * G)

        with ExitStack() as st:
            st.callback(stage_over)
            G = 4
            GROUPS = TILES // G

            def sbt(name, shape, dt=F32):
                return st.enter_context(nc.sbuf_tensor(name, shape, dt))
            ya = sbt("c_ya", [P, 2, G, D])
            yb = sbt("c_yb", [P, 2, G, D])
            ys = sbt("c_ys", [P, 2, G, D])
            yn = sbt("c_yn", [P, 2, G, D])
            ot = sbt("c_ot", [P, 2, G, D])
            stats = sbt("c_stats", [P, 2, G, 6])
            mv = sbt("c_mv", [P, 2, G, 2])
            lv = sbt("c_lv", [P, 2, G])
            rs = sbt("c_rs", [P, 2, G])
            s_in = [sem("c_in0"), sem("c_in1")]
            s_out = [sem("c_out0"), sem("c_out1")]
            s_ys, s_st, s_var, s_ln, s_rs, s_yn, s_ot = (sem("c_" + n) for n in ("ys", "st", "var", "ln", "rs", "yn", "ot"))
            first_v = choice[0:TOKENS].rearrange("(u v s p) d -> s u p v d", v=G, s=STEPS, p=P)
            other_v = choice[TOKENS:2 * TOKENS].rearrange("(u v s p) d -> s u p v d", v=G, s=STEPS, p=P)
            out_v = out.rearrange("(u v) (s p) d -> s u p v d", v=G, p=P)
            block = st.enter_context(nc.Block())

            def part(v_, g, k):
                return v_[bass.ds((g - k) // 2 if isinstance(g, int) else (g - k) >> 1, 1), k].rearrange("a p v d -> p (a v) d")

            @block.sync
            def _(sp):
                def load(g, k):
                    need(sp, s_ys, g, 2)
                    sp.dma_start(ya[:, k], part(first_v, g, k)).then_inc(s_in[k], 16)
                    sp.dma_start(yb[:, k], part(other_v, g, k)).then_inc(s_in[k], 16)

                def store(g, k):
                    need(sp, s_ot, g)
                    sp.dma_start(part(out_v, g, k), ot[:, k]).then_inc(s_out[k], 16)
                skewed(sp, GROUPS, 2, 6, [(0, load), (2, store)])
                for k in range(2):
                    sp.wait_ge(s_out[k], 16 * GROUPS // 2)

            @block.vector
            def _(v):
                def total(g, k):
                    v.wait_ge(s_in[k], 32 * (g // 2 + 1) if isinstance(g, int) else 32 * (g >> 1) + 32)
                    need(v, s_yn, g, 2)
                    v.tensor_tensor(ys[:, k], ya[:, k], yb[:, k], ALU.add).then_inc(s_ys, 1)
                    need(v, s_ys, g)
                    for i in range(G):
                        ins = v.bn_stats(stats[:, k, i, :], ys[:, k, i, :])
                    ins.then_inc(s_st, 1)
                    need_apart(v, s_st, g)
                    need_apart(v, s_ln, g, 2)
                    for i in range(G):
                        ins = v.bn_aggr(mv[:, k, i, :], stats[:, k, i, :])
                    ins.then_inc(s_var, 1)

                def finish(g, k):
                    need(v, s_rs, g)
                    need(v, s_ot, g, 2)
                    for i in range(G):
                        ins = v.tensor_scalar(yn[:, k, i, :], ys[:, k, i, :], mv[:, k, i, 0:1], rs[:, k, i:i + 1],
                                              ALU.subtract, ALU.mult)
                    ins.then_inc(s_yn, 1)
                skewed(v, GROUPS, 2, 6, [(0, total), (1, finish)])

            @block.gpsimd
            def _(g_):
                def add_x1(g, k):
                    need_apart(g_, s_yn, g)
                    count = 16 * (g // 2) if isinstance(g, int) else 16 * (g >> 1)
                    if not isinstance(g, int) or g >= 2:
                        g_.wait_ge(s_out[k], count)
                    g_.tensor_tensor(ot[:, k], yn[:, k], x1[:, bass.ds(G * g, G), :], ALU.add).then_inc(s_ot, 1)
                skewed(g_, GROUPS, 2, 6, [(0, add_x1)])

            @block.scalar
            def _(a):
                def root(g, k):
                    need(a, s_var, g)
                    a.activation(lv[:, k], mv[:, k, :, 1], ACT.Ln, bias=eps[:, 0:1]).then_inc(s_ln, 1)
                    need(a, s_ln, g)
                    need(a, s_yn, g, 2)
                    a.activation(rs[:, k], lv[:, k], ACT.Exp, scale=-0.5).then_inc(s_rs, 1)
                skewed(a, GROUPS, 2, 6, [(0, root)])


_INS = ['L0_attn_x', 'L0_attn_ln_w', 'L0_attn_ln_b', 'L0_attn_in_proj_w', 'L0_attn_conv_w', 'L0_attn_conv_b',
        'L0_attn_dt_bias', 'L0_attn_A_log', 'L0_attn_D_skip', 'L0_attn_rms_w', 'L0_attn_out_proj_w', 'L0_attn_mlp_w1',
        'L0_attn_mlp_b1', 'L0_attn_mlp_w2', 'L0_attn_mlp_b2', 'L0_ffn_Wr', 'L0_ffn_br', 'L0_ffn_W1', 'L0_ffn_b1',
        'L0_ffn_W2', 'L0_ffn_b2']


def kernel(**inputs):
    import numpy as _np
    import concourse.bacc as _bacc
    from concourse import mybir as _mybir
    from concourse.bass_utils import run_bass_kernel_spmd as _run

    nc = _bacc.Bacc("TRN2", target_bir_lowering=False, num_devices=1)
    arrays, args = {}, []
    for name in _INS:
        a = _np.ascontiguousarray(inputs[name])
        arrays[f"in_{name}_dram"] = a
        args.append(nc.dram_tensor(f"in_{name}_dram", a.shape, _mybir.dt.from_np(a.dtype), kind="ExternalInput").ap())
    args.append(nc.dram_tensor("out_0_dram", (SEQS, LEN, D), F32, kind="ExternalOutput").ap())
    build(nc, *args)
    r = _run(nc, [arrays], core_ids=[0])
    return r.results[0]["out_0_dram"]
```

```python
from contextlib import ExitStack

import concourse.bass as bass
from concourse import mybir

F32 = mybir.dt.float32
BF16 = mybir.dt.bfloat16
I32 = mybir.dt.int32
U32 = mybir.dt.uint32
ALU = mybir.AluOpType
ACT = mybir.ActivationFunctionType
AX = mybir.AxisListType

P = 128
SEQS, LEN, D = 8, 1024, 128
STEPS = LEN // P
TILES = SEQS * STEPS
TOKENS = SEQS * LEN
HEADS, HD, INNER, STATE = 32, 8, 256, 128
TAPS = 4
HALO = TAPS - 1
XBLK = HALO + P
CONV = INNER + 2 * STATE
CHUNK = 64
FF = 512
NF = FF // P
EPS = 1e-5
EXPERTS = 8
CAP = -(-12 * TOKENS // (10 * EXPERTS))
ROWS = 256
ESTEPS = -(-CAP // ROWS)
REGION = ESTEPS * ROWS
SLOTS = EXPERTS * REGION
COLS = SLOTS // P
FILLS = 2 * TOKENS // (8 * P)
ROWLEN = D + 2
STEEP = 2.0 ** 100
FAR = 65536.0


def need(eng, sem, t, back=0):
    value = t + 1 - back
    if not isinstance(value, int) or value > 0:
        eng.wait_ge(sem, value)


carrier = [None]


def need_apart(eng, sem, t, back=0):
    need(eng, sem, t, back)
    if not isinstance(t, int):
        eng.sem_inc(carrier[0], 1)


def skewed(eng, steps, unroll, head, stages):
    def at(i, which):
        for lag, stage in stages:
            t = i - lag
            if which is None:
                if 0 <= t < steps:
                    stage(t, t % unroll)
            else:
                stage(t, (which - lag) % unroll)
    for i in range(head):
        at(i, None)
    with eng.Fori(head // unroll, steps // unroll) as j:
        for u in range(unroll):
            at(j * unroll + u, u)
    for i in range(steps, steps + max(lag for lag, _ in stages)):
        at(i, None)


def build(nc, x, ln_w, ln_b, in_proj_w, conv_w, conv_b, dt_bias, A_log, D_skip, rms_w, out_proj_w,
          mlp_w1, mlp_b1, mlp_w2, mlp_b2, Wr, br, W1, b1, W2, b2, out):
    table = nc.dram_tensor("token_rows", (TOKENS, ROWLEN), F32, kind="Internal").ap()
    choice = nc.dram_tensor("choice_rows", (2 * TOKENS, D), F32, kind="Internal").ap()
    with ExitStack() as ctx:
        ctx.enter_context(nc.allow_non_contiguous_dma(reason="columns of a few hundred biases, one element a partition"))

        def sb(name, shape, dt=F32):
            return ctx.enter_context(nc.sbuf_tensor(name, shape, dt))

        stage_sems = []
        carrier[0] = nc.alloc_semaphore(name="carrier")

        def sem(name):
            s = nc.alloc_semaphore(name=name)
            stage_sems.append(s)
            return s

        def stage_over():
            nc.clear_and_free_semaphores(list(stage_sems))
            stage_sems.clear()
            nc.all_engine_barrier()

        ident = sb("ident", [P, P])
        ones = sb("ones", [P, P])
        centre = sb("centre", [P, P])
        spans = sb("spans", [P, 3, P])
        causal = sb("causal", [P, P])
        eps = sb("eps", [P, 1])
        steep = sb("steep", [1, 1], I32)
        zrow = sb("zrow", [P, 8 * D])
        filled = nc.alloc_semaphore(name="filled")
        lnw = sb("lnw", [P, 1])
        lnb = sb("lnb", [P, 1])
        b1_col = sb("b1_col", [P, NF])
        brow = sb("brow", [P, EXPERTS])
        b2row = sb("b2row", [P, D])
        dskip = sb("dskip", [P, HEADS])
        w_in = sb("w_in", [P, CONV])
        tap_w = sb("tap_w", [P, 4, TAPS])
        tap_b = sb("tap_b", [P, 4])
        w_z = sb("w_z", [P, INNER])
        w_dt = sb("w_dt", [P, HEADS])
        w_out = sb("w_out", [P, 2, D])
        w_m1 = sb("w_m1", [P, FF])
        w_m2 = sb("w_m2", [P, NF, D])
        w_r = sb("w_r", [P, EXPERTS])
        mean = sb("mean", [P, TILES])
        rstd = sb("rstd", [P, TILES])
        ssq = sb("ssq", [P, TILES])
        token_of, choice_of = (sb(n, [P, COLS], U32) for n in ("token_of", "choice_of"))
        is_other, is_first = (sb(n, [P, COLS]) for n in ("is_other", "is_first"))
        logits = sb("logits", [P, TILES, EXPERTS])
        arena = sb("arena", [P, 72 * XBLK])
        xT = arena[:, :].rearrange("p (t c) -> p t c", c=XBLK)
        x1 = arena[:, 0:TILES * D].rearrange("p (t d) -> p t d", d=D)
        arena2 = sb("arena2", [P, TILES * ROWLEN])
        dec = arena2[:, 0:4 * TILES * HEADS].rearrange("p (f t h) -> p f t h", f=4, h=HEADS)
        pre, post, gapA, gapB = (dec[:, f] for f in range(4))
        rows = arena2[:, :].rearrange("p (t c) -> p t c", c=ROWLEN)
        arena3 = sb("arena3", [P, TILES * D])
        proj = arena3[:, :].rearrange("p (t d) -> p t d", d=D)
        tmp = arena3[:, :].rearrange("p (f t h) -> p f t h", f=4, h=HEADS)
        dt, da, tail, work = (tmp[:, f] for f in range(4))

        xall = arena2[:, 0:TILES * D].rearrange("p (t d) -> p t d", d=D)
        mv = sb("moments", [P, TILES, 2])

        def group(g):
            return bass.ds(SEQS * g, SEQS)

        def tile(g, b):
            return xall[:, bass.ds(SEQS * g + b, 1), :].rearrange("p a d -> p (a d)")

        with ExitStack() as st:
            st.callback(stage_over)
            def sbt(name, shape, dt=F32):
                return st.enter_context(nc.sbuf_tensor(name, shape, dt))
            wo = sbt("wo", [P, 2, D])
            rmsw = sbt("rmsw", [P, 2])
            LOADS = 16
            stats = sbt("n_stats", [P, 2, SEQS, 6])
            mvs = sbt("n_mvs", [P, 2, SEQS, 2])
            loaded, fold, masks, s_stat, s_agg, s_var = (sem(n) for n in ("loaded", "fold", "masks", "stat", "agg", "var"))
            s_x = [sem("x0"), sem("x1")]
            x_v = x.rearrange("b (s p) d -> s p b d", p=P)
            block = st.enter_context(nc.Block())

            @block.sync
            def _(sp):
                for k in range(2):
                    sp.dma_start(xall[:, group(k), :], x_v[k]).then_inc(s_x[k], 16)
                with sp.Fori(1, STEPS // 2) as j:
                    for k in range(2):
                        sp.wait_ge(s_x[k], 16 * j)
                        sp.dma_start(xall[:, group(2 * j + k), :],
                                     x_v[bass.ds(2 * j + k, 1)].rearrange("a p b d -> p (a b) d")).then_inc(s_x[k], 16)

            @block.scalar
            def _(a):
                loads = [(w_in[:, :], in_proj_w[:, INNER:INNER + CONV]),
                         (tap_w[:, :, :], conv_w.rearrange("(m p) k -> p m k", p=P)),
                         (tap_b[:, :], conv_b.rearrange("(m p) -> p m", p=P)),
                         (wo[:, :, :], out_proj_w.rearrange("(c p) d -> p c d", p=P)),
                         (rmsw[:, :], rms_w.rearrange("(c p) -> p c", p=P)),
                         (lnw[:, :], ln_w.rearrange("(p a) -> p a", a=1)),
                         (lnb[:, :], ln_b.rearrange("(p a) -> p a", a=1)),
                         (b1_col[:, :], mlp_b1.rearrange("(c p) -> p c", p=P)),
                         (brow[:, :], br.partition_broadcast(P)),
                         (b2row[:, :], mlp_b2.partition_broadcast(P)),
                         (dskip[:, :], D_skip.partition_broadcast(P)),
                         (w_z[:, :], in_proj_w[:, 0:INNER]),
                         (w_dt[:, :], in_proj_w[:, INNER + CONV:INNER + CONV + HEADS]),
                         (w_m1[:, :], mlp_w1),
                         (w_m2[:, :, :], mlp_w2.rearrange("(c p) d -> p c d", p=P)),
                         (w_r[:, :], Wr)]
                assert len(loads) == LOADS
                for dst, src in loads:
                    a.dma_start(dst, src).then_inc(loaded, 16)
                a.wait_ge(loaded, 16 * len(loads))

            @block.gpsimd
            def _(g):
                g.memset(zrow[:, :], 0.0)
                g.memset(eps[:, :], EPS)
                g.memset(ones[:, :], 1.0)
                g.memset(xT[:, 0:SEQS, 0:HALO], 0.0)
                g.memset(ident[:, :], 0.0)
                g.memset(spans[:, :, :], 1.0)
                for q in range(4):
                    g.memset(centre[:, 32 * q:32 * q + 32], 1.0 if q % 2 else -1.0)
                g.memset(causal[:, :], 1.0).then_inc(masks, 1)
                g.wait_ge(masks, 1)
                n = 1

                def keep(ap, base, step, chan, cmp=ALU.is_ge, fill=0.0):
                    nonlocal n
                    g.affine_select(out=ap, in_=ap, compare_op=cmp, fill=fill, base=base,
                                    pattern=[[step, ap.shape[-1]]], channel_multiplier=chan).then_inc(masks, 1)
                    n += 1
                    g.wait_ge(masks, n)
                keep(ident[:, :], 0, -1, 1, ALU.not_equal, 1.0)
                for c in range(P // CHUNK):
                    part = causal[:, CHUNK * c:CHUNK * (c + 1)]
                    keep(part, CHUNK * c, 1, -1)
                    keep(part, -CHUNK * c, 0, 1)
                for q in range(4):
                    part = centre[:, 32 * q:32 * q + 32]
                    if q % 2:
                        keep(part, 32 * q, 1, -1)
                        keep(part, -32 * q, 0, 1)
                    else:
                        keep(part, -32 * q - 1, -1, 1)
                        keep(part, 32 * q + 31, 0, -1)
                keep(spans[:, 0, :], 31, 0, -1)
                keep(spans[:, 1, :], -32, 0, 1)
                keep(spans[:, 1, :], 95, 0, -1)
                keep(spans[:, 2, :], -96, 0, 1)

            @block.vector
            def _(v):
                def statistics(g, k):
                    n = g // 2 if isinstance(g, int) else (g - k) >> 1
                    v.wait_ge(s_x[k], 16 * (n + 1))
                    need(v, s_var, g, 2)
                    for b in range(SEQS):
                        i = v.bn_stats(stats[:, k, b, :], tile(g, b))
                    i.then_inc(s_stat, 1)

                def moments(g, k):
                    need_apart(v, s_stat, g)
                    for b in range(SEQS):
                        i = v.bn_aggr(mvs[:, k, b, :], stats[:, k, b, :])
                    i.then_inc(s_agg, 1)

                def keep_moments(g, k):
                    need(v, s_agg, g)
                    v.tensor_copy(mv[:, group(g), :], mvs[:, k]).then_inc(s_var, 1)

                skewed(v, STEPS, 2, 4, [(2, keep_moments), (1, moments), (0, statistics)])
                v.wait_ge(loaded, 16 * LOADS)
                for c in range(2):
                    v.tensor_scalar(w_out[:, c, :], wo[:, c, :], rmsw[:, c:c + 1], None, ALU.mult).then_inc(fold, 1)

        with ExitStack() as st:
            st.callback(stage_over)

            def sbt(name, shape, dt=F32):
                return st.enter_context(nc.sbuf_tensor(name, shape, dt))

            def pst(name, shape):
                return st.enter_context(nc.psum_tensor(name, shape, F32))
            var2, sd1, sd2, scaled_v, scale2 = (sbt("n_" + n, [P, TILES]) for n in ("var2", "sd1", "sd2", "sv", "scale2"))
            hn = sbt("n_hn", [P, 2, SEQS, D])
            xs = sbt("n_xs", [P, 2, SEQS, P])
            dtb = sbt("n_dtb", [P, HEADS])
            pT = [pst(f"n_pT{k}", [P, SEQS, P]) for k in range(2)]
            pD = [pst(f"n_pD{k}", [P, 512]) for k in range(2)]
            (s_l1, s_l2, s_q, s_v2, s_sum, s_root, s_hn, s_turn, s_xs, s_kept, s_halo, s_raw,
             s_rawr, s_dtb, s_r) = (sem("n_" + n) for n in (
                 "lone", "ltwo", "q", "vtwo", "sum", "root", "hn", "turned", "xs", "kept", "halo", "raw",
                 "rawr", "dtb", "r"))
            block = st.enter_context(nc.Block())

            @block.sync
            def _(sp):
                sp.dma_start(dtb[:, :], dt_bias.partition_broadcast(P)).then_inc(s_dtb, 16)

            @block.vector
            def _(v):
                def apply(g, k):
                    need(v, s_turn, g, 2)
                    for b in range(SEQS):
                        t = bass.ds(SEQS * g + b, 1)
                        i = v.tensor_scalar(hn[:, k, b, :], tile(g, b), mean[:, t], scale2[:, t], ALU.subtract, ALU.mult)
                    i.then_inc(s_hn, 1)

                def raw_dt(g, k):
                    need(v, s_raw, g)
                    v.tensor_tensor(dt[:, group(g), :], pD[k][:, 0:SEQS * HEADS].rearrange("p (b h) -> p b h", h=HEADS),
                                    dtb[:, :].unsqueeze(1).broadcast_to([P, SEQS, HEADS]), ALU.add).then_inc(s_rawr, 1)
                v.wait_ge(s_dtb, 16)
                v.tensor_copy(mean[:, :], mv[:, :, 0]).then_inc(s_r, 1)
                v.wait_ge(s_l1, 1)
                v.reciprocal(rstd[:, :], sd1[:, :]).then_inc(s_root, 1)
                v.wait_ge(s_root, 1)
                v.tensor_tensor(scaled_v[:, :], rstd[:, :], mv[:, :, 1], ALU.mult).then_inc(s_q, 1)
                v.wait_ge(s_q, 1)
                v.tensor_tensor(var2[:, :], scaled_v[:, :], rstd[:, :], ALU.mult).then_inc(s_v2, 1)
                v.wait_ge(s_l2, 1)
                v.tensor_tensor(sd1[:, :], sd1[:, :], sd2[:, :], ALU.mult).then_inc(s_sum, 1)
                v.wait_ge(s_sum, 1)
                v.reciprocal(scale2[:, :], sd1[:, :]).then_inc(s_root, 1)
                v.wait_ge(s_root, 2)
                v.wait_ge(s_r, 1)
                skewed(v, STEPS, 2, 4, [(0, apply), (3, raw_dt)])

            @block.gpsimd
            def _(g_):
                def store(g, k):
                    need_apart(g_, s_xs, g)
                    g_.tensor_copy(xT[:, bass.ds(SEQS * g, 4), HALO:XBLK], xs[:, k, 0:4]).then_inc(s_kept, 1)
                    g_.tensor_copy(xT[:, bass.ds(SEQS * g + SEQS, SEQS), 0:HALO], xs[:, k, :, P - HALO:P]).then_inc(s_halo, 1)
                skewed(g_, STEPS, 2, 4, [(0, store)])

            @block.tensor
            def _(pe):
                def turn(g, k):
                    need(pe, s_hn, g)
                    need(pe, s_xs, g, 2)
                    for b in range(SEQS):
                        i = pe.transpose(pT[k][:, b, :], hn[:, k, b, :], ident[:, :])
                    i.then_inc(s_turn, 1)

                def dts(g, k):
                    need(pe, s_xs, g)
                    need(pe, s_rawr, g, 2)
                    for b in range(SEQS):
                        i = pe.matmul(pD[k][:, HEADS * b:HEADS * (b + 1)], xs[:, k, b, :], w_dt[:, :],
                                      start=True, stop=True)
                    i.then_inc(s_raw, 1)
                skewed(pe, STEPS, 2, 4, [(0, turn), (1, dts)])

            @block.scalar
            def _(a):
                a.activation(sd1[:, :], mv[:, :, 1], ACT.Sqrt, bias=eps[:, 0:1]).then_inc(s_l1, 1)
                a.wait_ge(s_v2, 1)
                a.activation(sd2[:, :], var2[:, :], ACT.Sqrt, bias=eps[:, 0:1]).then_inc(s_l2, 1)

                def affine(g, k):
                    need(a, s_turn, g)
                    need(a, s_halo, g, 2)
                    need(a, s_kept, g, 2)
                    need(a, s_raw, g, 2)
                    a.activation(xT[:, bass.ds(SEQS * g + 4, 4), HALO:XBLK], pT[k][:, 4:8, :], ACT.Identity,
                                 bias=lnb[:, 0:1], scale=lnw[:, 0:1])
                    for h in range(2):
                        i = a.activation(xs[:, k, 4 * h:4 * h + 4, :], pT[k][:, 4 * h:4 * h + 4, :], ACT.Identity,
                                         bias=lnb[:, 0:1], scale=lnw[:, 0:1])
                    i.then_inc(s_xs, 1)
                skewed(a, STEPS, 2, 4, [(0, affine)])

        with ExitStack() as st:
            st.callback(stage_over)
            def pst(name, shape):
                return st.enter_context(nc.psum_tensor(name, shape, F32))
            alog = st.enter_context(nc.sbuf_tensor("d_alog", [P, HEADS], F32))
            peak = st.enter_context(nc.sbuf_tensor("d_peak", [P, 8], F32))
            peak1 = st.enter_context(nc.sbuf_tensor("d_peak1", [P, 1], F32))
            peak_all = st.enter_context(nc.sbuf_tensor("d_peak_all", [P, 1], F32))
            s_peak, s_pt = sem("d_peaks"), sem("d_pt")
            aneg = st.enter_context(nc.sbuf_tensor("d_aneg", [P, HEADS], F32))
            pc = [pst(f"d_pc{q}", [P, 512]) for q in range(4)]
            pg = [pst(f"d_pg{q}", [P, 512]) for q in range(4)]
            s_al, s_abs, s_exp, s_ln, s_a, s_neg, s_dt, s_da, s_pc, s_pg, s_post, s_pre, s_gap, s_fin = (
                sem("d_" + n) for n in ("al", "abs", "exp", "ln", "a", "neg", "dt", "da", "pc", "pg", "post",
                                        "pre", "gap", "fin"))
            QT = TILES // 4
            block = st.enter_context(nc.Block())

            def quarter(f, q):
                return f[:, QT * q:QT * (q + 1), :]

            def flat(f, q):
                return quarter(f, q).rearrange("p t h -> p (t h)")

            @block.sync
            def _(sp):
                sp.dma_start(alog[:, :], A_log.partition_broadcast(P)).then_inc(s_al, 16)
                zeros = choice.rearrange("(n p r) d -> n p (r d)", p=P, r=8)
                for n in range(2 * TOKENS // (8 * P)):
                    sp.dma_start(zeros[n], zrow[:, :]).then_inc(filled, 16)

            @block.scalar
            def _(a):
                for q in range(4):
                    a.activation(flat(work, q), flat(dt, q), ACT.Abs).then_inc(s_abs, 1)
                a.wait_ge(s_al, 16)
                a.activation(aneg[:, :], alog[:, :], ACT.Exp).then_inc(s_a, 1)
                for q in range(4):
                    a.wait_ge(s_abs, q + 1)
                    a.activation(flat(work, q), flat(work, q), ACT.Exp, scale=-1.0).then_inc(s_exp, 1)
                for q in range(4):
                    a.wait_ge(s_exp, q + 1)
                    a.activation(flat(work, q), flat(work, q), ACT.Ln, bias=1.0).then_inc(s_ln, 1)
                for q in range(4):
                    a.wait_ge(s_pc, q + 1)
                    a.activation(flat(post, q), pc[q][:, :], ACT.Exp).then_inc(s_post, 1)
                    a.activation(flat(pre, q), pc[q][:, :], ACT.Exp, scale=-1.0).then_inc(s_pre, 1)
                for f, dst in enumerate((gapA, tail, gapB)):
                    for q in range(4):
                        a.wait_ge(s_pg, 4 * f + q + 1)
                        a.activation(flat(dst, q), pg[q][:, :], ACT.Exp).then_inc(s_gap, 1)

            @block.vector
            def _(v):
                v.wait_ge(s_a, 1)
                v.tensor_scalar(alog[:, :], aneg[:, :], -1.0, None, ALU.mult).then_inc(s_neg, 1)
                v.wait_ge(s_neg, 1)
                for q in range(4):
                    v.wait_ge(s_ln, q + 1)
                    v.scalar_tensor_tensor(out=flat(dt, q), in0=flat(dt, q), scalar=0.0, in1=flat(work, q),
                                           op0=ALU.max, op1=ALU.add).then_inc(s_dt, 1)
                    v.wait_ge(s_dt, q + 1)
                    v.tensor_tensor(quarter(da, q), quarter(dt, q), alog[:, :].unsqueeze(1).broadcast_to([P, QT, HEADS]),
                                    ALU.mult).then_inc(s_da, 1)
                for q in range(4):
                    v.wait_ge(s_pre, q + 1)
                    v.tensor_reduce(peak[:, q:q + 1], flat(post, q), AX.X, ALU.max).then_inc(s_peak, 1)
                    v.tensor_reduce(peak[:, 4 + q:5 + q], flat(pre, q), AX.X, ALU.max).then_inc(s_peak, 1)
                v.wait_ge(s_peak, 8)
                v.tensor_reduce(peak1[:, :], peak[:, :], AX.X, ALU.max).then_inc(s_peak, 1)
                for q in range(4):
                    v.tensor_tensor(flat(pre, q), flat(pre, q), flat(dt, q), ALU.mult).then_inc(s_fin, 1)
                v.wait_ge(s_gap, 8)
                v.tensor_tensor(gapA[:, SEQS:TILES, :], gapA[:, SEQS:TILES, :], tail[:, 0:TILES - SEQS, :],
                                ALU.mult).then_inc(s_fin, 1)
                v.wait_ge(s_pt, 1)
                v.tensor_reduce(peak_all[0:1, :], pc[0][0:1, 0:P], AX.X, ALU.max).then_inc(s_peak, 1)
                v.wait_ge(s_peak, 10)
                v.tensor_scalar(steep[0:1, :], peak_all[0:1, :], STEEP, None, ALU.is_gt).then_inc(s_fin, 1)

            @block.tensor
            def _(pe):
                for q in range(4):
                    pe.wait_ge(s_da, q + 1)
                    pe.matmul(pc[q][:, :], centre[:, :], flat(da, q), start=True, stop=True).then_inc(s_pc, 1)
                for f, span in enumerate((0, 2, 1)):
                    for q in range(4):
                        if f:
                            pe.wait_ge(s_gap, 4 * f + q - 3)
                        pe.matmul(pg[q][:, :], spans[:, span, :], flat(da, q), start=True, stop=True).then_inc(s_pg, 1)
                pe.wait_ge(s_pre, 4)
                pe.wait_ge(s_peak, 9)
                pe.transpose(pc[0][0:1, 0:P], peak1[:, :], ident[:, :]).then_inc(s_pt, 1)

        is_steep = nc.values_load(steep[0:1, 0:1], min_val=0, max_val=1,
                                  skip_runtime_bounds_check_because="a comparison wrote it")

        with nc.If(is_steep > 0):
            with ExitStack() as st:
                st.callback(stage_over)

                def sbt(name, shape, dt=F32):
                    return st.enter_context(nc.sbuf_tensor(name, shape, dt))

                def pst(name, shape=[P, 512]):
                    return st.enter_context(nc.psum_tensor(name, shape, F32))
                dts, das = pre, post
                upto = sbt("g_upto", [P, P])
                after = sbt("g_after", [P, P])
                cv = sbt("g_cv", [P, 4, P])
                xs, bs, cs, bt, ud, ed, wt = (sbt("g_" + n, [P, P]) for n in ("xs", "bs", "cs", "bt", "ud", "ed", "wt"))
                gram_ = sbt("g_gram", [P, P])
                xt, zs, xd, xr, dx, y0, y1, y2, yg, sq, yt = (sbt("g_" + n, [P, INNER]) for n in (
                    "xt", "zs", "xd", "xr", "dx", "y0", "y1", "y2", "yg", "sq", "yt"))
                da_t, e_upto, e_after, e_all = (sbt("g_" + n, [P, HEADS]) for n in ("da", "eupto", "eafter", "eall"))
                state = sbt("g_state", [P, SEQS, INNER])
                decayed = sbt("g_decayed", [P, INNER])
                pU = [pst("g_pU0"), pst("g_pU1")]
                pTr, pG, pD, pY, pS, pO = (pst("g_" + n) for n in ("pTr", "pG", "pD", "pY", "pS", "pO"))
                (s_masks, s_const, s_done, s_u, s_tap, s_xs, s_b, s_c, s_z, s_pz, s_ptr, s_xt, s_bt, s_da, s_sums, s_exp, s_pg,
                 s_g, s_xd, s_xr, s_dx, s_ud, s_pd, s_ed, s_w, s_py, s_pi, s_ps, s_dec, s_ya, s_yb, s_yc, s_yg, s_pyt, s_yt,
                 s_po) = (sem("g_" + n) for n in (
                     "masks", "const", "done", "u", "tap", "xs", "b", "c", "z", "pz", "ptr", "xt", "bt", "da", "sums", "exp", "pg",
                     "g", "xd", "xr", "dx", "ud", "pd", "ed", "w", "py", "pi", "ps", "dec", "ya", "yb", "yc", "yg", "pyt", "yt",
                     "po"))
                block = st.enter_context(nc.Block())

                def flat1(ap):
                    return ap.rearrange("p a c -> p (a c)")

                def heads(ap):
                    return ap.rearrange("p (h c) -> p h c", c=HD)

                def over_channels(f):
                    return f.unsqueeze(2).broadcast_to([P, HEADS, HD])

                def at_tile(ap, t):
                    return flat1(ap[:, bass.ds(t, 1), :])

                @block.sync
                def _(sp):
                    sp.sem_inc(carrier[0], 1)

                @block.gpsimd
                def _(g):
                    g.memset(upto[:, :], 1.0).then_inc(s_masks, 1)
                    g.memset(after[:, :], 1.0).then_inc(s_masks, 1)
                    g.wait_ge(s_masks, 2)
                    g.affine_select(out=upto[:, :], in_=upto[:, :], compare_op=ALU.is_ge, fill=0.0, base=0,
                                    pattern=[[1, P]], channel_multiplier=-1).then_inc(s_masks, 1)
                    g.affine_select(out=after[:, :], in_=after[:, :], compare_op=ALU.is_ge, fill=0.0, base=-1,
                                    pattern=[[-1, P]], channel_multiplier=1).then_inc(s_masks, 1)

                @block.tensor
                def _(pe):
                    pe.wait_ge(s_masks, 4)
                    with pe.Fori(0, TILES) as t:
                        pe.wait_ge(s_done, 3 * t + 3)
                        tile = at_tile(xT, t)
                        for m in range(4):
                            i = pe.matmul(pU[m // 2][:, XBLK * (m % 2):XBLK * (m % 2 + 1)], w_in[:, P * m:P * (m + 1)], tile,
                                          start=True, stop=True)
                        i.then_inc(s_u, 1)
                        need(pe, s_xs, t)
                        pe.matmul(pG[:, P:P + INNER], xs[:, :], w_z[:, :], start=True, stop=True).then_inc(s_pz, 1)
                        pe.wait_ge(s_tap, 4 * t + 4)
                        for m in range(3):
                            i = pe.transpose(pTr[:, P * m:P * (m + 1)], cv[:, m, :], ident[:, :])
                        i.then_inc(s_ptr, 1)
                        need(pe, s_da, t)
                        need(pe, s_bt, t)
                        for n, mask in enumerate((upto, after, ones)):
                            c0 = 3 * P + HEADS * n
                            i = pe.matmul(pTr[:, c0:c0 + HEADS], mask[:, :], da_t[:, :], start=True, stop=True)
                        i.then_inc(s_sums, 1)
                        need(pe, s_b, t)
                        need(pe, s_c, t)
                        need(pe, s_z, t)
                        pe.matmul(pG[:, 0:P], bs[:, :], cs[:, :], start=True, stop=True).then_inc(s_pg, 1)
                        need_apart(pe, s_xd, t)
                        with pe.Fori(0, HEADS) as h:
                            n = HEADS * t + h + 1
                            pe.wait_ge(s_ud, n)
                            pe.matmul(pD[:, 0:P], after[:, :], ud[:, :], start=True, stop=True).then_inc(s_pd, 1)
                            pe.wait_ge(s_w, n)
                            pe.matmul(pY[:, bass.ds(HD * h, HD)], wt[:, :], xd[:, bass.ds(HD * h, HD)],
                                      start=True, stop=True).then_inc(s_py, 1)
                        pe.matmul(pS[:, 0:INNER], cs[:, :], at_tile(state, t & (SEQS - 1)), start=True, stop=True).then_inc(s_pi, 1)
                        need(pe, s_xr, t)
                        need(pe, s_ya, t)
                        pe.matmul(pS[:, INNER:2 * INNER], bt[:, :], xr[:, :], start=True, stop=True).then_inc(s_ps, 1)
                        need(pe, s_yg, t)
                        for c in range(2):
                            i = pe.transpose(pO[:, P * c:P * (c + 1)], yg[:, P * c:P * (c + 1)], ident[:, :])
                        i.then_inc(s_pyt, 1)
                        need(pe, s_yt, t)
                        for c in range(2):
                            i = pe.matmul(pO[:, 2 * P:3 * P], yt[:, P * c:P * (c + 1)], w_out[:, c, :], start=(c == 0), stop=(c == 1))
                        i.then_inc(s_po, 1)

                @block.scalar
                def _(a):
                    with a.Fori(0, TILES) as t:
                        need(a, s_u, t)
                        for m in range(4):
                            i = a.activation(cv[:, m, :], pU[m // 2][:, XBLK * (m % 2):XBLK * (m % 2) + P], ACT.Identity,
                                             bias=tap_b[:, m:m + 1], scale=tap_w[:, m, 0:1])
                        i.then_inc(s_tap, 1)
                        need(a, s_pz, t)
                        a.activation(zs[:, :], pG[:, P:P + INNER], ACT.Silu).then_inc(s_z, 1)
                        need(a, s_ptr, t)
                        a.activation(xt[:, :], pTr[:, 0:INNER], ACT.Silu).then_inc(s_xt, 1)
                        a.activation(bt[:, :], pTr[:, INNER:3 * P], ACT.Silu).then_inc(s_bt, 1)
                        a.activation(bs[:, :], cv[:, 2, :], ACT.Silu).then_inc(s_b, 1)
                        a.activation(cs[:, :], cv[:, 3, :], ACT.Silu).then_inc(s_c, 1)
                        need(a, s_sums, t)
                        for n, dst in enumerate((e_upto, e_after, e_all)):
                            c0 = 3 * P + HEADS * n
                            i = a.activation(dst[:, :], pTr[:, c0:c0 + HEADS], ACT.Exp)
                        i.then_inc(s_exp, 1)
                        with a.Fori(0, HEADS) as h:
                            a.wait_ge(s_pd, HEADS * t + h + 1)
                            a.activation(ed[:, :], pD[:, 0:P], ACT.Exp).then_inc(s_ed, 1)
                        need(a, s_pyt, t)
                        a.activation(yt[:, :], pO[:, 0:2 * P], ACT.Copy).then_inc(s_yt, 1)
                        a.activation(sq[:, :], yg[:, :], ACT.Square, accum_out=ssq[:, bass.ds(t, 1)]).then_inc(s_done, 1)
                        need(a, s_po, t)
                        a.activation(at_tile(proj, t), pO[:, 2 * P:3 * P], ACT.Copy).then_inc(s_done, 1)

                @block.vector
                def _(v):
                    v.tensor_copy(dts[:, :, :], dt[:, :, :]).then_inc(s_const, 1)
                    v.tensor_copy(das[:, :, :], da[:, :, :]).then_inc(s_const, 1)
                    v.memset(state[:, :, :], 0.0).then_inc(s_const, 1)
                    v.wait_ge(s_masks, 4)
                    v.wait_ge(s_const, 3)
                    v.sem_inc(s_done, 3)
                    with v.Fori(0, TILES) as t:
                        need(v, s_u, t)
                        v.tensor_copy(xs[:, :], xT[:, bass.ds(t, 1), HALO:XBLK].rearrange("p a c -> p (a c)")).then_inc(s_xs, 1)
                        v.tensor_copy(da_t[:, :], at_tile(das, t)).then_inc(s_da, 1)
                        for tap in range(1, TAPS):
                            v.wait_ge(s_tap, 4 * t + tap)
                            for m in range(4):
                                c0 = XBLK * (m % 2) + tap
                                i = v.scalar_tensor_tensor(out=cv[:, m, :], in0=pU[m // 2][:, c0:c0 + P], scalar=tap_w[:, m, tap:tap + 1],
                                                           in1=cv[:, m, :], op0=ALU.mult, op1=ALU.add)
                            i.then_inc(s_tap, 1)
                        need(v, s_xt, t)
                        v.tensor_tensor(heads(xd[:, :]), heads(xt[:, :]), over_channels(at_tile(dts, t)), ALU.mult).then_inc(s_xd, 1)
                        v.tensor_tensor(heads(dx[:, :]), heads(xt[:, :]), over_channels(dskip[:, :]), ALU.mult).then_inc(s_dx, 1)
                        need(v, s_exp, t)
                        need(v, s_xd, t)
                        v.tensor_tensor(heads(xr[:, :]), heads(xd[:, :]), over_channels(e_after[:, :]), ALU.mult).then_inc(s_xr, 1)
                        need(v, s_pg, t)
                        v.tensor_tensor(gram_[:, :], pG[:, 0:P], upto[:, :], ALU.mult).then_inc(s_g, 1)
                        need_apart(v, s_g, t)
                        with v.Fori(0, HEADS) as h:
                            v.tensor_scalar(ud[:, :], upto[:, :], da_t[:, bass.ds(h, 1)], None, ALU.mult).then_inc(s_ud, 1)
                            v.wait_ge(s_ed, HEADS * t + h + 1)
                            v.tensor_tensor(wt[:, :], ed[:, :], gram_[:, :], ALU.mult).then_inc(s_w, 1)
                        need(v, s_pi, t)
                        v.tensor_tensor(heads(y0[:, :]), heads(pS[:, 0:INNER]), over_channels(e_upto[:, :]), ALU.mult).then_inc(s_ya, 1)
                        need(v, s_ya, t)
                        v.tensor_tensor(y1[:, :], y0[:, :], pY[:, 0:INNER], ALU.add).then_inc(s_yb, 1)
                        need(v, s_yb, t)
                        v.tensor_tensor(y2[:, :], y1[:, :], dx[:, :], ALU.add).then_inc(s_yc, 1)
                        need(v, s_yc, t)
                        need(v, s_z, t)
                        v.tensor_tensor(yg[:, :], y2[:, :], zs[:, :], ALU.mult).then_inc(s_yg, 1)
                        mine = at_tile(state, t & (SEQS - 1))
                        v.tensor_tensor(heads(decayed[:, :]), heads(mine), over_channels(e_all[:, :]), ALU.mult).then_inc(s_dec, 1)
                        need(v, s_dec, t)
                        need(v, s_ps, t)
                        v.tensor_tensor(mine, decayed[:, :], pS[:, INNER:2 * INNER], ALU.add).then_inc(s_done, 1)


        with nc.Else():
            with ExitStack() as st:
                st.callback(stage_over)
                NB = 4

                def sbt(name, shape, dt=F32):
                    return st.enter_context(nc.sbuf_tensor(name, shape, dt))

                def pst(name, shape=[P, 512]):
                    return st.enter_context(nc.psum_tensor(name, shape, F32))
                cv = sbt("s_cv", [P, NB, 4, P])
                xs = sbt("s_xs", [P, NB, P])
                xt = sbt("s_xt", [P, NB, INNER])
                zs = sbt("s_zs", [P, NB, INNER])
                bs = sbt("s_bs", [P, NB, P])
                cs = sbt("s_cs", [P, NB, 3 * P])
                bt = sbt("s_bt", [P, NB, 2, P])
                gm = sbt("s_gm", [P, NB, P])
                xa = sbt("s_xa", [P, NB, INNER])
                dx = sbt("s_dx", [P, NB, INNER])
                state = sbt("s_state", [P, SEQS, INNER])
                sa = sbt("s_sa", [P, NB, INNER])
                ua = sbt("s_ua", [P, 2, INNER])
                sB = sbt("s_sb", [P, NB, INNER])
                y1 = sbt("s_y1", [P, NB, INNER])
                y2 = sbt("s_y2", [P, 2, INNER])
                yg = sbt("s_yg", [P, NB, INNER])
                sq = sbt("s_sq", [P, INNER])
                yt = sbt("s_yt", [P, NB, 2, P])
                pU = [pst("s_pU0"), pst("s_pU1")]
                pZ, pTr, pG, pS, pY, pO = (pst("s_" + n) for n in ("pZ", "pTr", "pG", "pS", "pY", "pO"))
                (s_z0, s_xs, s_pz, s_zs, s_ptr, s_xt, s_bs, s_cs, s_pg, s_gm, s_bt, s_xa, s_dx, s_ps, s_sa, s_ua, s_sb,
                 s_st, s_py, s_y1, s_y2, s_yg, s_sq, s_pyt, s_yt, s_po, s_o) = (sem("s_" + n) for n in (
                     "zero", "xs", "pz", "zs", "ptr", "xt", "bs", "cs", "pg", "gm", "bt", "xa", "dx", "ps", "sa",
                     "ua", "sb", "st", "py", "y1", "y2", "yg", "sq", "pyt", "yt", "po", "o"))
                s_u, s_tap0, s_tap1, s_tap2, s_tap3 = ([sem(f"s_{n}{m}") for m in range(2)] for n in ("u", "ta", "tb", "tc", "td"))
                s_z1 = sem("s_zeroc")
                s_tap = [s_tap0, s_tap1, s_tap2, s_tap3]
                block = st.enter_context(nc.Block())
                HEAD = 16

                def heads(ap):
                    return ap.rearrange("p (h c) -> p h c", c=HD)

                def spread(f, t):
                    return f[:, bass.ds(t, 1), :].rearrange("p a h -> p (a h)").unsqueeze(2).broadcast_to([P, HEADS, HD])

                def c_pair(k):
                    return cs[:, k, :].rearrange("p (a c) -> p a c", c=P + CHUNK)[:, :, 0:CHUNK]

                def columns(b):
                    return pU[b][:, 0:2 * XBLK].rearrange("p (m c) -> p m c", c=XBLK)

                @block.sync
                def _(sp):
                    sp.sem_inc(carrier[0], 1)

                def mine(t):
                    q = t % SEQS if isinstance(t, int) else t & (SEQS - 1)
                    return state[:, bass.ds(q, 1), :].rearrange("p a c -> p (a c)")

                @block.gpsimd
                def _(g):
                    def gated(t, k):
                        need_apart(g, s_y1, t)
                        need_apart(g, s_dx, t)
                        g.tensor_tensor(y2[:, k % 2, :], y1[:, k, :], dx[:, k, :], ALU.add).then_inc(s_y2, 1)
                        need_apart(g, s_y2, t)
                        need_apart(g, s_zs, t)
                        need_apart(g, s_sq, t, NB)
                        need_apart(g, s_pyt, t, NB)
                        g.tensor_tensor(yg[:, k, :], y2[:, k % 2, :], zs[:, k, :], ALU.mult).then_inc(s_yg, 1)

                    def scale(t, k):
                        need_apart(g, s_xt, t)
                        need_apart(g, s_py, t, NB)
                        g.tensor_tensor(heads(xa[:, k, :]), heads(xt[:, k, :]), spread(pre, t), ALU.mult).then_inc(s_xa, 1)
                        need_apart(g, s_y2, t, NB)
                        g.tensor_tensor(heads(dx[:, k, :]), heads(xt[:, k, :]),
                                        dskip[:, :].unsqueeze(2).broadcast_to([P, HEADS, HD]), ALU.mult).then_inc(s_dx, 1)

                    def carry_a(t, k):
                        need_apart(g, s_py, t, NB)
                        need_apart(g, s_ua, t, NB)
                        need_apart(g, s_st, t, SEQS)
                        g.tensor_tensor(heads(sa[:, k, :]), heads(mine(t)), spread(gapA, t), ALU.mult).then_inc(s_sa, 1)
                    g.memset(cs[:, :, :], 0.0).then_inc(s_z1, 1)
                    g.wait_ge(s_z0, 2)
                    skewed(g, TILES, NB, HEAD, [(7, gated), (3, scale), (4, carry_a)])

                @block.tensor
                def _(pe):
                    def project(t, k):
                        tile = xT[:, bass.ds(t, 1), :].rearrange("p a c -> p (a c)")
                        for b in range(2):
                            need(pe, s_tap[3][b], t, 1)
                            for m in range(2):
                                c0 = P * (2 * b + m)
                                i = pe.matmul(pU[b][:, XBLK * m:XBLK * (m + 1)], w_in[:, c0:c0 + P], tile, start=True, stop=True)
                            i.then_inc(s_u[b], 1)

                    def project_z(t, k):
                        need(pe, s_xs, t)
                        need(pe, s_zs, t, 1)
                        pe.matmul(pZ[:, 0:INNER], xs[:, k, :], w_z[:, :], start=True, stop=True).then_inc(s_pz, 1)

                    def turn_in(t, k):
                        need(pe, s_xt, t, 1)
                        need(pe, s_bt, t, 1)
                        need(pe, s_tap[3][0], t)
                        for m in range(2):
                            pe.transpose(pTr[:, P * m:P * (m + 1)], cv[:, k, m, :], ident[:, :])
                        need(pe, s_tap[3][1], t)
                        pe.transpose(pTr[:, 2 * P:3 * P], cv[:, k, 2, :], ident[:, :]).then_inc(s_ptr, 1)

                    def gram(t, k):
                        need(pe, s_bs, t)
                        need(pe, s_cs, t)
                        need(pe, s_gm, t, 1)
                        pe.matmul(pG[:, 0:P].rearrange("p (a c) -> p a c", a=2), bs[:, k, :], c_pair(k),
                                  start=True, stop=True).then_inc(s_pg, 1)

                    def states(t, k):
                        need(pe, s_bt, t)
                        need(pe, s_xa, t)
                        need(pe, s_st, t, 1)
                        for c in range(2):
                            i = pe.matmul(pS[:, INNER * c:INNER * (c + 1)], bt[:, k, c, :], xa[:, k, :], start=True, stop=True)
                        i.then_inc(s_ps, 1)

                    def outputs(t, k):
                        need(pe, s_gm, t)
                        need(pe, s_y1, t, 1)
                        pe.matmul(pY[:, 0:INNER], gm[:, k, :], xa[:, k, :], start=True, stop=False)
                        need(pe, s_sa, t)
                        pe.matmul(pY[:, 0:INNER], cs[:, k, 0:P], sa[:, k, :], start=False, stop=False)
                        need(pe, s_sb, t)
                        pe.matmul(pY[:, 0:INNER], cs[:, k, P:2 * P], sB[:, k, :], start=False, stop=True).then_inc(s_py, 1)

                    def turn_out(t, k):
                        need(pe, s_yg, t)
                        need(pe, s_o, t, 1)
                        for c in range(2):
                            i = pe.transpose(pO[:, P * c:P * (c + 1)], yg[:, k, P * c:P * (c + 1)], ident[:, :])
                        i.then_inc(s_pyt, 1)

                    def out_project(t, k):
                        need(pe, s_yt, t)
                        for c in range(2):
                            i = pe.matmul(pO[:, 2 * P:3 * P], yt[:, k, c, :], w_out[:, c, :], start=(c == 0), stop=(c == 1))
                        i.then_inc(s_po, 1)
                    skewed(pe, TILES, NB, HEAD, [(0, project), (9, out_project), (6, outputs), (4, states), (2, turn_in),
                                                 (3, gram), (5, project_z), (8, turn_out)])

                @block.scalar
                def _(a):
                    def first_tap(t, k):
                        need(a, s_ptr, t, NB)
                        need(a, s_bs, t, NB)
                        need(a, s_cs, t, NB)
                        for b in range(2):
                            need(a, s_u[b], t)
                            for m in range(2 * b, 2 * b + 2):
                                i = a.activation(cv[:, k, m, :], columns(b)[:, m - 2 * b, 0:P], ACT.Identity,
                                                 bias=tap_b[:, m:m + 1], scale=tap_w[:, m, 0:1])
                            i.then_inc(s_tap[0][b], 1)

                    def silu_bc(t, k):
                        need(a, s_tap[3][1], t)
                        need(a, s_pg, t, NB)
                        a.activation(bs[:, k, :], cv[:, k, 2, :], ACT.Silu).then_inc(s_bs, 1)
                        need(a, s_py, t, NB)
                        a.activation(c_pair(k), cv[:, k, 3, :].rearrange("p (a c) -> p a c", a=2), ACT.Silu).then_inc(s_cs, 1)

                    def silu_turned(t, k):
                        need(a, s_ptr, t)
                        need(a, s_xa, t, NB)
                        need(a, s_dx, t, NB)
                        a.activation(xt[:, k, :], pTr[:, 0:INNER], ACT.Silu).then_inc(s_xt, 1)
                        need(a, s_ps, t, NB)
                        for c in range(2):
                            r = slice(CHUNK * c, CHUNK * (c + 1))
                            i = a.activation(bt[r, k, c, :], pTr[r, INNER:INNER + P], ACT.Silu)
                        i.then_inc(s_bt, 1)

                    def fetch(t, k):
                        need(a, s_pz, t, NB)
                        a.activation(xs[:, k, :], xT[:, bass.ds(t, 1), HALO:XBLK].rearrange("p a c -> p (a c)"), ACT.Copy).then_inc(s_xs, 1)

                    def silu_z(t, k):
                        need(a, s_pz, t)
                        need(a, s_yg, t, NB)
                        a.activation(zs[:, k, :], pZ[:, 0:INNER], ACT.Silu).then_inc(s_zs, 1)

                    def squares(t, k):
                        need(a, s_pyt, t)
                        need(a, s_po, t, NB)
                        a.activation(yt[:, k].rearrange("p c n -> p (c n)"), pO[:, 0:2 * P], ACT.Copy).then_inc(s_yt, 1)
                        need(a, s_sq, t, 1)
                        a.activation(sq[:, :], yg[:, k, :], ACT.Square, accum_out=ssq[:, bass.ds(t, 1)]).then_inc(s_sq, 1)

                    def projected(t, k):
                        need(a, s_po, t)
                        a.activation(proj[:, bass.ds(t, 1), :].rearrange("p a d -> p (a d)"), pO[:, 2 * P:3 * P],
                                     ACT.Copy).then_inc(s_o, 1)
                    a.wait_ge(s_z0, 2)
                    a.wait_ge(s_z1, 1)
                    skewed(a, TILES, NB, HEAD, [(0, first_tap), (9, projected), (3, silu_turned), (2, silu_bc), (6, silu_z), (4, fetch),
                                                (8, squares)])

                @block.vector
                def _(v):
                    def taps(b, tap):
                        def stage(t, k):
                            need(v, s_tap[tap - 1][b], t)
                            for m in range(2 * b, 2 * b + 2):
                                i = v.scalar_tensor_tensor(out=cv[:, k, m, :], in0=columns(b)[:, m - 2 * b, tap:tap + P],
                                                           scalar=tap_w[:, m, tap:tap + 1], in1=cv[:, k, m, :],
                                                           op0=ALU.mult, op1=ALU.add)
                            i.then_inc(s_tap[tap][b], 1)
                        return stage

                    def mask(t, k):
                        need(v, s_pg, t)
                        need(v, s_py, t, NB)
                        v.tensor_tensor(gm[:, k, :], pG[:, 0:P], causal[:, :], ALU.mult).then_inc(s_gm, 1)

                    def add_a(t, k):
                        need(v, s_ps, t)
                        need(v, s_sa, t)
                        need(v, s_sb, t, 2)
                        v.tensor_tensor(ua[:, k % 2, :], sa[:, k, :], pS[:, 0:INNER], ALU.add).then_inc(s_ua, 1)

                    def carry_b(t, k):
                        need(v, s_ua, t)
                        v.tensor_tensor(heads(sB[:, k, :]), heads(ua[:, k % 2, :]), spread(gapB, t), ALU.mult).then_inc(s_sb, 1)

                    def add_b(t, k):
                        need(v, s_sb, t)
                        v.tensor_tensor(mine(t), sB[:, k, :], pS[:, INNER:2 * INNER], ALU.add).then_inc(s_st, 1)

                    def scaled(t, k):
                        need(v, s_py, t)
                        need(v, s_y2, t, NB)
                        v.tensor_tensor(heads(y1[:, k, :]), heads(pY[:, 0:INNER]), spread(post, t), ALU.mult).then_inc(s_y1, 1)
                    v.memset(bt[:, :, :, :], 0.0).then_inc(s_z0, 1)
                    v.memset(state[:, :, :], 0.0).then_inc(s_z0, 1)
                    v.wait_ge(s_z0, 2)
                    skewed(v, TILES, NB, HEAD, [(1, taps(0, 1)), (1, taps(1, 1)), (1, taps(0, 2)), (1, taps(1, 2)), (1, taps(0, 3)),
                                                (1, taps(1, 3)), (5, add_a), (4, mask), (5, carry_b), (7, scaled), (5, add_b)])

        with ExitStack() as st:
            st.callback(stage_over)
            NB, G = 4, 2
            GROUPS, N = TILES // G, G * P

            def sbt(name, shape, dt=F32):
                return st.enter_context(nc.sbuf_tensor(name, shape, dt))

            def pst(name, shape=[P, 512]):
                return st.enter_context(nc.psum_tensor(name, shape, F32))
            root_y, sd_y, minus_m, mr = (sbt("m_" + n, [P, TILES]) for n in ("rooty", "sdy", "mm", "mr"))
            res = sbt("m_res", [P, NB, G, D])
            h0 = sbt("m_h0", [P, NB, G, D])
            h0b = sbt("m_h0b", [P, 8, G, D])
            stats = sbt("m_stats", [P, 3, NB, G, 6])
            mv = sbt("m_mv", [P, 3, NB, G, 2])
            sd = sbt("m_sd", [P, 3, NB, G])
            rs = sbt("m_rs", [P, 3, NB, G])
            hn = sbt("m_hn", [P, NB, G, D])
            hT = sbt("m_hT", [P, NB, N])
            h1 = sbt("m_h1", [P, NB, NF, N])
            at = sbt("m_at", [P, NB, G, D])
            un = sbt("m_un", [P, NB, G, D])
            xl = sbt("m_xl", [P, NB, G, D])
            xlT = sbt("m_xlT", [P, NB, N])
            pT, pX, pM0, pM1, pL = (pst("m_" + n) for n in ("pT", "pX", "pM0", "pM1", "pL"))
            pM = [pM0, pM1]
            pH = [pst("m_pH0", [P, 512]), pst("m_pH1", [P, 512])]
            s_x = [sem(f"m_x{k}") for k in range(2)]
            (s_r, s_res, s_h0, s_h0b, s_pT, s_hT, s_ph, s_h1a, s_h1b, s_pm, s_at, s_un, s_x1, s_xl, s_keep, s_px, s_xlT, s_pl,
             s_lg, s_hn, s_extra) = (sem("m_" + n) for n in (
                 "r", "res", "h0", "h0b", "pT", "hT", "ph", "h1a", "h1b", "pm", "at", "un", "xone", "xl", "keep", "px",
                 "xlT", "pl", "lg", "hn", "extra"))
            s_ph2 = sem("m_ph2")
            s_extra2 = sem("m_extra2")
            s_st = [sem(f"m_st{i}") for i in range(3)]
            s_var = [sem(f"m_var{i}") for i in range(3)]
            s_sd = [sem(f"m_sd{i}") for i in range(3)]
            s_rs = [sem(f"m_rs{i}") for i in range(3)]
            x_v = x.rearrange("b (s p) d -> s p b d", p=P)
            block = st.enter_context(nc.Block())

            def skewed8(eng, stages):
                skewed(eng, GROUPS, 8, 16, stages)

            @block.sync
            def _(sp):
                for k in range(2):
                    sp.dma_start(rows[:, bass.ds(SEQS * k, SEQS), 0:D], x_v[k]).then_inc(s_x[k], 16)
                with sp.Fori(1, STEPS // 2) as j:
                    for k in range(2):
                        sp.wait_ge(s_x[k], 16 * j)
                        sp.dma_start(rows[:, bass.ds(2 * SEQS * j + SEQS * k, SEQS), 0:D],
                                     x_v[bass.ds(2 * j + k, 1)].rearrange("a p b d -> p (a b) d")).then_inc(s_x[k], 16)

            def tiles(ap, g):
                return ap[:, bass.ds(G * g, G), :]


            @block.gpsimd
            def _(g_):
                def residual_bias(g, m):
                    need_apart(g_, s_h0, g)
                    need_apart(g_, s_at, g, 8)
                    g_.tensor_tensor(h0b[:, m], h0[:, m % NB], b2row[:, :].unsqueeze(1).broadcast_to([P, G, D]), ALU.add).then_inc(s_h0b, 1)

                def add_x(g, m):
                    need_apart(g_, s_un, g)
                    g_.tensor_tensor(tiles(x1, g), rows[:, bass.ds(G * g, G), 0:D], un[:, m % NB], ALU.add).then_inc(s_x1, 1)

                def keep(g, m):
                    need_apart(g_, s_xl, g)
                    g_.tensor_copy(rows[:, bass.ds(G * g, G), 0:D], xl[:, m % NB]).then_inc(s_keep, 1)
                g_.tensor_tensor(mr[:, :], mean[:, :], rstd[:, :], ALU.mult).then_inc(s_extra, 1)
                g_.wait_ge(s_extra, 1)
                g_.tensor_scalar(minus_m[:, :], mr[:, :], -1.0, None, ALU.mult).then_inc(s_r, 1)
                skewed8(g_, [(0, residual_bias), (8, add_x), (11, keep)])

            @block.scalar
            def _(a):
                def root(n):
                    def stage(g, m):
                        k = m % NB
                        need(a, s_var[n], g)
                        need(a, s_rs[n], g, NB)
                        a.activation(sd[:, n, k], mv[:, n, k, :, 1], ACT.Sqrt, bias=eps[:, 0:1]).then_inc(s_sd[n], 1)
                    return stage

                def centre_x(g, m):
                    a.wait_ge(s_x[m // 4], 16 * (g // 8 + 1) if isinstance(g, int) else 16 * ((g - m) >> 3) + 16)
                    need(a, s_h0, g, NB)
                    for i in range(G):
                        t = bass.ds(G * g + i, 1)
                        ins = a.activation(res[:, m % NB, i, :], rows[:, t, 0:D].rearrange("p a d -> p (a d)"), ACT.Identity, bias=minus_m[:, t], scale=rstd[:, t])
                    ins.then_inc(s_res, 1)

                def turned(g, m):
                    need(a, s_pT, g)
                    need(a, s_ph, g, NB)
                    a.activation(hT[:, m % NB, :], pT[:, 0:N], ACT.Identity, bias=lnb[:, 0:1], scale=lnw[:, 0:1]).then_inc(s_hT, 1)

                def relus(g, m):
                    need(a, s_pm, g, NB)
                    for half_, (ready, done) in enumerate(((s_ph, s_h1a), (s_ph2, s_h1b))):
                        need(a, ready, g)
                        for c in range(2 * half_, 2 * half_ + 2):
                            ins = a.activation(h1[:, m % NB, c, :], pH[half_][:, N * (c % 2):N * (c % 2 + 1)], ACT.Relu,
                                               bias=b1_col[:, c:c + 1])
                        ins.then_inc(done, 1)

                def turned_xl(g, m):
                    need(a, s_px, g)
                    need(a, s_pl, g, NB)
                    a.activation(xlT[:, m % NB, :], pX[:, 0:N], ACT.Copy).then_inc(s_xlT, 1)
                a.activation(sd_y[:, :], ssq[:, :], ACT.Sqrt, bias=eps[:, 0:1], scale=1.0 / INNER).then_inc(s_extra2, 1)
                a.wait_ge(s_r, 2)
                skewed8(a, [(0, centre_x), (1, root(0)), (7, root(1)), (10, root(2)), (3, turned), (12, turned_xl), (4, relus)])

            @block.vector
            def _(v):
                def x1_of(g):
                    return lambda i: x1[:, bass.ds(G * g + i, 1), :].rearrange("p a d -> p (a d)")

                def statistics(n, of):
                    def stage(g, m):
                        need(v, s_rs[n], g, NB)
                        need(v, (s_h0, s_at, s_x1)[n], g)
                        for i in range(G):
                            ins = v.bn_stats(stats[:, n, m % NB, i, :], of(g, m % NB)(i))
                        ins.then_inc(s_st[n], 1)
                    return stage

                def moments(n):
                    def stage(g, m):
                        need_apart(v, s_st[n], g)
                        for i in range(G):
                            ins = v.bn_aggr(mv[:, n, m % NB, i, :], stats[:, n, m % NB, i, :])
                        ins.then_inc(s_var[n], 1)
                    return stage

                def normed(n, dst, src, k, done):
                    for i in range(G):
                        ins = v.tensor_scalar(dst[:, k, i, :], src(i), mv[:, n, k, i, 0:1], rs[:, n, k, i:i + 1],
                                              ALU.subtract, ALU.mult)
                    ins.then_inc(done, 1)

                def of_h0(g, k):
                    return lambda i: h0[:, k, i, :]

                def of_at(g, k):
                    return lambda i: at[:, k, i, :]

                def of_x1(g, k):
                    return x1_of(g)

                def residual(g, m):
                    k = m % NB
                    need(v, s_res, g)
                    need(v, s_h0b, g, NB)
                    need(v, s_hn, g, NB)
                    for i in range(G):
                        t = bass.ds(G * g + i, 1)
                        ins = v.scalar_tensor_tensor(out=h0[:, k, i, :], in0=proj[:, t, :].rearrange("p a d -> p (a d)"),
                                                     scalar=root_y[:, t], in1=res[:, k, i, :], op0=ALU.mult, op1=ALU.add)
                    ins.then_inc(s_h0, 1)

                def apply0(g, m):
                    need(v, s_rs[0], g)
                    need(v, s_pT, g, NB)
                    normed(0, hn, of_h0(g, m % NB), m % NB, s_hn)

                def mlp_out(g, m):
                    need(v, s_pm, g)
                    need(v, s_h0b, g)
                    need(v, s_un, g, NB)
                    v.tensor_tensor(at[:, m % NB].rearrange("p a d -> p (a d)"), pM[m % 2][:, 0:N], h0b[:, m].rearrange("p a d -> p (a d)"), ALU.add).then_inc(s_at, 1)

                def apply1(g, m):
                    need(v, s_rs[1], g)
                    need(v, s_x1, g, NB)
                    normed(1, un, of_at(g, m % NB), m % NB, s_un)

                def apply2(g, m):
                    need(v, s_rs[2], g)
                    need(v, s_px, g, NB)
                    need(v, s_keep, g, NB)
                    normed(2, xl, x1_of(g), m % NB, s_xl)

                def logit(g, m):
                    need(v, s_pl, g)
                    v.tensor_tensor(tiles(logits, g), pL[:, 0:G * EXPERTS].rearrange("p (a e) -> p a e", e=EXPERTS),
                                    brow[:, :].unsqueeze(1).broadcast_to([P, G, EXPERTS]), ALU.add).then_inc(s_lg, 1)
                def invert(n):
                    def stage(g, m):
                        need(v, s_sd[n], g)
                        v.reciprocal(rs[:, n, m % NB], sd[:, n, m % NB]).then_inc(s_rs[n], 1)
                    return stage
                v.wait_ge(s_extra2, 1)
                v.reciprocal(root_y[:, :], sd_y[:, :]).then_inc(s_r, 1)
                v.wait_ge(s_r, 2)
                skewed8(v, [(6, mlp_out), (0, residual), (9, statistics(2, of_x1)), (6, statistics(1, of_at)),
                            (0, statistics(0, of_h0)), (9, moments(2)), (6, moments(1)), (0, moments(0)), (10, invert(2)),
                            (7, invert(1)), (1, invert(0)), (2, apply0), (8, apply1), (11, apply2), (13, logit)])

            @block.tensor
            def _(pe):
                def turn(g, m):
                    need(pe, s_hn, g)
                    need(pe, s_hT, g, 1)
                    for i in range(G):
                        ins = pe.transpose(pT[:, P * i:P * (i + 1)], hn[:, m % NB, i, :], ident[:, :])
                    ins.then_inc(s_pT, 1)

                def up(g, m):
                    need(pe, s_hT, g)
                    for half_, (done, free) in enumerate(((s_ph, s_h1a), (s_ph2, s_h1b))):
                        need(pe, free, g, 1)
                        for c in range(2):
                            f = 2 * half_ + c
                            ins = pe.matmul(pH[half_][:, N * c:N * (c + 1)], w_m1[:, P * f:P * (f + 1)], hT[:, m % NB, :], start=True, stop=True)
                        ins.then_inc(done, 1)

                def down(g, m):
                    need(pe, s_h1a, g)
                    need(pe, s_h1b, g)
                    need(pe, s_at, g, 2)
                    for i in range(G):
                        for c in range(NF):
                            ins = pe.matmul(pM[m % 2][:, P * i:P * (i + 1)], h1[:, m % NB, c, P * i:P * (i + 1)], w_m2[:, c, :],
                                            start=(c == 0), stop=(c == NF - 1))
                    ins.then_inc(s_pm, 1)

                def turn_xl(g, m):
                    need(pe, s_xl, g)
                    need(pe, s_xlT, g, 1)
                    for i in range(G):
                        ins = pe.transpose(pX[:, P * i:P * (i + 1)], xl[:, m % NB, i, :], ident[:, :])
                    ins.then_inc(s_px, 1)

                def route(g, m):
                    need(pe, s_xlT, g)
                    need(pe, s_lg, g, 1)
                    for i in range(G):
                        ins = pe.matmul(pL[:, EXPERTS * i:EXPERTS * (i + 1)], xlT[:, m % NB, P * i:P * (i + 1)], w_r[:, :], start=True, stop=True)
                    ins.then_inc(s_pl, 1)
                skewed8(pe, [(5, down), (3, up), (12, route), (2, turn), (11, turn_xl)])

        with ExitStack() as st:
            st.callback(stage_over)
            def sbt(name, shape, dt=F32):
                return st.enter_context(nc.sbuf_tensor(name, shape, dt))

            def pst(name, shape=[P, 512]):
                return st.enter_context(nc.psum_tensor(name, shape, F32))
            E = EXPERTS
            pr, eq, w, gt_, f1, f2, gates, selq = (sbt("r_" + n, [P, TILES, E]) for n in (
                "pr", "eq", "w", "gt", "f1", "f2", "gates", "selq"))
            rev = sbt("r_rev", [P, E])
            mx, sm, m1, m2, wm = (sbt("r_" + n, [P, TILES]) for n in ("mx", "sm", "m1", "m2", "wm"))
            slot, part_i = (sbt("r_" + n, [P, TILES], I32) for n in ("slot", "part"))
            col_of, lane_of, high = (sbt("r_" + n, [P, 2 * TILES], BF16) for n in ("col", "lane", "high"))
            cols, lanes = sbt("r_cols", [P, COLS], BF16), sbt("r_lanes", [P, P], BF16)
            own = sbt("r_own", [P, 1])
            SET = 4
            SETS = 2 * TILES // SET
            hot = sbt("r_hot", [P, 4, SET, P], BF16)
            here = sbt("r_here", [P, 4, SET, COLS], BF16)
            digits = sbt("r_digits", [P, 4, SET, 2, COLS], BF16)
            acc, vals, vacant = sbt("r_acc", [P, 2, COLS]), sbt("r_vals", [P, COLS]), sbt("r_vacant", [P, COLS])
            pL = pst("r_pL")
            s_hot, s_mm, s_rows = sem("r_hot"), sem("r_mm"), sem("r_rows")
            s_here, s_high, s_low, s_bits = (sem("r_" + n) for n in ("here", "high", "low", "bits"))
            gq = sbt("r_gq", [P, 4, P])
            gT, above, same, scg, sce, pos, full = (sbt("r_" + n, [P, 512]) for n in (
                "gT", "above", "same", "scg", "sce", "pos", "full"))
            thr, pick = (sbt("r_" + n, [P, 1], I32) for n in ("thr", "pick"))
            cand = sbt("r_cand", [P, 3], I32)
            cnt, reach, digit = sbt("r_cnt", [P, 3]), sbt("r_reach", [P, 3]), sbt("r_digit", [P, 1])
            ends = sbt("r_ends", [P, 2])
            offs = sbt("r_offs", [P, 5])
            base = sbt("r_base", [P, 1])
            same_e = sbt("r_same_e", [P, P])
            before = sbt("r_before", [P, P])
            pG, pC, pI = pst("r_pG"), pst("r_pC"), pst("r_pI")
            s_c, s_v, s_ex, s_exp, s_q, s_pg, s_cnt, s_tot, s_end, s_off, s_pos, s_pi, s_go = (
                sem("r_" + n) for n in ("c", "v", "ex", "exp", "q", "pg", "cnt", "tot", "end", "off", "pos", "pi", "go"))
            s_pick, s_thr, s_digit, s_cand = (sem("r_" + n) for n in ("pick", "thr", "digit", "cand"))
            PAIRS = 15
            options = sbt("r_options", [P, PAIRS + 1, 3], I32)
            block = st.enter_context(nc.Block())

            def sets(eng, stage):
                for k in range(4):
                    stage(0, k)
                with eng.Fori(1, SETS // 4 - 1) as j:
                    for k in range(4):
                        stage(j, k)
                for k in range(4):
                    stage(SETS // 4 - 1, k)

            def of_set(ap, i):
                return ap[:, bass.ds(SET * i, SET)]

            def over_e(ap):
                return ap.unsqueeze(2).broadcast_to([P, TILES, E])

            def by_chunk(ap, q):
                return ap.rearrange("p (h q b) e -> p q e b h", h=2, q=4)[:, q]

            @block.gpsimd
            def _(g):
                g.memset(full[:, :], 1.0).then_inc(s_c, 1)
                g.memset(same_e[:, :], 1.0).then_inc(s_c, 1)
                g.iota(rev[:, :], [[-1, E]], base=E, channel_multiplier=0, allow_small_or_imprecise_dtypes=True).then_inc(s_c, 1)
                for c in range(2):
                    g.iota(high[:, TILES * c:TILES * (c + 1)], [[1, STEPS], [STEPS, SEQS]], base=1 + TILES * c, channel_multiplier=0,
                           allow_small_or_imprecise_dtypes=True)
                g.iota(cols[:, :], [[1, COLS]], base=0, channel_multiplier=0, allow_small_or_imprecise_dtypes=True)
                g.iota(lanes[:, :], [[1, P]], base=0, channel_multiplier=0, allow_small_or_imprecise_dtypes=True)
                g.iota(own[:, :], [[0, 1]], base=0, channel_multiplier=1, allow_small_or_imprecise_dtypes=True).then_inc(s_c, 1)
                g.memset(base[:, :], -1.0).then_inc(s_c, 1)
                g.wait_ge(s_c, 5)
                n = 5
                se = same_e[:, :].rearrange("p (e c) -> p e c", c=16)
                for b_, s_, m_ in ((0, -16, 1), (15, 16, -1)):
                    g.affine_select(out=se, in_=se, compare_op=ALU.is_ge, fill=0.0, base=b_, pattern=[[s_, E], [0, 16]],
                                    channel_multiplier=m_).then_inc(s_c, 1)
                    n += 1
                    g.wait_ge(s_c, n)
                g.affine_select(out=before[:, :], in_=same_e[:, :], compare_op=ALU.is_ge, fill=0.0, base=-1,
                                pattern=[[1, P]], channel_multiplier=-1).then_inc(s_c, 1)
                for e in range(1, E):
                    g.affine_select(out=base[:, :], in_=base[:, :], compare_op=ALU.is_ge, fill=REGION * e - 1.0,
                                    base=16 * e - 1, pattern=[[0, 1]], channel_multiplier=-1).then_inc(s_c, 1)
                    g.wait_ge(s_c, n + 1 + e)
                for b in range(PAIRS):
                    for o in range(3):
                        g.memset(options[:, b, o:o + 1], (o + 1) << (2 * (PAIRS - 1 - b)))
                g.memset(options[:, PAIRS, :], 0).then_inc(s_bits, 1)

                def high_digit(j, k):
                    i = 4 * j + k
                    need_apart(g, s_mm, i, 4)
                    need_apart(g, s_here, i)
                    g.tensor_tensor(digits[:, k, :, 0, :], here[:, k], of_set(high, i).unsqueeze(2).broadcast_to([P, SET, COLS]),
                                    ALU.mult).then_inc(s_high, 1)
                sets(g, high_digit)

            @block.sync
            def _(sp):
                rows_d = table.rearrange("(b s p) c -> s p b c", s=STEPS, p=P)
                sp.wait_ge(s_go, 2)
                for step in range(STEPS):
                    sp.dma_start(rows_d[step], rows[:, SEQS * step:SEQS * (step + 1), :]).then_inc(s_rows, 16)
                sp.wait_ge(s_rows, 16 * STEPS)

            @block.scalar
            def _(a):
                a.wait_ge(s_ex, 1)
                a.activation(pr[:, :, :], eq[:, :, :], ACT.Exp).then_inc(s_exp, 1)

                def low_digit(j, k):
                    i = 4 * j + k
                    need(a, s_mm, i, 4)
                    need(a, s_here, i)
                    a.activation(digits[:, k, :, 1, :], here[:, k], ACT.Identity, scale=own[:, 0:1]).then_inc(s_low, 1)
                sets(a, low_digit)

            @block.tensor
            def _(pe):
                for q in range(4):
                    pe.wait_ge(s_q, q + 1)
                    pe.transpose(pG[:, P * q:P * (q + 1)], gq[:, q, :], ident[:, :]).then_inc(s_pg, 1)
                pe.wait_ge(s_c, 15)
                with pe.Fori(0, PAIRS) as i:
                    pe.wait_ge(s_cnt, i + 1)
                    pe.matmul(pC[:, 0:3], same_e[:, :], cnt[:, :], start=True, stop=True).then_inc(s_tot, 1)
                pe.wait_ge(s_end, 2)
                pe.matmul(pC[:, 0:2], before[:, :], ends[:, :], start=True, stop=True)
                pe.matmul(pC[:, 2:4], same_e[:, :], ends[:, :], start=True, stop=True).then_inc(s_off, 1)
                pe.wait_ge(s_pos, 1)
                for q in range(4):
                    pe.transpose(pI[:, P * q:P * (q + 1)], pos[:, P * q:P * (q + 1)], ident[:, :]).then_inc(s_pi, 1)

                def place(j, k):
                    i = 4 * j + k
                    need(pe, s_hot, i)
                    need(pe, s_high, i)
                    need(pe, s_low, i)
                    for u in range(SET):
                        first, last = (isinstance(i, int) and (i, u) == x for x in ((0, 0), (SETS - 1, SET - 1)))
                        ins = pe.matmul(pL[:, 0:2 * COLS], hot[:, k, u, :], digits[:, k, u].rearrange("p d c -> p (d c)"),
                                        start=first, stop=last)
                    ins.then_inc(s_mm, 1)
                sets(pe, place)

            @block.vector
            def _(v):
                chain = [0]

                def link(ins):
                    chain[0] += 1
                    ins.then_inc(s_v, 1)
                    v.wait_ge(s_v, chain[0])

                def best(src, top, first, weight):
                    link(v.tensor_reduce(top, src, AX.X, ALU.max))
                    link(v.tensor_tensor(eq[:, :, :], src, over_e(top), ALU.is_equal))
                    link(v.tensor_tensor(w[:, :, :], eq[:, :, :], rev[:, :].unsqueeze(1).broadcast_to([P, TILES, E]), ALU.mult))
                    link(v.tensor_reduce(weight, w[:, :, :], AX.X, ALU.max))
                    link(v.tensor_tensor(first, w[:, :, :], over_e(weight), ALU.is_equal))
                v.wait_ge(s_c, 5)
                link(v.tensor_reduce(mx[:, :], logits[:, :, :], AX.X, ALU.max))
                v.tensor_tensor(eq[:, :, :], logits[:, :, :], over_e(mx[:, :]), ALU.subtract).then_inc(s_ex, 1)
                v.wait_ge(s_exp, 1)
                link(v.tensor_reduce(sm[:, :], pr[:, :, :], AX.X, ALU.add))
                link(v.reciprocal(mx[:, :], sm[:, :]))
                link(v.tensor_tensor(pr[:, :, :], pr[:, :, :], over_e(mx[:, :]), ALU.mult))
                best(pr[:, :, :], m1[:, :], f1[:, :, :], wm[:, :])
                link(v.scalar_tensor_tensor(out=gt_[:, :, :], in0=f1[:, :, :], scalar=-2.0, in1=pr[:, :, :], op0=ALU.mult, op1=ALU.add))
                best(gt_[:, :, :], m2[:, :], f2[:, :, :], wm[:, :])
                link(v.tensor_tensor(selq[:, :, :], f1[:, :, :], f2[:, :, :], ALU.add))
                link(v.tensor_tensor(gates[:, :, :], pr[:, :, :], selq[:, :, :], ALU.mult))
                link(v.scalar_tensor_tensor(out=gates[:, :, :], in0=selq[:, :, :], scalar=-1.0, in1=gates[:, :, :],
                                            op0=ALU.add, op1=ALU.add))
                for q in range(4):
                    v.tensor_copy(gq[:, q, :].rearrange("p (e b h) -> p e b h", e=E, h=2), by_chunk(gates[:, :, :], q)).then_inc(s_q, 1)
                v.tensor_copy(rows[:, :, D], m1[:, :]).then_inc(s_go, 1)
                v.tensor_copy(rows[:, :, D + 1], m2[:, :]).then_inc(s_go, 1)
                v.memset(thr[:, :], 0)
                v.wait_ge(s_bits, 1)
                v.tensor_copy(cand[:, :], options[:, 0, :]).then_inc(s_cand, 1)
                v.wait_ge(s_pg, 4)
                link(v.tensor_copy(gT[:, :], pG[:, :]))
                def search(i):
                    need(v, s_cand, i)
                    for o in range(3):
                        ins = v.tensor_scalar((above, same, pos)[o][:, :], gT[:, :], cand[:, o:o + 1].bitcast(F32), 0.0, ALU.is_ge, ALU.add,
                                              accum_out=cnt[:, o:o + 1])
                    ins.then_inc(s_cnt, 1)
                    need(v, s_tot, i)
                    v.tensor_scalar(reach[:, :], pC[:, 0:3], float(CAP), 0.0, ALU.is_ge, ALU.add,
                                    accum_out=digit[:, :]).then_inc(s_digit, 1)
                    need(v, s_digit, i)
                    v.scalar_tensor_tensor(out=pick[:, :], in0=digit[:, :], scalar=1.0,
                                           in1=options[:, bass.ds(i, 1), 0:1].rearrange("p a b -> p (a b)"),
                                           op0=ALU.mult, op1=ALU.mult).then_inc(s_pick, 1)
                    need(v, s_pick, i)
                    v.tensor_tensor(thr[:, :], thr[:, :], pick[:, :], ALU.bitwise_or).then_inc(s_thr, 1)
                    need(v, s_thr, i)
                    v.tensor_tensor(cand[:, :], thr[:, :].broadcast_to([P, 3]),
                                    options[:, bass.ds(i + 1, 1), :].rearrange("p a b -> p (a b)"),
                                    ALU.bitwise_or).then_inc(s_cand, 1)
                with v.Fori(0, PAIRS // 3) as j:
                    for u in range(3):
                        search(3 * j + u)
                v.wait_ge(s_cnt, PAIRS)
                t = thr[:, :].bitcast(F32)
                v.tensor_scalar(above[:, :], gT[:, :], t, None, ALU.is_gt).then_inc(s_v, 1)
                chain[0] += 1
                link(v.tensor_scalar(same[:, :], gT[:, :], t, None, ALU.is_equal))
                v.tensor_tensor_scan(scg[:, :], full[:, :], above[:, :], 0.0, ALU.mult, ALU.add).then_inc(s_v, 1)
                chain[0] += 1
                link(v.tensor_tensor_scan(sce[:, :], full[:, :], same[:, :], 0.0, ALU.mult, ALU.add))
                v.tensor_copy(ends[:, 0:1], scg[:, 511:512]).then_inc(s_end, 1)
                v.tensor_copy(ends[:, 1:2], sce[:, 511:512]).then_inc(s_end, 1)
                v.wait_ge(s_off, 1)
                link(v.tensor_copy(offs[:, 0:4], pC[:, 0:4]))
                link(v.tensor_scalar(offs[:, 4:5], offs[:, 2:3], -1.0, float(CAP), ALU.mult, ALU.add))
                link(v.tensor_scalar(sce[:, :], sce[:, :], offs[:, 1:2], None, ALU.add))
                link(v.scalar_tensor_tensor(out=same[:, :], in0=sce[:, :], scalar=offs[:, 4:5], in1=same[:, :], op0=ALU.is_le, op1=ALU.mult))
                link(v.tensor_tensor(same[:, :], same[:, :], above[:, :], ALU.add))
                link(v.tensor_scalar(sce[:, :], sce[:, :], offs[:, 4:5], None, ALU.min))
                link(v.scalar_tensor_tensor(out=scg[:, :], in0=scg[:, :], scalar=offs[:, 0:1], in1=sce[:, :], op0=ALU.add, op1=ALU.add))
                link(v.tensor_scalar(scg[:, :], scg[:, :], base[:, 0:1], -FAR, ALU.add, ALU.add))
                link(v.tensor_tensor(scg[:, :], scg[:, :], same[:, :], ALU.mult))
                v.tensor_scalar(pos[:, :], scg[:, :], FAR, None, ALU.add).then_inc(s_pos, 1)
                for q in range(4):
                    v.wait_ge(s_pi, 4)
                    link(v.tensor_copy(by_chunk(gates[:, :, :], q), pI[:, P * q:P * (q + 1)].rearrange("p (e b h) -> p e b h", e=E, h=2)))
                for c, f in enumerate((f1, f2)):
                    link(v.tensor_tensor(w[:, :, :], f[:, :, :], gates[:, :, :], ALU.mult))
                    link(v.tensor_reduce(mx[:, :], w[:, :, :], AX.X, ALU.add))
                    link(v.tensor_copy(slot[:, :], mx[:, :]))
                    link(v.tensor_scalar(part_i[:, :], slot[:, :], P - 1, None, ALU.bitwise_and))
                    link(v.tensor_copy(lane_of[:, TILES * c:TILES * (c + 1)], part_i[:, :]))
                    link(v.tensor_scalar(part_i[:, :], slot[:, :], 7, None, ALU.logical_shift_right))
                    link(v.tensor_copy(col_of[:, TILES * c:TILES * (c + 1)], part_i[:, :]))

                def mark(j, k):
                    i = 4 * j + k
                    need(v, s_low, i, 4)
                    need(v, s_high, i, 4)
                    v.tensor_tensor(here[:, k], cols[:, :].unsqueeze(1).broadcast_to([P, SET, COLS]),
                                    of_set(col_of, i).unsqueeze(2).broadcast_to([P, SET, COLS]), ALU.is_equal).then_inc(s_here, 1)
                    need(v, s_mm, i, 4)
                    v.tensor_tensor(hot[:, k], lanes[:, :].unsqueeze(1).broadcast_to([P, SET, P]),
                                    of_set(lane_of, i).unsqueeze(2).broadcast_to([P, SET, P]), ALU.is_equal).then_inc(s_hot, 1)
                sets(v, mark)
                v.wait_ge(s_mm, SETS)
                link(v.tensor_copy(acc[:, :, :].rearrange("p d c -> p (d c)"), pL[:, 0:2 * COLS]))
                link(v.scalar_tensor_tensor(out=vals[:, :], in0=acc[:, 0, :], scalar=float(P), in1=acc[:, 1, :],
                                            op0=ALU.mult, op1=ALU.add))
                link(v.tensor_scalar(vals[:, :], vals[:, :], -float(P), None, ALU.add))
                link(v.tensor_scalar(vacant[:, :], acc[:, 0, :], 0.0, FAR + P, ALU.is_equal, ALU.mult))
                link(v.tensor_scalar(is_other[:, :], vals[:, :], float(TOKENS), None, ALU.is_ge))
                link(v.tensor_scalar(is_first[:, :], is_other[:, :], -1.0, 1.0, ALU.mult, ALU.add))
                link(v.tensor_tensor(acc[:, 1, :], vals[:, :], vacant[:, :], ALU.add))
                link(v.tensor_copy(choice_of[:, :], acc[:, 1, :]))
                link(v.scalar_tensor_tensor(out=vals[:, :], in0=is_other[:, :], scalar=-float(TOKENS), in1=vals[:, :],
                                            op0=ALU.mult, op1=ALU.add))
                link(v.tensor_scalar(vals[:, :], vals[:, :], 0.0, None, ALU.max))
                link(v.tensor_copy(token_of[:, :], vals[:, :]))

        with ExitStack() as st:
            st.callback(stage_over)
            G = ROWS // P
            TURN = 2 * ESTEPS
            TOTAL = EXPERTS * ESTEPS
            NB = ESTEPS

            def sbt(name, shape, dt=F32):
                return st.enter_context(nc.sbuf_tensor(name, shape, dt))

            def pst(name, shape=[P, 512]):
                return st.enter_context(nc.psum_tensor(name, shape, F32))
            source = sbt("e_source", [P, NB, G], U32)
            dest = sbt("e_dest", [P, NB, G], U32)
            xg = sbt("e_xg", [P, NB, G, ROWLEN])
            g1, g2, gate = (sbt("e_" + n, [P, NB, G]) for n in ("g1", "g2", "gate"))
            xgT = sbt("e_xgT", [P, 2, ROWS])
            hb = sbt("e_h", [P, 2, NF, ROWS])
            ysum = sbt("e_ysum", [P, 2, G, D])
            yo = sbt("e_yo", [P, NB, G, D])
            we1 = sbt("e_w1", [P, 2, FF])
            we2 = sbt("e_w2", [P, 2, NF, D])
            be1 = sbt("e_b1", [P, 2, NF])
            be2 = sbt("e_b2", [P, 2, D])
            pT = [pst("e_pT0"), pst("e_pT1")]
            pH = [pst("e_pH0"), pst("e_pH1")]
            pO = [pst("e_pO0"), pst("e_pO1")]
            s_we = [sem("e_we0"), sem("e_we1")]
            s_xg = [sem(f"e_xg{k}") for k in range(NB)]
            s_scat = [sem(f"e_scat{k}") for k in range(NB)]
            (s_src, s_dest, s_g1, s_g2, s_gate, s_pt, s_xgT, s_ph0, s_ph1, s_h0, s_h1, s_po, s_ys, s_yo) = (
                sem("e_" + n) for n in ("src", "dest", "g1", "g2", "gate", "pt", "xgT", "ph0", "ph1", "h0", "h1", "po",
                                        "ys", "yo"))
            block = st.enter_context(nc.Block())

            def run(eng, stages):
                skewed(eng, TOTAL, TURN, TURN, stages)

            def earlier(n, m):
                return (n - m) // ESTEPS + m // NB

            def columns(n):
                return bass.ds(G * n, G)

            def arrived(eng, n, m):
                eng.wait_ge(s_xg[m % NB], 16 * G * (earlier(n, m) + 1))

            def left(eng, n, m):
                count = 16 * G * earlier(n, m)
                if not isinstance(count, int) or count > 0:
                    eng.wait_ge(s_scat[m % NB], count)

            def weights(eng, n, m):
                eng.wait_ge(s_we[m // ESTEPS], 64 * ((n - m) // TURN + 1))

            @block.sync
            def _(sp):
                def load(j):
                    for par in range(2):
                        if not isinstance(j, int):
                            sp.wait_ge(s_po, TURN * j - TURN + ESTEPS * (par + 1))
                            sp.wait_ge(s_ys, TURN * j - TURN + ESTEPS * (par + 1))
                        e = bass.ds(2 * j + par, 1)
                        sp.dma_start(we1[:, par, :], W1[e].rearrange("a p f -> p (a f)")).then_inc(s_we[par], 16)
                        sp.dma_start(we2[:, par], W2[e].rearrange("a (c p) d -> p (a c) d", p=P)).then_inc(s_we[par], 16)
                        sp.dma_start(be1[:, par, :], b1[e].rearrange("a (c p) -> p (a c)", p=P)).then_inc(s_we[par], 16)
                        sp.dma_start(be2[:, par, :], b2[e].rearrange("a d -> (a d)").partition_broadcast(P)).then_inc(s_we[par], 16)
                load(0)
                with sp.Fori(1, EXPERTS // 2) as j:
                    load(j)

            @block.gpsimd
            def _(g):
                def fetch(n, m):
                    need_apart(g, s_src, n)
                    need_apart(g, s_pt, n, NB)
                    need_apart(g, s_g1, n, NB)
                    need_apart(g, s_g2, n, NB)
                    for i in range(G):
                        g.indirect_dma_start(xg[:, m % NB, i, :], None, table,
                                             bass.IndirectOffsetOnAxis(ap=source[:, m % NB, i:i + 1], axis=0),
                                             bounds_check=TOKENS - 1, oob_is_err=False).then_inc(s_xg[m % NB], 16)

                def leave(n, m):
                    need_apart(g, s_yo, n)
                    need_apart(g, s_dest, n)
                    for i in range(G):
                        g.indirect_dma_start(choice, bass.IndirectOffsetOnAxis(ap=dest[:, m % NB, i:i + 1], axis=0),
                                             yo[:, m % NB, i, :], None, bounds_check=2 * TOKENS - 1,
                                             oob_is_err=False).then_inc(s_scat[m % NB], 16)
                g.wait_ge(filled, 16 * FILLS)
                run(g, [(1, fetch), (6, leave)])
                for k in range(NB):
                    g.wait_ge(s_scat[k], 16 * G * (TOTAL // NB))

            @block.tensor
            def _(pe):
                def turn(n, m):
                    arrived(pe, n, m)
                    need(pe, s_xgT, n, 2)
                    for i in range(G):
                        ins = pe.transpose(pT[m % 2][:, P * i:P * (i + 1)], xg[:, m % NB, i, 0:D], ident[:, :])
                    ins.then_inc(s_pt, 1)

                def up(n, m):
                    weights(pe, n, m)
                    need(pe, s_xgT, n)
                    for half_, (done, free) in enumerate(((s_ph0, s_h0), (s_ph1, s_h1))):
                        need(pe, free, n, 1)
                        for c in range(2):
                            f = 2 * half_ + c
                            ins = pe.matmul(pH[half_][:, ROWS * c:ROWS * (c + 1)], we1[:, m // ESTEPS, P * f:P * (f + 1)],
                                            xgT[:, m % 2, :], start=True, stop=True)
                        ins.then_inc(done, 1)

                def down(n, m):
                    need(pe, s_h0, n)
                    need(pe, s_h1, n)
                    need(pe, s_ys, n, 2)
                    for i in range(G):
                        for c in range(NF):
                            ins = pe.matmul(pO[m % 2][:, P * i:P * (i + 1)], hb[:, m % 2, c, P * i:P * (i + 1)],
                                            we2[:, m // ESTEPS, c, :], start=(c == 0), stop=(c == NF - 1))
                    ins.then_inc(s_po, 1)
                run(pe, [(4, up), (5, down), (3, turn)])

            @block.scalar
            def _(a):
                def silus(n, m):
                    weights(a, n, m)
                    need(a, s_po, n, 2)
                    for half_, (src, done) in enumerate(((s_ph0, s_h0), (s_ph1, s_h1))):
                        need(a, src, n)
                        for c in range(2):
                            f = 2 * half_ + c
                            ins = a.activation(hb[:, m % 2, f, :], pH[half_][:, ROWS * c:ROWS * (c + 1)], ACT.Silu,
                                               bias=be1[:, m // ESTEPS, f:f + 1])
                        ins.then_inc(done, 1)
                run(a, [(4, silus)])

            @block.vector
            def _(v):
                def sources(n, m):
                    if isinstance(n, int):
                        if n >= NB:
                            arrived(v, n - NB, (m - NB) % TURN)
                    else:
                        v.wait_ge(s_xg[m % NB], 16 * G * earlier(n, m))
                    v.tensor_copy(source[:, m % NB, :], token_of[:, columns(n)]).then_inc(s_src, 1)

                def gates_of(n, m):
                    k = m % NB
                    arrived(v, n, m)
                    v.tensor_tensor(g1[:, k, :], xg[:, k, :, D], is_first[:, columns(n)], ALU.mult).then_inc(s_g1, 1)
                    v.tensor_tensor(g2[:, k, :], xg[:, k, :, D + 1], is_other[:, columns(n)], ALU.mult).then_inc(s_g2, 1)
                    need(v, s_g1, n)
                    need(v, s_g2, n)
                    v.tensor_tensor(gate[:, k, :], g1[:, k, :], g2[:, k, :], ALU.add).then_inc(s_gate, 1)

                def fetched(n, m):
                    need(v, s_pt, n)
                    need(v, s_ph1, n, 2)
                    need(v, s_ph0, n, 2)
                    v.tensor_copy(xgT[:, m % 2, :], pT[m % 2][:, 0:ROWS]).then_inc(s_xgT, 1)

                def results(n, m):
                    weights(v, n, m)
                    need(v, s_po, n)
                    need(v, s_yo, n, 2)
                    v.tensor_tensor(ysum[:, m % 2], pO[m % 2][:, 0:ROWS].rearrange("p (g d) -> p g d", g=G),
                                    be2[:, m // ESTEPS, :].unsqueeze(1).broadcast_to([P, G, D]), ALU.add).then_inc(s_ys, 1)
                    left(v, n, m)
                    v.tensor_copy(dest[:, m % NB, :], choice_of[:, columns(n)]).then_inc(s_dest, 1)
                    need(v, s_ys, n)
                    need(v, s_gate, n)
                    for i in range(G):
                        ins = v.tensor_scalar(yo[:, m % NB, i, :], ysum[:, m % 2, i, :], gate[:, m % NB, i:i + 1], None, ALU.mult)
                    ins.then_inc(s_yo, 1)
                run(v, [(0, sources), (3, fetched), (3, gates_of), (5, results)])

        with ExitStack() as st:
            st.callback(stage_over)
            G, NB = 4, 4
            GROUPS = TILES // G

            def sbt(name, shape, dt=F32):
                return st.enter_context(nc.sbuf_tensor(name, shape, dt))
            ya = sbt("c_ya", [P, NB, G, D])
            yb = sbt("c_yb", [P, NB, G, D])
            ys = sbt("c_ys", [P, NB, G, D])
            yn = sbt("c_yn", [P, NB, G, D])
            ot = sbt("c_ot", [P, NB, G, D])
            stats = sbt("c_stats", [P, NB, G, 6])
            mv = sbt("c_mv", [P, NB, G, 2])
            sd = sbt("c_sd", [P, NB, G])
            rs = sbt("c_rs", [P, NB, G])
            shift = sbt("c_shift", [P, NB, G])
            s_in = [sem(f"c_in{k}") for k in range(NB)]
            s_out = [sem(f"c_out{k}") for k in range(NB)]
            s_ys, s_st, s_var, s_sd, s_rs, s_shift, s_yn, s_ot = (
                sem("c_" + n) for n in ("ys", "st", "var", "sd", "rs", "shift", "yn", "ot"))
            first_v = choice[0:TOKENS].rearrange("(u v s p) d -> s u p v d", v=G, s=STEPS, p=P)
            other_v = choice[TOKENS:2 * TOKENS].rearrange("(u v s p) d -> s u p v d", v=G, s=STEPS, p=P)
            out_v = out.rearrange("(u v) (s p) d -> s u p v d", v=G, p=P)
            block = st.enter_context(nc.Block())

            def part(v_, g, k):
                k = k % 2
                return v_[bass.ds((g - k) // 2 if isinstance(g, int) else (g - k) >> 1, 1), k].rearrange("a p v d -> p (a v) d")

            @block.sync
            def _(sp):
                def load(g, k):
                    need(sp, s_ys, g, NB)
                    sp.dma_start(ya[:, k], part(first_v, g, k)).then_inc(s_in[k], 16)
                    sp.dma_start(yb[:, k], part(other_v, g, k)).then_inc(s_in[k], 16)

                skewed(sp, GROUPS, NB, 8, [(0, load)])

            @block.vector
            def _(v):
                def total(g, k):
                    v.wait_ge(s_in[k], 32 * (g // NB + 1) if isinstance(g, int) else 32 * (g >> 2) + 32)
                    need(v, s_yn, g, NB)
                    v.tensor_tensor(ys[:, k], ya[:, k], yb[:, k], ALU.add).then_inc(s_ys, 1)
                    need(v, s_ys, g)
                    for i in range(G):
                        ins = v.bn_stats(stats[:, k, i, :], ys[:, k, i, :])
                    ins.then_inc(s_st, 1)
                    need_apart(v, s_st, g)
                    need_apart(v, s_sd, g, NB)
                    need_apart(v, s_shift, g, NB)
                    for i in range(G):
                        ins = v.bn_aggr(mv[:, k, i, :], stats[:, k, i, :])
                    ins.then_inc(s_var, 1)

                def invert(g, k):
                    need(v, s_sd, g)
                    v.reciprocal(rs[:, k], sd[:, k]).then_inc(s_rs, 1)
                    need(v, s_rs, g)
                    v.scalar_tensor_tensor(out=shift[:, k], in0=mv[:, k, :, 0], scalar=-1.0, in1=rs[:, k],
                                           op0=ALU.mult, op1=ALU.mult).then_inc(s_shift, 1)
                skewed(v, GROUPS, NB, 8, [(0, total), (1, invert)])

            @block.gpsimd
            def _(g_):
                def add_x1(g, k):
                    need_apart(g_, s_yn, g)
                    if not isinstance(g, int) or g >= NB:
                        g_.wait_ge(s_out[k], 16 * (g // NB) if isinstance(g, int) else 16 * (g >> 2))
                    g_.tensor_tensor(ot[:, k], yn[:, k], x1[:, bass.ds(G * g, G), :], ALU.add).then_inc(s_ot, 1)
                skewed(g_, GROUPS, NB, 8, [(0, add_x1)])

            @block.scalar
            def _(a):
                def root(g, k):
                    need(a, s_var, g)
                    need(a, s_rs, g, NB)
                    a.activation(sd[:, k], mv[:, k, :, 1], ACT.Sqrt, bias=eps[:, 0:1]).then_inc(s_sd, 1)

                def finish(g, k):
                    need(a, s_shift, g)
                    need(a, s_ot, g, NB)
                    for i in range(G):
                        ins = a.activation(yn[:, k, i, :], ys[:, k, i, :], ACT.Identity, bias=shift[:, k, i:i + 1],
                                           scale=rs[:, k, i:i + 1])
                    ins.then_inc(s_yn, 1)
                def store(g, k):
                    need(a, s_ot, g)
                    a.dma_start(part(out_v, g, k), ot[:, k]).then_inc(s_out[k], 16)
                skewed(a, GROUPS, NB, 8, [(0, root), (1, finish), (3, store)])
                for k in range(NB):
                    a.wait_ge(s_out[k], 16 * GROUPS // NB)


_INS = ['L0_attn_x', 'L0_attn_ln_w', 'L0_attn_ln_b', 'L0_attn_in_proj_w', 'L0_attn_conv_w', 'L0_attn_conv_b',
        'L0_attn_dt_bias', 'L0_attn_A_log', 'L0_attn_D_skip', 'L0_attn_rms_w', 'L0_attn_out_proj_w', 'L0_attn_mlp_w1',
        'L0_attn_mlp_b1', 'L0_attn_mlp_w2', 'L0_attn_mlp_b2', 'L0_ffn_Wr', 'L0_ffn_br', 'L0_ffn_W1', 'L0_ffn_b1',
        'L0_ffn_W2', 'L0_ffn_b2']


def kernel(**inputs):
    import numpy as _np
    import concourse.bacc as _bacc
    from concourse import mybir as _mybir
    from concourse.bass_utils import run_bass_kernel_spmd as _run

    nc = _bacc.Bacc("TRN2", target_bir_lowering=False, num_devices=1)
    arrays, args = {}, []
    for name in _INS:
        a = _np.ascontiguousarray(inputs[name])
        arrays[f"in_{name}_dram"] = a
        args.append(nc.dram_tensor(f"in_{name}_dram", a.shape, _mybir.dt.from_np(a.dtype), kind="ExternalInput").ap())
    args.append(nc.dram_tensor("out_0_dram", (SEQS, LEN, D), F32, kind="ExternalOutput").ap())
    build(nc, *args)
    r = _run(nc, [arrays], core_ids=[0])
    return r.results[0]["out_0_dram"]
```
